# Optimizing a Trainium2 kernel written in Bass

```python
import numpy as np
import jax
import jax.numpy as jnp

def _softmax(x, axis=-1):
    return jax.nn.softmax(x, axis=axis)

def _gelu(x):
    return jax.nn.gelu(x, approximate=True)

def _silu(x):
    return jax.nn.silu(x)

def _sigmoid(x):
    return jax.nn.sigmoid(x)

def _layernorm(x, axis=-1, eps=1e-05):
    m = jnp.mean(x, axis=axis, keepdims=True)
    v = jnp.var(x, axis=axis, keepdims=True)
    return (x - m) / jnp.sqrt(v + eps)

def _scatter_add(tgt, idx, src, axis=0):
    return tgt.at[idx].add(src)

def _segment_sum(src, seg, n):
    return jax.ops.segment_sum(src, seg, n)
kernel_name = 'mk_adaln_ffn_d2_seqx_r4_989cb8'

def setup_inputs(seed: int=0):
    np.random.seed(seed)
    _w = jnp.asarray

    def _rec_inputs():
        import jax
        import jax.numpy as jnp
        _rk = jax.random.key(seed)
        x = -0.0003929 + 0.9999 * jax.random.normal(jax.random.fold_in(_rk, 1), (32, 64, 1024), jnp.float32)
        _lenS = 64 - jax.random.randint(jax.random.fold_in(_rk, 7), (32,), 0, max(1, 64 // 4) + 1, jnp.int32)
        _lenS2 = 64 - jax.random.randint(jax.random.fold_in(_rk, 8), (32,), 0, max(1, 64 // 4) + 1, jnp.int32)
        itok_B_8_3872 = jax.random.randint(jax.random.fold_in(_rk, 11), (32,), 8, 3873, jnp.int32)
        itok_B_14_62 = jax.random.randint(jax.random.fold_in(_rk, 12), (32,), 14, 63, jnp.int32)
        return (x, itok_B_8_3872, itok_B_14_62)
    x, itok_B_8_3872, itok_B_14_62 = _rec_inputs()

    def _L0_cond_setup():
        import math
        import jax, jax.numpy as jnp
        import numpy as np
        H, N, B, L = (64, 64, 16, 1024)
        DT_MIN, DT_MAX = (0.001, 0.1)

        def _get_kernel(log_dt, C, log_A_real, A_imag, length):
            Cc = C[..., 0] + 1j * C[..., 1]
            dt = jnp.exp(log_dt)
            A = -jnp.exp(log_A_real) + 1j * A_imag
            dtA = A * dt[:, None]
            P = dtA[:, :, None] * jnp.arange(length, dtype=jnp.float32)
            Cs = Cc * (jnp.exp(dtA) - 1.0) / A
            K = 2.0 * jnp.einsum('hn,hnl->hl', Cs, jnp.exp(P)).real
            return K
        key = jax.random.key(seed)
        ks = jax.random.split(key, 6)
        u = jax.random.normal(ks[0], (B, H, L), dtype=jnp.float32)
        length = jax.random.randint(ks[1], (B,), 0, L)
        log_dt = jax.random.uniform(ks[2], (H,), dtype=jnp.float32) * (math.log(DT_MAX) - math.log(DT_MIN)) + math.log(DT_MIN)
        C = jax.random.normal(ks[3], (H, N, 2), dtype=jnp.float32)
        log_A_real = jnp.log(0.5 * jnp.ones((H, N), dtype=jnp.float32))
        A_imag = math.pi * jnp.broadcast_to(jnp.arange(N, dtype=jnp.float32), (H, N))
        D = jax.random.normal(ks[4], (H,), dtype=jnp.float32)
        return {'u': u, 'length': length, 'log_dt': log_dt, 'C': C, 'log_A_real': log_A_real, 'A_imag': A_imag, 'D': D}
    _L0_cond_all = _L0_cond_setup()
    _L0_cond_in = {k: v for k, v in _L0_cond_all.items() if k in ('log_dt', 'C', 'log_A_real', 'A_imag', 'D')}
    del _L0_cond_all

    def _L0_ffn_setup():
        import jax, jax.numpy as jnp
        import numpy as np
        B_L, B_H = (4, 8)
        LIN_SLOPE, LIN_INTER, EST_T = (1.0, 0.0, 64.0)
        BATCH, SEQ, IN_F, OUT_F = (4, 512, 1024, 1024)
        MAX_BITS = 8

        def dequant_kbit(qweight, lut, bit):
            O, I32 = (qweight.shape[1], qweight.shape[2])
            shifts = jnp.arange(32, dtype=jnp.int32)
            idx = jnp.zeros((O, I32 * 32), dtype=jnp.int32)
            for p in range(bit):
                bits = (qweight[p][:, :, None] >> shifts & 1).reshape(O, I32 * 32)
                idx = idx | bits << p
            return jnp.take_along_axis(lut, idx, axis=1)
        key = jax.random.key(seed)
        k = jax.random.split(key, 5)
        x = jax.random.normal(k[0], (BATCH, SEQ, IN_F), dtype=jnp.float32)
        qweight = jax.random.randint(k[1], (MAX_BITS, OUT_F, IN_F // 32), 0, 2147483647, dtype=jnp.int32)
        lut4 = jax.random.normal(k[2], (OUT_F, 2 ** B_L), dtype=jnp.float32) * 0.02
        lut8 = jax.random.normal(k[3], (OUT_F, 2 ** B_H), dtype=jnp.float32) * 0.02
        bias = jax.random.normal(k[4], (OUT_F,), dtype=jnp.float32) * 0.01
        return {'x': x, 'qweight': qweight, 'lut4': lut4, 'lut8': lut8, 'bias': bias}
    _L0_ffn_all = _L0_ffn_setup()
    _L0_ffn_in = {k: v for k, v in _L0_ffn_all.items() if k in ('qweight', 'lut4', 'lut8', 'bias')}
    del _L0_ffn_all

    def _L1_cond_setup():
        import jax, jax.numpy as jnp
        import numpy as np
        B, S, D_IN, D_OUT = (4, 512, 1024, 1024)
        L, R = (64, 16)
        LORA_ALPHA = 32
        LORA_SCALING = LORA_ALPHA / R
        key = jax.random.key(seed)
        k = jax.random.split(key, 6)
        return {'X': jax.random.normal(k[0], (B, S, D_IN), dtype=jnp.float32), 'W': jax.random.normal(k[1], (D_OUT, D_IN), dtype=jnp.float32) * (1.0 / np.sqrt(D_IN)), 'b': jax.random.normal(k[2], (D_OUT,), dtype=jnp.float32), 'lora_A': jax.random.normal(k[3], (L, D_IN, R), dtype=jnp.float32) * (1.0 / np.sqrt(D_IN)), 'lora_B': jax.random.normal(k[4], (L, D_OUT, R), dtype=jnp.float32) * (1.0 / np.sqrt(D_OUT)), 'lora_ids': jax.random.randint(k[5], (B,), 0, L, dtype=jnp.int64)}
    _L1_cond_all = _L1_cond_setup()
    _L1_cond_in = {k: v for k, v in _L1_cond_all.items() if k in ('W', 'b', 'lora_A', 'lora_B')}
    del _L1_cond_all

    def _L1_ffn_setup():
        import jax, jax.numpy as jnp
        import numpy as np
        NUM_EXPERTS = 8
        RANK = 32
        ALPHA = 16.0
        TOP_K = 2
        TEMPERATURE = 1.0
        GAMMA = 0.5
        SOFT_TOPK_TEMP = 0.5
        N_GRAM = 2
        EPS = 1e-06
        key = jax.random.key(seed)
        ks = jax.random.split(key, 6)
        d_in, d_out = (1024, 1024)
        Bsz, T = (4, 512)
        x = jax.random.normal(ks[0], (Bsz, T, d_in), dtype=jnp.float32)
        W = jax.random.normal(ks[1], (d_out, d_in), dtype=jnp.float32) / np.sqrt(d_in)
        b = jax.random.normal(ks[2], (d_out,), dtype=jnp.float32) * 0.01
        A = jax.random.normal(ks[3], (d_in, RANK), dtype=jnp.float32) / np.sqrt(d_in)
        Bmat = jax.random.normal(ks[4], (RANK, d_out), dtype=jnp.float32) * 0.01
        LiMEs = jax.random.normal(ks[5], (NUM_EXPERTS, RANK), dtype=jnp.float32) * 0.1
        return {'x': x, 'W': W, 'b': b, 'A': A, 'Bmat': Bmat, 'LiMEs': LiMEs}
    _L1_ffn_all = _L1_ffn_setup()
    _L1_ffn_in = {k: v for k, v in _L1_ffn_all.items() if k in ('W', 'b', 'A', 'Bmat', 'LiMEs')}
    del _L1_ffn_all
    return {'x': x, 'itok_B_8_3872': itok_B_8_3872, 'itok_B_14_62': itok_B_14_62, 'L0_cond_log_dt': _L0_cond_in['log_dt'], 'L0_cond_C': _L0_cond_in['C'], 'L0_cond_log_A_real': _L0_cond_in['log_A_real'], 'L0_cond_A_imag': _L0_cond_in['A_imag'], 'L0_cond_D': _L0_cond_in['D'], 'L0_ffn_qweight': _L0_ffn_in['qweight'], 'L0_ffn_lut4': _L0_ffn_in['lut4'], 'L0_ffn_lut8': _L0_ffn_in['lut8'], 'L0_ffn_bias': _L0_ffn_in['bias'], 'L1_cond_W': _L1_cond_in['W'], 'L1_cond_b': _L1_cond_in['b'], 'L1_cond_lora_A': _L1_cond_in['lora_A'], 'L1_cond_lora_B': _L1_cond_in['lora_B'], 'L1_ffn_W': _L1_ffn_in['W'], 'L1_ffn_b': _L1_ffn_in['b'], 'L1_ffn_A': _L1_ffn_in['A'], 'L1_ffn_Bmat': _L1_ffn_in['Bmat'], 'L1_ffn_LiMEs': _L1_ffn_in['LiMEs']}

def reference(x, itok_B_8_3872, itok_B_14_62, L0_cond_log_dt, L0_cond_C, L0_cond_log_A_real, L0_cond_A_imag, L0_cond_D, L0_ffn_qweight, L0_ffn_lut4, L0_ffn_lut8, L0_ffn_bias, L1_cond_W, L1_cond_b, L1_cond_lora_A, L1_cond_lora_B, L1_ffn_W, L1_ffn_b, L1_ffn_A, L1_ffn_Bmat, L1_ffn_LiMEs):
    import jax
    import jax.numpy as jnp

    def _L0_cond_ref(u, length, log_dt, C, log_A_real, A_imag, D):
        import math
        import jax, jax.numpy as jnp
        import numpy as np
        H, N, B, L = (64, 64, 16, 1024)
        DT_MIN, DT_MAX = (0.001, 0.1)

        def _get_kernel(log_dt, C, log_A_real, A_imag, length):
            Cc = C[..., 0] + 1j * C[..., 1]
            dt = jnp.exp(log_dt)
            A = -jnp.exp(log_A_real) + 1j * A_imag
            dtA = A * dt[:, None]
            P = dtA[:, :, None] * jnp.arange(length, dtype=jnp.float32)
            Cs = Cc * (jnp.exp(dtA) - 1.0) / A
            K = 2.0 * jnp.einsum('hn,hnl->hl', Cs, jnp.exp(P)).real
            return K
        Bq, Hq, Lq = u.shape
        mask = (jnp.arange(Lq) < length[:, None]).astype(u.dtype)
        u_m = u * mask[:, None, :]
        kernel = _get_kernel(log_dt, C, log_A_real, A_imag, Lq)
        n = 2 * Lq
        k_f = jnp.fft.rfft(kernel, n=n)
        u_f = jnp.fft.rfft(u_m, n=n)
        y = jnp.fft.irfft(u_f * k_f, n=n)[..., :Lq]
        y = y + u_m * D[:, None]
        return y * mask[:, None, :]

    def _L0_ffn_ref(x, qweight, lut4, lut8, bias):
        import jax, jax.numpy as jnp
        import numpy as np
        B_L, B_H = (4, 8)
        LIN_SLOPE, LIN_INTER, EST_T = (1.0, 0.0, 64.0)
        BATCH, SEQ, IN_F, OUT_F = (4, 512, 1024, 1024)
        MAX_BITS = 8

        def dequant_kbit(qweight, lut, bit):
            O, I32 = (qweight.shape[1], qweight.shape[2])
            shifts = jnp.arange(32, dtype=jnp.int32)
            idx = jnp.zeros((O, I32 * 32), dtype=jnp.int32)
            for p in range(bit):
                bits = (qweight[p][:, :, None] >> shifts & 1).reshape(O, I32 * 32)
                idx = idx | bits << p
            return jnp.take_along_axis(lut, idx, axis=1)
        e = jnp.linalg.norm(x, axis=-1) * LIN_SLOPE + LIN_INTER
        mask = e > EST_T
        w_l = dequant_kbit(qweight, lut4, B_L)
        w_h = dequant_kbit(qweight, lut8, B_H)
        y_l = jnp.einsum('bsi,oi->bso', x, w_l)
        y_h = jnp.einsum('bsi,oi->bso', x, w_h)
        y = jnp.where(mask[..., None], y_h, y_l) + bias
        return y

    def _L1_cond_ref(X, W, b, lora_A, lora_B, lora_ids):
        import jax, jax.numpy as jnp
        import numpy as np
        B, S, D_IN, D_OUT = (4, 512, 1024, 1024)
        L, R = (64, 16)
        LORA_ALPHA = 32
        LORA_SCALING = LORA_ALPHA / R
        output = jnp.einsum('bsd,od->bso', X, W) + b
        A = lora_A[lora_ids]
        Bm = lora_B[lora_ids]
        inter = jnp.einsum('bwr,bsw->bsr', A, X)
        lora_out = output + jnp.einsum('bsr,bwr->bsw', inter, Bm) * LORA_SCALING
        return lora_out

    def _L1_ffn_ref(x, W, b, A, Bmat, LiMEs):
        import jax, jax.numpy as jnp
        import numpy as np
        NUM_EXPERTS = 8
        RANK = 32
        ALPHA = 16.0
        TOP_K = 2
        TEMPERATURE = 1.0
        GAMMA = 0.5
        SOFT_TOPK_TEMP = 0.5
        N_GRAM = 2
        EPS = 1e-06
        Bsz, T, d_in = x.shape
        E = LiMEs.shape[0]
        scaling = ALPHA / RANK
        H = jnp.einsum('btd,od->bto', x, W) + b
        z = jnp.einsum('btd,dr->btr', x, A)
        anchors = jnp.arange(N_GRAM - 1, T, N_GRAM)
        H_slice = H[:, anchors, :E]
        delta_slice = jnp.einsum('bar,er->bae', z[:, anchors], LiMEs)
        H_scale = jnp.maximum(jnp.max(jnp.abs(H_slice)), EPS)
        d_scale = jnp.maximum(jnp.max(jnp.abs(delta_slice)), EPS)
        logits = ((1.0 - GAMMA) * (H_slice / H_scale) + GAMMA * (delta_slice / d_scale)) / TEMPERATURE
        probs = jax.nn.softmax(logits, axis=-1)
        topk_vals, _ = jax.lax.top_k(probs, TOP_K)
        thresh = topk_vals[..., -1:]
        mask = jax.nn.sigmoid((probs - thresh) / SOFT_TOPK_TEMP)
        weights = probs * mask
        weights = weights / (jnp.sum(weights, axis=-1, keepdims=True) + 1e-09)
        weights_full = jnp.repeat(weights, N_GRAM, axis=1)
        p_mix = jnp.einsum('bte,er->btr', weights_full, LiMEs)
        delta = jnp.einsum('btr,ro->bto', z * p_mix, Bmat) * scaling
        return H + delta
    x = x + _L0_ffn_ref(_L0_cond_ref(x, itok_B_8_3872, L0_cond_log_dt, L0_cond_C, L0_cond_log_A_real, L0_cond_A_imag, L0_cond_D), L0_ffn_qweight, L0_ffn_lut4, L0_ffn_lut8, L0_ffn_bias)
    x = x + _L1_ffn_ref(_L1_cond_ref(x, L1_cond_W, L1_cond_b, L1_cond_lora_A, L1_cond_lora_B, itok_B_14_62), L1_ffn_W, L1_ffn_b, L1_ffn_A, L1_ffn_Bmat, L1_ffn_LiMEs)
    return x

_drawn_inputs = setup_inputs


def setup_inputs(seed=0):
    import zlib

    import numpy as np

    out = dict(_drawn_inputs(seed))
    spreads = {'L0_cond_log_A_real': (-0.6931471824645996, 0.2)}
    factors = {'L0_ffn_bias': 8.0,
     'L1_ffn_b': 8.0,
     'L1_ffn_A': 8.0,
     'L1_ffn_Bmat': 8.0,
     'L1_ffn_LiMEs': 8.0}
    for name, (base, spread) in spreads.items():
        noise = np.random.default_rng([zlib.crc32(name.encode()), seed]).standard_normal(out[name].shape)
        drawn = base * np.exp(spread * noise) if base else spread * noise
        out[name] = jnp.asarray(drawn.astype(out[name].dtype))
    for name, factor in factors.items():
        out[name] = (out[name] * factor).astype(out[name].dtype)
    return out
```

```python
from contextlib import ExitStack

import numpy as np

import concourse.bass as bass
from concourse import mybir

F32 = mybir.dt.float32
BF16 = mybir.dt.bfloat16
I32 = mybir.dt.int32
I16 = mybir.dt.int16
U8 = mybir.dt.uint8
ALU = mybir.AluOpType
ACT = mybir.ActivationFunctionType
AX = mybir.AxisListType

P = 128
B, H, L = 32, 64, 1024
T = B * H
KC = L // P
N = 64
NQ = H // 4
TC = 512
NCH = T // TC
R0, R1_, E = 16, 32, 8
BC = TC // H
EST_T = 64.0
LORA_SCALE = 2.0
DELTA_SCALE = 0.5
TWO_PI = 6.283185
MAGIC = 12582912.0
KPAD = P + L
LW = 52
NPAIR = 4

C_ID, C_LORA, C_R32, C_R1, C_PHI, C_NPHI, C_LOW, C_OWN, C_END = 0, 128, 640, 672, 704, 705, 706, 707, 715


def shape_constants():
    p = np.arange(P)
    c = np.zeros((P, C_END), np.float32)
    c[:, C_ID:C_ID + P] = np.eye(P)
    c[:, C_LORA:C_LORA + TC] = LORA_SCALE * (p[:, None] // R0 == np.arange(TC)[None] // H)
    c[:, C_R32:C_R32 + 32] = 32 * np.arange(32)
    c[:, C_R1:C_R1 + 32] = np.arange(32)
    c[:, C_PHI] = 0.25 * (p >= N)
    c[:, C_NPHI] = -0.25 * (p >= N)
    c[:, C_LOW] = p % 16
    c[:, C_OWN:C_OWN + 8] = p[:, None] // 16 == np.arange(8)[None]
    feature = np.arange(L, dtype=np.float32)
    return c, np.stack([feature, feature.reshape(KC, P)[:, ::-1].reshape(L)])


def build_kernel(nc, a, out):
    k_pad = nc.dram_tensor("k_pad", (H, KPAD), F32).ap()
    code_lo = nc.dram_tensor("code_lo", (L, L), U8).ap()
    lut_parts = nc.dram_tensor("lut_parts", (L, 16 * LW), BF16).ap()
    high_rows = nc.dram_tensor("high_rows", (T,), U8).ap()

    ctx = ExitStack()
    with ctx:
        ctx.enter_context(nc.allow_non_contiguous_dma(reason="biases and the skip weights: a few KB, once"))

        def sb(name, shape, dt):
            return ctx.enter_context(nc.sbuf_tensor(name, shape, dt))

        def sem(name):
            return ctx.enter_context(nc.semaphore(name))

        act = sb("act", [P, KC, TC + T], F32)
        w01 = sb("w01", [P, 2 * KC * L], F32)
        w2 = sb("w2", [P, KC * L], F32)
        r3 = sb("r3", [P, 4 * L], F32)
        u = sb("u", [P, 2048], F32)
        v = sb("v", [P, 1024], F32)
        cst = sb("cst", [P, C_END - 512], F32)
        identb = sb("identb", [P, P], BF16)
        bias = sb("bias", [P, 3 * KC + 1], F32)
        ids = sb("ids", [1, B], I32)
        ssq = sb("ssq", [P, NQ], F32)
        high = sb("high", [P, NQ], U8)
        aw = sb("aw", [P, KC, R1_ + E], F32)
        small = sb("small", [P, 136], F32)
        lim_sb = sb("lim_sb", [R1_, R1_ + E], F32)
        ps = ctx.enter_context(nc.psum_tensor("ps", [P, 8, 512], F32))

        ident = cst[:, C_ID:C_ID + P]

        def cc(at, n=1):
            at = at if at < C_LORA else at - 512
            return cst[:, at:at + n]

        wl = w01[:, 0:KC * L].rearrange("p (k o) -> p k o", k=KC)
        wh = w01[:, KC * L:2 * KC * L].rearrange("p (k o) -> p k o", k=KC)

        w2b = w2[:, :]
        ut = w2b[:, 0:1024].rearrange("p (c t) -> p c t", c=KC)
        xq = w2b[:, 1024:2048]
        xm = w2b[:, 2048:3072]
        ys = w2b[:, 3072:4096]
        code_t = w2b[:, 4096:6144].bitcast(I32).rearrange("p (k o) -> p k o", k=KC)
        bits = w2b[:, 6144:6656].bitcast(I32).rearrange("p (b k o) -> p b k o", b=4, k=KC)
        mask = w2b[:, 6656:7168].bitcast(BF16)
        mask_rev = w2b[:, 7168:7680].bitcast(BF16)
        lp = w2b[:, 7680:7680 + 8 * LW // 2].bitcast(BF16).rearrange("p (g w) -> p g w", w=LW)
        lb = [u[:, 512 * i:512 * i + 408].bitcast(BF16).rearrange("p (g w o) -> p g w o", g=2, o=8) for i in range(2)]
        junk = u[:, 1024:1536].bitcast(BF16)
        toe = r3[:, :].rearrange("p (h c) -> p h c", h=4)
        oh = [act[:, 2 * i:2 * i + 2, 0:TC].bitcast(BF16) for i in range(2)]
        rep = [act[:, 4 + 2 * i:6 + 2 * i, 0:TC].bitcast(U8) for i in range(2)]

        q_in = w01[:, 0:2048].bitcast(I32).rearrange("p (o b w) -> p o b w", o=8, b=8)
        q_t = w01[:, 2048:3072].bitcast(I32)
        q_lo = w01[:, 3072:5120].bitcast(I32)
        codes = w01[:, 5120:9216].bitcast(BF16).rearrange("p (o i) -> p o i", o=8)
        codes_lo = w01[:, 9216:11264].bitcast(U8).rearrange("p (o i) -> p o i", o=8)
        lut_in = w01[:, 11264:13312].rearrange("p (o a b) -> p o a b", o=8, a=16)
        lut4_in = w01[:, 13312:13440].rearrange("p (o b) -> p o b", o=8)
        flat = act[:, :, :].rearrange("p k t -> p (k t)")
        lutp = flat[:, 0:2176].rearrange("p (o b w) -> p o b w", o=8, b=16)
        parts = flat[:, 2176:2176 + 3328].bitcast(BF16).rearrange("p (o b w) -> p o b w", o=8, b=16)
        tp = [flat[:, 5504 + 2048 * i:5504 + 2048 * (i + 1)].rearrange("p (h m) -> p h m", h=H) for i in range(7)]
        sm = w01[:, 13440:13440 + 24 * 64].rearrange("p (s h) -> p s h", h=64)
        c_in = w01[0:H, 14976:15104].rearrange("p (n two) -> p two n", two=2)
        dup = w01[0:H, 15104:15616].rearrange("p (s d n) -> p s d n", s=4, d=2)
        kt = w01[:, 15616:16128].rearrange("p (q b) -> p q b", q=NQ)
        d_col = w01[:, 16128:16144]
        zeros = w01[0:H, 16144:16272]
        lens = small[:, 0:2]
        lens_i = small[:, 2:3].bitcast(I32)
        frow = w2b[:, 0:2048].rearrange("p (two l) -> p two l", two=2)

        xrow = r3[:, :].rearrange("p (t l) -> p t l", t=4)
        xres = [u[:, TC * i:TC * i + TC] for i in range(2)]
        w_in = u[:, 1024:2048]
        high_all = v[:, 0:T // 4].bitcast(U8)
        high_now = v[:, T // 4:T // 4 + TC // 4].bitcast(U8)
        w1t = w2[:, :].rearrange("p (k o) -> p k o", k=KC)
        mid = w01[:, :].rearrange("p (k t) -> p k t", k=KC)
        la = r3[:, 0:1024].rearrange("p (k r) -> p k r", k=KC)
        lbn = r3[:, 1024:2048].rearrange("p (m r) -> p m r", m=KC)
        lbt = r3[:, 2048:3072]
        inter = r3[:, 3072:3584]
        lmask = r3[:, 3584:4096]
        zh = u[0:R1_ + E, 0:T]
        zbias = small[0:R1_ + E, 3:4]
        ones = small[:, 8:136]
        lim = lim_sb[:, :]
        tail = act[:, :, T:T + TC]
        gt = tail[:, 0, 0:128].rearrange("p (s g e) -> p s g e", s=2, g=8)
        gs = [tail[:, 0, 128 + 64 * i:192 + 64 * i].rearrange("p (g e) -> p g e", g=8) for i in range(6)]
        g1 = [tail[:, 1, 8 * i:8 * i + 8] for i in range(12)]
        w_in2 = [tail[:, 4 + 2 * i:6 + 2 * i, :] for i in range(2)]
        zp = r3[0:R1_, 0:T]
        bm = r3[0:R1_, T:T + L]
        wt = r3[0:E, T + L:T + 2 * L]
        stage = [v[:, TC * i:TC * i + TC] for i in range(2)]
        rows_out = tail.rearrange("p (t two) l -> p t two l", two=2)

        cst_in = sem("cst_in"); ssm_in = sem("ssm_in"); q_loaded = sem("q_loaded"); lut_loaded = sem("lut_loaded")
        len_in = sem("len_in"); d_in = sem("d_in"); bias_in = sem("bias_in")
        held = sem("held")
        dve = sem("dve"); pool = sem("pool")
        act_id = sem("act_id"); act_dup = sem("act_dup"); act_ex = sem("act_ex"); act_big = sem("act_big")
        act_code = sem("act_code"); act_lo = sem("act_lo"); code_t_ready = sem("code_t_ready")
        dve_code = sem("dve_code"); dve_lo = sem("dve_lo"); dve_ssm = sem("dve_ssm"); dve_k = sem("dve_k")
        dve_lut = sem("dve_lut"); pe_dup = sem("pe_dup"); pe_code = sem("pe_code"); pe_k = sem("pe_k")
        masks_ready = sem("masks_ready"); p_ready = sem("p_ready"); qc_ready = sem("qc_ready")
        k_stored = sem("k_stored"); lo_stored = sem("lo_stored"); parts_stored = sem("parts_stored")
        xq_in = sem("xq_in"); toe_in = sem("toe_in"); rep_in = [sem("rep_in0"), sem("rep_in1")]; lp_in = sem("lp_in")
        xm_done = sem("xm_done"); lb_done = sem("lb_done"); oh_done = sem("oh_done")
        px_full = sem("px_full"); px_free = sem("px_free"); conv_done = sem("conv_done"); ys_done = sem("ys_done")
        sq_done = sem("sq_done"); unit_done = sem("unit_done"); pair_done = sem("pair_done")
        mux = sem("mux"); mux_free = sem("mux_free"); wl_free = sem("wl_free"); bits_done = sem("bits_done")

        high_done = sem("high_done"); high_out = sem("high_out"); high_in = sem("high_in"); xr_in = sem("xr_in")
        l0_full = sem("l0_full"); l0_free = sem("l0_free"); l0_sel = sem("l0_sel"); l0_pick = sem("l0_pick"); xt_full = sem("xt_full")
        xres_full = sem("xres_full"); w1_in = sem("w1_in"); w1_full = sem("w1_full"); w1_free = sem("w1_free")
        ids_in = sem("ids_in"); aw_in = sem("aw_in"); lmask_in = sem("lmask_in"); la_in = sem("la_in"); lbn_in = sem("lbn_in")
        aw_full = sem("aw_full"); aw_done = sem("aw_done"); bt_full = sem("bt_full"); bt_done = sem("bt_done")
        in_full = sem("in_full"); in_done = sem("in_done"); c_full = sem("c_full"); c_free = sem("c_free")
        zh_full = sem("zh_full"); zh_done = sem("zh_done")
        g_full = sem("g_full"); g_dve = sem("g_dve"); g_act = sem("g_act"); w2_in = [sem("w2_in0"), sem("w2_in1")]
        w2_full = sem("w2_full"); w2_free = sem("w2_free"); bm_in = sem("bm_in")
        f_full = sem("f_full"); f_free = sem("f_free"); st_used = sem("st_used"); row_free = sem("row_free")
        out_done = sem("out_done")

        block = ctx.enter_context(nc.Block())

        @block.sync
        def _(sp):
            sp.dma_start(cst[:, 0:P], a["cst"][:, 0:P]).then_inc(cst_in, 16)
            sp.dma_start(cst[:, P:C_END - 512], a["cst"][:, 640:C_END]).then_inc(cst_in, 16)
            for b in range(8):
                sp.dma_start(q_in[:, :, b, :], a["L0_ffn_qweight"][b].rearrange("(o p) w -> p o w", p=P)
                             ).then_inc(q_loaded, 16)
            sp.dma_start(ids[:, :], a["itok_B_14_62"].rearrange("(one b) -> one b", one=1)).then_inc(ids_in, 16)
            sp.dma_start(frow, a["feature_rows"].partition_broadcast(P)).then_inc(len_in, 16)
            for hh in range(4):
                sp.dma_start(lens_i[32 * hh:32 * hh + 32, :],
                             a["itok_B_8_3872"].rearrange("(b one) -> b one", one=1)).then_inc(len_in, 16)
            sp.dma_start(lut_in, a["L0_ffn_lut8"].rearrange("(o p) (a b) -> p o a b", p=P, a=16)).then_inc(lut_loaded, 16)
            sp.dma_start(lut4_in, a["L0_ffn_lut4"].rearrange("(o p) b -> p o b", p=P)).then_inc(lut_loaded, 16)
            sp.wait_ge(act_lo, 8)
            sp.dma_start(code_lo.rearrange("(o p) i -> p o i", p=P), codes_lo).then_inc(lo_stored, 16)
            sp.wait_ge(dve_lut, 1)
            sp.dma_start(lut_parts.rearrange("(o p) w -> p o w", p=P), parts.rearrange("p o b w -> p o (b w)")
                         ).then_inc(parts_stored, 16)
            sp.wait_ge(dve_k, 2)
            sp.dma_start(k_pad[:, 0:P], zeros).then_inc(k_stored, 16)
            for hh in range(4):
                sp.dma_start(k_pad[:, P:KPAD].rearrange("(q hh) (a b) -> hh a q b", hh=4, b=32)[hh],
                             kt[32 * hh:32 * hh + 32]).then_inc(k_stored, 16)
            sp.wait_ge(lo_stored, 16)
            sp.wait_ge(parts_stored, 16)
            sp.wait_ge(k_stored, 80)
            sp.wait_ge(masks_ready, 1)
            x_h = a["x"].rearrange("b h l -> h b l")
            lo_rep = bass.AP(code_lo.tensor, 0, [[64 * L, NQ], [8 * L, 8], [L, 8], [0, 16], [1, L]])
            lp_src = lut_parts.rearrange("(q g o) (b w) -> q (o b) g w", q=NQ, g=8, w=LW)
            toe_src = bass.AP(k_pad.tensor, 1, [[4 * KPAD, NQ], [1, P], [KPAD, 4], [1, L]])
            with sp.Fori(0, NQ) as q:
                sp.wait_ge(xm_done, q + 1)
                for hh in range(4):
                    sp.dma_start(xq[32 * hh:32 * hh + 32], x_h[bass.ds(q * 4 + hh, 1)].rearrange("h b l -> (h b) l")
                                 ).then_inc(xq_in, 16)
                for half in range(2):
                    sp.wait_ge(oh_done, q * 4 + 2 * half + 2)
                    sp.sem_inc(held, 1)
                    for g in range(4):
                        sp.dma_start(rep[half][:, g // 2, (g % 2) * L:(g % 2 + 1) * L],
                                     lo_rep[bass.ds(q, 1), 4 * half + g]
                                     ).then_inc(rep_in[half], 16)
                sp.wait_ge(lb_done, q * 4 + 4)
                sp.dma_start(lp, lp_src[bass.ds(q, 1)]).then_inc(lp_in, 16)
                sp.wait_ge(conv_done, q + 1)
                for hh in range(4):
                    sp.dma_start(toe[:, hh, :], toe_src[bass.ds(q, 1), :, hh]).then_inc(toe_in, 16)

            sp.wait_ge(high_done, 1)
            for hh in range(4):
                sp.dma_start(high_rows.rearrange("(b q hh) -> hh b q", q=NQ, hh=4)[hh], high[32 * hh:32 * hh + 32, :]
                             ).then_inc(high_out, 16)
            sp.wait_ge(high_out, 64)
            sp.dma_start(high_all, high_rows.partition_broadcast(P)).then_inc(high_in, 16)
            sp.wait_ge(sq_done, NQ + 1)
            sp.wait_ge(pair_done, 4 * NQ + 2)
            x_rows = a["x"].rearrange("b h l -> (b h) l").rearrange("(c t p) l -> c p t l", c=NCH, p=P)
            with sp.Fori(0, NCH) as c:
                sp.wait_ge(xt_full, c * 8 + 8)
                sp.dma_start(xrow, x_rows[bass.ds(c, 1)]).then_inc(xr_in, 16)
                for s in range(2):
                    sp.wait_ge(w1_full, c * 4 + 2 * s + 2)
                    sp.dma_start(w_in, a["L1_cond_W"].rearrange("(n p) i -> n p i", p=P)[bass.ds(c * 2 + s, 1)]
                                 ).then_inc(w1_in, 16)
            sp.wait_ge(l0_free, 8 * NCH + 2)
            sp.wait_ge(w1_full, 4 * NCH + 2)
            sp.dma_start(u[0:E, 0:L], a["L1_ffn_W"][0:E, :]).then_inc(aw_in, 16)
            sp.dma_start(aw[:, :, 0:R1_], a["L1_ffn_A"].rearrange("(k p) r -> p k r", p=P)).then_inc(aw_in, 16)
            sp.dma_start(lim_sb[0:E, 0:R1_], a["L1_ffn_LiMEs"]).then_inc(aw_in, 16)
            sp.dma_start(small[R1_:R1_ + E, 3:4], a["L1_ffn_b"][0:E].rearrange("(e one) -> e one", one=1)
                         ).then_inc(aw_in, 16)
            sp.dma_start(lmask, a["cst"][:, C_LORA:C_LORA + TC]).then_inc(lmask_in, 16)
            sp.wait_ge(ids_in, 16)
            lora_a = a["L1_cond_lora_A"].rearrange("n (k p) r -> n p k r", p=P)
            lora_b = a["L1_cond_lora_B"].rearrange("n (k p) r -> n p k r", p=P)
            with sp.Fori(0, NCH) as c:
                sp.wait_ge(in_full, c + 1)
                sp.wait_ge(bt_full, c * 2 + 2)
                for n in range(BC):
                    who = sp.value_load(ids[0:1, bass.ds(c * BC + n, 1)], min_val=0, max_val=63)
                    sp.dma_start(la[:, :, R0 * n:R0 * n + R0], lora_a[bass.ds(who, 1)]).then_inc(la_in, 16)
                    sp.dma_start(lbn[:, :, R0 * n:R0 * n + R0], lora_b[bass.ds(who, 1)]).then_inc(lbn_in, 16)
            for n in range(KC):
                if n >= 2:
                    sp.wait_ge(w2_full, 2 * n - 2)
                sp.dma_start(w_in2[n % 2], a["L1_ffn_W"][P * n:P * n + P, :]).then_inc(w2_in[n % 2], 16)
                if n == 1:
                    sp.wait_ge(c_full, 8 * NCH)
                    sp.wait_ge(zh_full, NCH)
                    sp.dma_start(bm, a["L1_ffn_Bmat"]).then_inc(bm_in, 16)
            o_rows = out.rearrange("b h l -> (b h) l").rearrange("(c t p) (two l) -> c p t two l", c=NCH, p=P, two=2)
            with sp.Fori(0, NCH) as c:
                sp.wait_ge(row_free, c * 8 + 12)
                for t in range(4):
                    sp.dma_start(o_rows[bass.ds(c, 1), :, t], rows_out[:, t]).then_inc(out_done, 16)
            sp.wait_ge(out_done, 64 * NCH + 64)

        @block.gpsimd
        def _(pl):
            pl.sem_inc(xm_done, 1)
            pl.sem_inc(lb_done, 4)
            pl.memset(zeros, 0.0).then_inc(pool, 1)
            pl.memset(d_col, 0.0).then_inc(pool, 1)
            pl.memset(small[:, 8:136], 1.0).then_inc(pool, 1)
            pl.memset(small[0:R1_, 3:4], 0.0).then_inc(pool, 1)
            pl.wait_ge(pool, 4)
            for hh in range(4):
                pl.dma_start(d_col[32 * hh:32 * hh + 1, :],
                             a["L0_cond_D"].rearrange("(q hh) -> hh q", hh=4)[hh:hh + 1, :]).then_inc(d_in, 16)
            pl.wait_ge(masks_ready, 1)
            with pl.Fori(0, NQ) as q:
                pl.wait_ge(xq_in, q * 64 + 64)
                pl.wait_ge(px_full, q * 4 + 2)
                pl.tensor_tensor(xm.rearrange("p (c l) -> p c l", c=KC),
                                 xq.rearrange("p (c l) -> p c l", c=KC)[:, :, ::-1],
                                 mask_rev.rearrange("p (c l) -> p c l", c=KC), ALU.mult).then_inc(xm_done, 1)
                pl.wait_ge(lp_in, q * 16 + 16)
                for pr in range(NPAIR):
                    pl.wait_ge(pair_done, q * 4 + pr + 1)
                    for g in range(2):
                        ins = pl.tensor_tensor(
                            lb[pr % 2][:, g], lp[:, 2 * pr + g, 0:51].unsqueeze(2).broadcast_to([P, 51, 8]),
                            cc(C_OWN, 8).unsqueeze(1).broadcast_to([P, 51, 8]), ALU.mult)
                    ins.then_inc(lb_done, 1)

        @block.scalar
        def _(ac):
            ac.sem_inc(px_free, 1)
            ac.sem_inc(sq_done, 1)
            ac.sem_inc(w1_free, 2)
            ac.sem_inc(xres_full, 2)
            ac.sem_inc(bt_done, 2)
            ac.sem_inc(c_free, 4)
            ac.sem_inc(zh_done, 1)
            ac.sem_inc(row_free, 4)
            ac.sem_inc(out_done, 64)
            ac.dma_start(c_in.rearrange("p two n -> p n two"), a["L0_cond_C"]).then_inc(ssm_in, 16)
            for s, name in ((0, "L0_cond_log_A_real"), (1, "L0_cond_A_imag")):
                for d in range(2):
                    ac.dma_start(dup[:, s, d], a[name]).then_inc(ssm_in, 16)
            ac.dma_start(sm[:, 0], a["L0_cond_log_dt"].partition_broadcast(P)).then_inc(ssm_in, 16)
            for n, name in enumerate(("L0_ffn_bias", "L1_cond_b", "L1_ffn_b")):
                ac.dma_start(bias[:, KC * n:KC * n + KC], a[name].rearrange("(m p) -> p m", p=P)).then_inc(bias_in, 16)
            ac.wait_ge(cst_in, 32)
            ac.activation(identb[:, :], ident, ACT.Copy).then_inc(act_id, 1)
            ac.wait_ge(ssm_in, 96)
            for s in range(2):
                for d in range(2):
                    ac.activation(dup[:, 2 + s, d], c_in[:, s], ACT.Copy).then_inc(act_dup, 1)
            ac.activation(sm[:, 1], sm[:, 0], ACT.Exp).then_inc(act_ex, 1)
            ac.wait_ge(pe_dup, 1)
            ac.activation(sm[:, 2], ps[:, 0, 0:64], ACT.Exp).then_inc(act_ex, 1)
            ac.wait_ge(dve_code, 1)
            src = w01[:, 0:2048].bitcast(U8).rearrange("p (o j w k) -> p o w k j", o=8, j=8, w=32)
            for o in range(8):
                ac.activation(codes[:, o].rearrange("p (w k j) -> p w k j", w=32, k=4), src[:, o], ACT.Copy
                              ).then_inc(act_code, 1)
            ac.wait_ge(dve_lo, 1)
            src = q_lo.bitcast(U8).rearrange("p (o j w k) -> p o w k j", o=8, j=8, w=32)
            for o in range(8):
                ac.activation(codes_lo[:, o].rearrange("p (w k j) -> p w k j", w=32, k=4), src[:, o], ACT.Copy
                              ).then_inc(act_lo, 1)
            ac.wait_ge(dve_ssm, 1)
            ac.activation(sm[:, 6], sm[:, 3], ACT.Tanh, scale=0.5).then_inc(act_ex, 1)
            ac.wait_ge(dve_ssm, 2)
            ac.activation(sm[:, 7], sm[:, 5], ACT.Sin, scale=TWO_PI / 2).then_inc(act_ex, 1)
            ac.activation(sm[:, 8], sm[:, 5], ACT.Sin, scale=TWO_PI).then_inc(act_ex, 1)
            for k in range(KC):
                ac.wait_ge(pe_code, k + 1)
                ac.activation(code_t[:, k].bitcast(U8), ps[:, 4 + k % 4, :].bitcast(BF16), ACT.Copy
                              ).then_inc(code_t_ready, 1)
            ac.wait_ge(dve_ssm, 3)
            ac.activation(tp[0], tp[0], ACT.Exp).then_inc(act_big, 1)
            ac.activation(tp[1], tp[1], ACT.Exp).then_inc(act_big, 1)
            for i in range(3):
                ac.wait_ge(dve_ssm, 4 + i)
                ac.activation(tp[2 + i], tp[2 + i], ACT.Sin, scale=TWO_PI).then_inc(act_big, 1)
            ac.wait_ge(bias_in, 48)
            with ac.Fori(0, NQ) as q:
                for k in range(2):
                    ac.wait_ge(px_full, q * 4 + k + 5)
                    ac.activation(ut[:, 4 * k:4 * k + 4], ps[:, 2].rearrange("p (c t) -> p c t", c=4), ACT.Copy
                                  ).then_inc(px_free, 1)
                ac.wait_ge(ys_done, q + 2)
                ac.activation(junk, ys, ACT.Square, accum_out=ssq[:, bass.ds(q, 1)]).then_inc(sq_done, 1)
                for k in range(2):
                    ac.wait_ge(px_full, q * 4 + k + 7)
                    dst = act[:, 4 * k:4 * k + 4, TC:TC + T].rearrange("p c (b h) -> p c b h", b=B)
                    ac.activation(dst[:, :, :, bass.ds(q * 4, 4)],
                                  ps[:, 2].rearrange("p (c hh b) -> p c b hh", c=4, hh=4), ACT.Copy
                                  ).then_inc(px_free, 1)

            ac.wait_ge(mux_free, 8 * NQ + 2)
            ac.wait_ge(pair_done, 4 * NQ + 2)
            with ac.Fori(0, NCH) as c:
                for m in range(KC):
                    ac.wait_ge(xt_full, c * 8 + m + 9)
                    ac.wait_ge(l0_free, c * 8 + m + 1)
                    ac.activation(xres[m % 2], ps[:, 4 + m % 2, :], ACT.Copy).then_inc(xres_full, 1)
                    if m in (1, 5):
                        for b in range(2):
                            ac.wait_ge(w1_full, c * 4 + m // 2 + b + 3)
                            ac.activation(w1t[:, 4 * b:4 * b + 4, bass.ds(c * 256 + P * (m // 4), P)],
                                          ps[:, 6 + b].rearrange("p (k o) -> p k o", k=4), ACT.Copy
                                          ).then_inc(w1_free, 1)
            ac.wait_ge(aw_full, 1)
            ac.wait_ge(aw_in, 64)
            ac.activation(aw[:, :, R1_:R1_ + E], ps[:, 7, 0:64].rearrange("p (k e) -> p k e", e=E), ACT.Copy
                          ).then_inc(aw_done, 1)
            ac.activation(lim_sb[:, R1_:R1_ + E], ps[0:R1_, 7, 64:72], ACT.Copy).then_inc(aw_done, 1)
            with ac.Fori(0, NCH) as c:
                for b in range(2):
                    ac.wait_ge(bt_full, c * 2 + b + 3)
                    ac.activation(lbt[:, TC * b:TC * b + TC], ps[:, 4 + b, :], ACT.Copy).then_inc(bt_done, 1)
                for m in range(KC):
                    ac.wait_ge(c_full, c * 8 + m + 1)
                    ac.activation(mid[:, m, bass.ds(c * TC, TC)], ps[:, m % 4, :], ACT.Identity,
                                  bias=bias[:, KC + m:KC + m + 1]).then_inc(c_free, 1)
                ac.wait_ge(zh_full, c + 1)
                ac.activation(zh[:, bass.ds(c * TC, TC)], ps[0:R1_ + E, 7, :], ACT.Identity, bias=zbias
                              ).then_inc(zh_done, 1)
            def w2_rows(n):
                for b in range(2):
                    ac.wait_ge(w2_full, 2 * n + b + 1)
                    ac.activation(w1t[:, 4 * b:4 * b + 4, P * n:P * n + P],
                                  ps[:, 4 + 2 * (n % 2) + b].rearrange("p (k o) -> p k o", k=4), ACT.Copy
                                  ).then_inc(w2_free, 1)

            for n in range(6):
                w2_rows(n)
            ac.wait_ge(g_dve, 11)
            ac.activation(gs[2], gs[1], ACT.Exp).then_inc(g_act, 1)
            ac.wait_ge(g_dve, 23)
            ac.activation(gs[4], gs[0], ACT.Sigmoid, scale=2.0).then_inc(g_act, 1)
            for n in range(6, KC):
                w2_rows(n)
            for b in range(2):
                ac.wait_ge(g_full, 4 + b)
                ac.activation(wt[:, TC * b:TC * b + TC], ps[0:E, 2 + b, :], ACT.Copy).then_inc(g_act, 1)
            with ac.Fori(0, NCH) as c:
                for m in range(KC):
                    ac.wait_ge(st_used, c * 8 + m + 3)
                    if m == 0:
                        ac.wait_ge(out_done, c * 64 + 64)
                    ac.activation(rows_out[:, :, m // 4, P * (m % 4):P * (m % 4) + P],
                                  ps[:, 4 + m % 4].rearrange("p (t o) -> p t o", t=4), ACT.Copy).then_inc(row_free, 1)

        @block.tensor
        def _(pe):
            pe.sem_inc(conv_done, 1)
            pe.sem_inc(px_full, 4)
            pe.sem_inc(pair_done, 2)
            pe.wait_ge(cst_in, 32)
            pe.wait_ge(act_dup, 4)
            for s in range(4):
                mm = pe.transpose(ps[:, 0, 64 * s:64 * s + 64], dup[:, s].rearrange("p d n -> p (d n)"),
                                  ident[0:H, 0:H])
            mm.then_inc(pe_dup, 1)
            pe.wait_ge(act_id, 1)
            for k in range(KC):
                for o in range(8):
                    pe.wait_ge(act_code, max(o + 1, 8 if k else 0))
                    if k >= 4:
                        pe.wait_ge(code_t_ready, k - 3)
                    mm = pe.transpose(ps[:, 4 + k % 4, :].bitcast(BF16)[:, o * P:o * P + P],
                                      codes[:, o, k * P:k * P + P], identb[:, :])
                mm.then_inc(pe_code, 1)
            pe.wait_ge(p_ready, 1)
            pe.wait_ge(qc_ready, 1)
            for h in range(H):
                r = 32 * (h % 4)
                mm = pe.matmul(ps[r:r + 32, 1, 32 * (h // 4):32 * (h // 4) + 32], tp[2][:, h], tp[4][:, h],
                               start=(h < 4), stop=True, skip_group_check=True)
            mm.then_inc(pe_k, 1)

            with pe.Fori(0, NQ) as q:
                def unit(pr, half):
                    n = q * 4 + pr
                    if half == 0:
                        pe.wait_ge(oh_done, n + 5)
                        pe.wait_ge(lb_done, n + 5)
                    pe.wait_ge(mux_free, n * 2 + half + 1)
                    bank = 4 + 2 * half
                    for it in range(4):
                        k = 4 * half + it
                        dst = ps[:, bank + it // 2, 256 * (it % 2):256 * (it % 2) + 256].rearrange(
                            "p (a o) -> p a o", o=16)
                        for g in range(2):
                            for part in range(3):
                                mm = pe.matmul(dst[:, :, 8 * g:8 * g + 8], oh[pr % 2][:, g, k * P:k * P + P],
                                               lb[pr % 2][:, g, 16 * part:16 * part + 16], start=(part == 0),
                                               stop=(part == 2), skip_group_check=True)
                    mm.then_inc(unit_done, 1)
                    if half == 0:
                        pe.wait_ge(wl_free, n + 1)
                    for it in range(4):
                        k = 4 * half + it
                        for g in range(2):
                            mm = pe.matmul(ps[:, 3, 48 * k + 24 * g:48 * k + 24 * g + 24],
                                           oh[pr % 2][:, g, k * P:k * P + P], lb[pr % 2][:, g, 48:51],
                                           start=True, stop=True, skip_group_check=True)
                    if half == 1:
                        mm.then_inc(pair_done, 1)

                def transposes(src, batch):
                    pe.wait_ge(px_free, q * 4 + batch + 1)
                    for c in range(4):
                        k = 4 * (batch % 2) + c
                        mm = pe.transpose(ps[:, 2, c * P:c * P + P], src[:, k * P:k * P + P], ident)
                    return mm

                unit(0, 0)
                pe.wait_ge(xm_done, q + 2)
                transposes(xm, 0).then_inc(px_full, 1)
                unit(0, 1)
                unit(1, 0)
                mm = transposes(xm, 1)
                mm.then_inc(px_full, 1)
                unit(1, 1)
                pe.wait_ge(px_free, q * 4 + 3)
                pe.wait_ge(toe_in, q * 64 + 64)
                pe.wait_ge(ys_done, q + 1)
                for j in range(KC):
                    for bank in range(2):
                        lo = max(512 * bank, P * j)
                        if lo >= 512 * bank + 512:
                            continue
                        for hh in range(4):
                            mm = pe.matmul(ps[32 * hh:32 * hh + 32, bank, lo - 512 * bank:512],
                                           ut[:, j, 32 * hh:32 * hh + 32],
                                           toe[:, hh, lo - P * j:512 * bank + 512 - P * j],
                                           start=(j == 0), stop=(j == 4 * bank + 3), skip_group_check=True)
                mm.then_inc(conv_done, 1)
                unit(2, 0)
                pe.wait_ge(ys_done, q + 2)
                transposes(ys, 2).then_inc(px_full, 1)
                unit(2, 1)
                unit(3, 0)
                transposes(ys, 3).then_inc(px_full, 1)
                unit(3, 1)

            pe.sem_inc(xt_full, 8)
            pe.sem_inc(w1_full, 2)
            pe.wait_ge(mux_free, 8 * NQ + 2)
            pe.wait_ge(wl_free, 4 * NQ + 1)
            pe.wait_ge(px_free, 4 * NQ + 1)
            with pe.Fori(0, NCH) as c:
                for m in range(KC):
                    pe.wait_ge(l0_free, c * 8 + m + 1)
                    for bank, w in ((m % 2, wl), (2 + m % 2, wh)):
                        for k in range(KC):
                            mm = pe.matmul(ps[:, bank, :], w[:, k, P * m:P * m + P],
                                           act[:, k, bass.ds(c * TC + TC, TC)], start=(k == 0), stop=(k == KC - 1))
                    mm.then_inc(l0_full, 1)
                    if m == 0:
                        pe.wait_ge(xr_in, c * 16 + 16)
                    pe.wait_ge(xres_full, c * 8 + m + 1)
                    for t in range(4):
                        mm = pe.transpose(ps[:, 4 + m % 2, P * t:P * t + P], xrow[:, t, P * m:P * m + P], ident)
                    mm.then_inc(xt_full, 1)
                    if m in (1, 5):
                        pe.wait_ge(w1_in, c * 32 + 16 * (m // 4) + 16)
                        for b in range(2):
                            pe.wait_ge(w1_free, c * 4 + m // 2 + b + 1)
                            for k in range(4):
                                mm = pe.transpose(ps[:, 6 + b, P * k:P * k + P],
                                                  w_in[:, P * (4 * b + k):P * (4 * b + k) + P], ident)
                            mm.then_inc(w1_full, 1)
            pe.sem_inc(in_full, 1)
            pe.sem_inc(bt_full, 2)
            pe.wait_ge(aw_in, 64)
            for k in range(KC):
                pe.transpose(ps[:, 7, E * k:E * k + E], u[0:E, P * k:P * k + P], ident[0:E, 0:E])
            pe.transpose(ps[0:R1_, 7, 64:72], lim_sb[0:E, 0:R1_], ident[0:E, 0:E]).then_inc(aw_full, 1)
            pe.wait_ge(w1_free, 4 * NCH + 2)
            pe.wait_ge(l0_free, 8 * NCH + 2)
            pe.wait_ge(aw_done, 2)
            with pe.Fori(0, NCH) as c:
                pe.wait_ge(lbn_in, c * 128 + 128)
                pe.wait_ge(bt_done, c * 2 + 2)
                for m in range(KC):
                    mm = pe.transpose(ps[:, 4 + m // 4, P * (m % 4):P * (m % 4) + P], lbn[:, m], ident)
                    if m % 4 == 3:
                        mm.then_inc(bt_full, 1)
                pe.wait_ge(la_in, c * 128 + 128)
                pe.wait_ge(in_done, c + 1)
                for k in range(KC):
                    mm = pe.matmul(ps[:, 6, :], la[:, k], act[:, k, bass.ds(c * TC, TC)], start=(k == 0),
                                   stop=(k == KC - 1))
                mm.then_inc(in_full, 1)
                for m in range(KC):
                    pe.wait_ge(c_free, c * 8 + m + 1)
                    for k in range(KC):
                        pe.matmul(ps[:, m % 4, :], w1t[:, k, P * m:P * m + P], act[:, k, bass.ds(c * TC, TC)],
                                  start=(k == 0), stop=False)
                    if m == 0:
                        pe.wait_ge(bt_done, c * 2 + 4)
                        pe.wait_ge(in_done, c + 2)
                    pe.matmul(ps[:, m % 4, :], lbt[:, P * m:P * m + P], inter, start=False, stop=True
                              ).then_inc(c_full, 1)
                pe.wait_ge(c_free, c * 8 + 12)
                pe.wait_ge(zh_done, c + 1)
                for k in range(KC):
                    mm = pe.matmul(ps[0:R1_ + E, 7, :], aw[:, k, :], mid[:, k, bass.ds(c * TC, TC)], start=(k == 0),
                                   stop=(k == KC - 1))
                mm.then_inc(zh_full, 1)
            def w2_rows(n):
                pe.wait_ge(w2_in[n % 2], 16 * (n // 2) + 16)
                for b in range(2):
                    if n >= 2:
                        pe.wait_ge(w2_free, 2 * n + b - 3)
                    for k in range(4):
                        mm = pe.transpose(ps[:, 4 + 2 * (n % 2) + b, P * k:P * k + P],
                                          w_in2[n % 2][:, b, P * k:P * k + P], ident)
                    mm.then_inc(w2_full, 1)

            pe.wait_ge(zh_done, NCH + 1)
            anchors = zh.rearrange("r (n two) -> r n two", two=2)[:, :, 1]
            for g in range(8):
                pe.matmul(ps[:, 0, E * g:E * g + E], anchors[0:R1_, P * g:P * g + P], lim_sb[:, R1_:R1_ + E],
                          start=True, stop=True, skip_group_check=True)
            for g in range(8):
                mm = pe.matmul(ps[:, 3, E * g:E * g + E], anchors[R1_:R1_ + E, P * g:P * g + P],
                               cst[R1_:R1_ + E, R1_:R1_ + E], start=True, stop=True, skip_group_check=True)
            mm.then_inc(g_full, 1)
            w2_rows(0)
            w2_rows(1)
            pe.wait_ge(g_dve, 2)
            pe.transpose(ps[0:2, 1, 0:P], g1[0][:, 0:2], ident).then_inc(g_full, 1)
            w2_rows(2)
            w2_rows(3)
            pe.wait_ge(g_dve, 5)
            pe.matmul(ps[:, 2, 0:2], ones[0:2, :], g1[2][0:2, 0:2], start=True, stop=True).then_inc(g_full, 1)
            for n in range(4, KC):
                w2_rows(n)
            pe.wait_ge(g_dve, 28)
            for g in range(8):
                mm = pe.transpose(ps[0:E, 2 + g // 4, P * (g % 4):P * (g % 4) + P], gs[5][:, g], ident)
                if g % 4 == 3:
                    mm.then_inc(g_full, 1)
            pe.wait_ge(g_act, 4)
            for b in range(2):
                mm = pe.matmul(ps[0:R1_, b, :], lim_sb[0:E, 0:R1_], wt[:, TC * b:TC * b + TC], start=True, stop=True)
            mm.then_inc(g_full, 1)
            pe.sem_inc(st_used, 2)
            pe.wait_ge(w2_free, 16)
            pe.wait_ge(bm_in, 16)
            pe.wait_ge(g_dve, 30)
            with pe.Fori(0, NCH) as c:
                def rows(m):
                    pe.wait_ge(f_free, c * 8 + m + 5)
                    pe.wait_ge(row_free, c * 8 + m + 1)
                    for t in range(4):
                        mm = pe.transpose(ps[:, 4 + m % 4, P * t:P * t + P], stage[m % 2][:, P * t:P * t + P], ident)
                    mm.then_inc(st_used, 1)

                for m in range(KC):
                    pe.wait_ge(f_free, c * 8 + m + 1)
                    for k in range(KC):
                        pe.matmul(ps[:, m % 4, :], w1t[:, k, P * m:P * m + P], mid[:, k, bass.ds(c * TC, TC)],
                                  start=(k == 0), stop=False)
                    pe.matmul(ps[:, m % 4, :], bm[:, P * m:P * m + P], zp[:, bass.ds(c * TC, TC)], start=False,
                              stop=True).then_inc(f_full, 1)
                    if m:
                        rows(m - 1)
                rows(KC - 1)

        @block.vector
        def _(ve):
            count = [0]

            def link(ins):
                count[0] += 1
                ins.then_inc(dve, 1)
                ve.wait_ge(dve, count[0])

            ve.sem_inc(oh_done, 4)
            ve.sem_inc(ys_done, 1)
            ve.sem_inc(mux_free, 2)
            ve.sem_inc(wl_free, 1)
            ve.wait_ge(q_loaded, 128)
            planes = w01[:, 0:2048].bitcast(I32)
            for s, keep in ((4, 0x0F0F0F0F), (2, 0x33333333), (1, 0x55555555)):
                v4 = planes.rearrange("p (x two y) -> p x two y", two=2, y=s * 32)
                lo, hi = v4[:, :, 0], v4[:, :, 1]
                t = q_t.rearrange("p (x y) -> p x y", y=s * 32)
                link(ve.scalar_tensor_tensor(t, lo, s, hi, ALU.logical_shift_right, ALU.bitwise_xor))
                link(ve.tensor_scalar(t, t, keep, None, ALU.bitwise_and))
                link(ve.tensor_tensor(hi, hi, t, ALU.bitwise_xor))
                link(ve.scalar_tensor_tensor(lo, t, s, lo, ALU.logical_shift_left, ALU.bitwise_xor))
            ve.sem_inc(dve_code, 1)
            ve.tensor_scalar(q_lo, planes, 0x0F0F0F0F, None, ALU.bitwise_and).then_inc(dve_lo, 1)
            ve.wait_ge(act_ex, 2)
            link(ve.scalar_tensor_tensor(sm[:, 3], sm[:, 2], -1.0, sm[:, 1], ALU.mult, ALU.mult))
            ve.sem_inc(dve_ssm, 1)
            link(ve.tensor_tensor(sm[:, 4], ps[:, 0, 64:128], sm[:, 1], ALU.mult))
            link(ve.tensor_scalar(sm[:, 4], sm[:, 4], float(1 / (2 * np.pi)), None, ALU.mult))
            link(ve.tensor_scalar(sm[:, 9], sm[:, 4], MAGIC, MAGIC, ALU.add, ALU.subtract))
            link(ve.tensor_tensor(sm[:, 5], sm[:, 4], sm[:, 9], ALU.subtract))
            ve.sem_inc(dve_ssm, 1)
            def over(row, ramp):
                return sm[:, row].unsqueeze(2).broadcast_to([P, H, 32]), ramp.unsqueeze(1).broadcast_to([P, H, 32])

            ve.wait_ge(cst_in, 32)
            r32, r1 = cc(C_R32, 32), cc(C_R1, 32)
            ve.tensor_tensor(tp[0], *over(3, r32), ALU.mult).then_inc(dve, 1)
            count[0] += 1
            link(ve.tensor_tensor(tp[1], *over(3, r1), ALU.mult))
            ve.sem_inc(dve_ssm, 1)
            link(ve.tensor_tensor(tp[5], *over(5, r32), ALU.mult))
            link(ve.tensor_tensor(tp[6], *over(5, r1), ALU.mult))

            def reduced(dst, src, phase, quarter):
                link(ve.tensor_scalar(tp[dst], tp[src], phase, quarter, ALU.add, ALU.add))
                link(ve.tensor_scalar(rnd, tp[dst], MAGIC, MAGIC, ALU.add, ALU.subtract))
                link(ve.tensor_tensor(tp[dst], tp[dst], rnd, ALU.subtract))
                ve.sem_inc(dve_ssm, 1)

            rnd = w01[:, 11264:13312].rearrange("p (h m) -> p h m", h=H)
            ve.wait_ge(lut_loaded, 32)
            ve.tensor_copy(lutp[:, :, :, 0:16], lut_in.rearrange("p o a b -> p o b a")).then_inc(dve, 1)
            count[0] += 1
            link(ve.tensor_copy(lutp[:, :, :, 16:17], lut4_in.unsqueeze(3)))

            def put(part, src):
                ve.tensor_copy(parts[:, :, :, 16 * part:16 * part + 16], src[:, :, :, 0:16]).then_inc(dve, 1)
                count[0] += 1
                link(ve.tensor_copy(parts[:, :, :, 48 + part:49 + part], src[:, :, :, 16:17]))

            def rest(part):
                ve.tensor_tensor(lutp[:, :, :, 0:16], lutp[:, :, :, 0:16], parts[:, :, :, 16 * part:16 * part + 16],
                                 ALU.subtract).then_inc(dve, 1)
                count[0] += 1
                link(ve.tensor_tensor(lutp[:, :, :, 16:17], lutp[:, :, :, 16:17], parts[:, :, :, 48 + part:49 + part],
                                      ALU.subtract))

            link(ve.memset(parts[:, :, :, 51:52], 0.0))
            put(0, lutp)
            rest(0)
            put(1, lutp)
            rest(1)
            put(2, lutp)
            ve.sem_inc(dve_lut, 1)
            reduced(2, 5, cc(C_PHI), 0.25)
            reduced(3, 5, cc(C_PHI), 0.0)
            reduced(4, 6, cc(C_NPHI), 0.25)
            ve.wait_ge(len_in, 80)
            link(ve.tensor_copy(lens[:, 0:1], lens_i))
            ve.tensor_scalar(mask, frow[:, 0], lens[:, 0:1], None, ALU.is_lt).then_inc(dve, 1)
            count[0] += 1
            link(ve.tensor_scalar(mask_rev, frow[:, 1], lens[:, 0:1], None, ALU.is_lt))
            ve.sem_inc(masks_ready, 1)
            ve.wait_ge(act_ex, 5)
            t = lambda n: sm[:, n]
            one_minus, em1 = t(9), t(10)
            link(ve.tensor_scalar(one_minus, t(6), -1.0, 1.0, ALU.mult, ALU.add))
            link(ve.reciprocal(t(11), one_minus))
            link(ve.scalar_tensor_tensor(em1, t(6), 2.0, t(11), ALU.mult, ALU.mult))
            link(ve.scalar_tensor_tensor(t(12), t(7), -2.0, t(7), ALU.mult, ALU.mult))
            link(ve.scalar_tensor_tensor(t(13), t(12), 1.0, em1, ALU.add, ALU.mult))
            link(ve.tensor_tensor(t(13), t(13), t(12), ALU.add))
            link(ve.scalar_tensor_tensor(t(14), em1, 1.0, t(8), ALU.add, ALU.mult))
            cr, ci, ai = ps[:, 0, 128:192], ps[:, 0, 192:256], ps[:, 0, 64:128]
            link(ve.tensor_tensor(t(15), cr, t(13), ALU.mult))
            link(ve.tensor_tensor(t(16), ci, t(14), ALU.mult))
            link(ve.tensor_tensor(t(15), t(15), t(16), ALU.subtract))
            link(ve.tensor_tensor(t(16), cr, t(14), ALU.mult))
            link(ve.tensor_tensor(t(17), ci, t(13), ALU.mult))
            link(ve.tensor_tensor(t(16), t(16), t(17), ALU.add))
            link(ve.tensor_tensor(t(17), t(2), t(2), ALU.mult))
            link(ve.tensor_copy(t(20), ai))
            link(ve.tensor_tensor(t(18), t(20), t(20), ALU.mult))
            link(ve.tensor_tensor(t(17), t(17), t(18), ALU.add))
            link(ve.reciprocal(t(18), t(17)))
            link(ve.tensor_tensor(t(19), t(16), t(20), ALU.mult))
            link(ve.tensor_tensor(t(21), t(15), t(2), ALU.mult))
            link(ve.tensor_tensor(t(19), t(19), t(21), ALU.subtract))
            link(ve.scalar_tensor_tensor(t(22), t(19), 2.0, t(18), ALU.mult, ALU.mult))
            link(ve.tensor_tensor(t(19), t(16), t(2), ALU.mult))
            link(ve.tensor_tensor(t(21), t(15), t(20), ALU.mult))
            link(ve.tensor_tensor(t(19), t(19), t(21), ALU.add))
            link(ve.scalar_tensor_tensor(t(23), t(19), -2.0, t(18), ALU.mult, ALU.mult))
            ve.wait_ge(act_big, 5)
            full = lambda n: sm[:, n].unsqueeze(2).broadcast_to([P, H, 32])
            ve.tensor_tensor(tp[4], tp[4], tp[1], ALU.mult).then_inc(qc_ready, 1)
            link(ve.tensor_tensor(tp[2], tp[2], full(22), ALU.mult))
            link(ve.tensor_tensor(tp[3], tp[3], full(23), ALU.mult))
            link(ve.tensor_tensor(tp[2], tp[2], tp[3], ALU.subtract))
            ve.tensor_tensor(tp[2], tp[2], tp[0], ALU.mult).then_inc(p_ready, 1)
            ve.wait_ge(pe_k, 1)
            link(ve.tensor_copy(kt.rearrange("p q b -> p (q b)"), ps[:, 1, :]))
            ve.wait_ge(d_in, 64)
            ve.wait_ge(pool, 3)
            link(ve.tensor_tensor(kt[:, :, 0], kt[:, :, 0], d_col, ALU.add))
            ve.sem_inc(dve_k, 2)
            ve.wait_ge(code_t_ready, 8)
            ve.wait_ge(lo_stored, 16)
            ve.wait_ge(parts_stored, 16)
            ve.wait_ge(k_stored, 80)

            def quad(q, last):
                ve.wait_ge(mux_free, q * 8 + 2)
                for b in range(4):
                    bit = 0x10101010 << b
                    bit -= (1 << 32) if bit >= 1 << 31 else 0
                    ve.tensor_scalar(bits[:, b], code_t[:, :, bass.ds(q * 16, 16)], bit, None, ALU.bitwise_and
                                     ).then_inc(bits_done, 1)
                ve.wait_ge(bits_done, q * 4 + 4)
                byte = bits.bitcast(U8)
                for pr in range(NPAIR):
                    for half in range(2):
                        base = q * 32 + (8 * pr + 4 * half)
                        t2 = ps[:, 4 + 2 * half:6 + 2 * half, :].rearrange("p x (it a o) -> p (x it) a o", it=2, o=16)
                        ve.wait_ge(unit_done, q * 8 + 2 * pr + half + 1)
                        ve.sem_inc(held, 1)
                        for step, w in enumerate((8, 4, 2, 1)):
                            if step:
                                ve.wait_ge(mux, base + step)
                                ve.sem_inc(held, 1)
                            m = byte[:, 3 - step, 4 * half:4 * half + 4, 16 * pr:16 * pr + 16]
                            ve.copy_predicated(t2[:, :, 0:w], m.unsqueeze(2).broadcast_to([P, 4, w, 16]),
                                               t2[:, :, w:2 * w]).then_inc(mux, 1)
                        ve.wait_ge(mux, base + 4)
                        ve.tensor_copy(wh[:, 4 * half:4 * half + 4, bass.ds(q * 64 + 16 * pr, 16)], t2[:, :, 0]
                                       ).then_inc(mux_free, 1)
                    ve.wait_ge(pair_done, q * 4 + pr + 3)
                    src = ps[:, 3, 0:384].rearrange("p (k g s o) -> p k g o s", k=KC, g=2, s=3)
                    ve.tensor_reduce(wl[:, :, bass.ds(q * 64 + 16 * pr, 16)].rearrange("p k (g o) -> p k g o", g=2),
                                     src, AX.X, ALU.add).then_inc(wl_free, 1)
                    if pr < 2 or not last:
                        nxt = (pr + 2) % 4
                        ve.wait_ge(rep_in[nxt // 2], (q + (pr + 2) // 4) * 64 + 64)
                        ve.tensor_scalar(oh[nxt % 2], rep[nxt // 2][:, nxt % 2].rearrange("p (g i) -> p g i", g=2),
                                         cc(C_LOW), None, ALU.is_equal).then_inc(oh_done, 1)
                    if pr == 1:
                        ve.wait_ge(conv_done, q + 2)
                        ve.wait_ge(px_free, q * 4 + 3)
                        ve.wait_ge(sq_done, q + 1)
                        ve.tensor_tensor(ys, ps[:, 0:2, :].rearrange("p x l -> p (x l)"), mask, ALU.mult
                                         ).then_inc(ys_done, 1)

            for pr in range(2):
                ve.wait_ge(rep_in[0], 64)
                ve.tensor_scalar(oh[pr], rep[0][:, pr].rearrange("p (g i) -> p g i", g=2), cc(C_LOW), None,
                                 ALU.is_equal).then_inc(oh_done, 1)
            with ve.Fori(0, NQ - 1) as q:
                quad(q, False)
            quad(NQ - 1, True)

            ve.wait_ge(sq_done, NQ + 1)
            ve.tensor_scalar(high[:, :], ssq[:, :], EST_T * EST_T, None, ALU.is_gt).then_inc(high_done, 1)
            ve.sem_inc(l0_free, 2)
            ve.wait_ge(high_in, 16)
            with ve.Fori(0, NCH) as c:
                ve.wait_ge(l0_free, c * 8 + 2)
                ve.tensor_copy(high_now, high_all[:, bass.ds(c * TC, TC)]).then_inc(l0_pick, 1)
                for m in range(KC):
                    if m == 0:
                        ve.wait_ge(l0_pick, c + 1)
                    ve.wait_ge(l0_full, c * 8 + m + 1)
                    ve.sem_inc(held, 1)
                    ve.copy_predicated(ps[:, m % 2, :], high_now, ps[:, 2 + m % 2, :]).then_inc(l0_sel, 1)
                    ve.wait_ge(l0_sel, c * 8 + m + 1)
                    ve.wait_ge(xres_full, c * 8 + m + 3)
                    ve.scalar_tensor_tensor(act[:, m, bass.ds(c * TC, TC)], ps[:, m % 2, :], bias[:, m:m + 1],
                                            xres[m % 2], ALU.add, ALU.add).then_inc(l0_free, 1)
            ve.sem_inc(in_done, 1)
            ve.wait_ge(lmask_in, 16)
            with ve.Fori(0, NCH) as c:
                ve.wait_ge(in_full, c + 2)
                ve.tensor_tensor(inter, ps[:, 6, :], lmask, ALU.mult).then_inc(in_done, 1)
            def step(ins):
                gate[0] += 1
                ins.then_inc(g_dve, 1)
                ve.wait_ge(g_dve, gate[0])

            gate = [0]
            wide = lambda x: x.unsqueeze(2).broadcast_to([P, 8, E])
            ve.wait_ge(g_full, 1)
            step(ve.tensor_copy(gt.rearrange("p s g e -> p s (g e)"), ps[:, 0:4:3, 0:64]))
            step(ve.tensor_reduce(g1[0][:, 0:2], gt, AX.XY, ALU.max, apply_absolute_value=True))
            ve.wait_ge(g_full, 2)
            step(ve.tensor_reduce(g1[1][0:2, 0:1], ps[0:2, 1, 0:P], AX.X, ALU.max))
            step(ve.tensor_scalar(g1[1][0:2, 1:2], g1[1][0:2, 0:1], 1e-6, None, ALU.max))
            step(ve.tensor_scalar(g1[2][0:2, 0:2], cst[0:2, 0:2], g1[1][0:2, 1:2], None, ALU.mult))
            ve.wait_ge(g_full, 3)
            step(ve.reciprocal(g1[3][:, 0:2], ps[:, 2, 0:2]))
            step(ve.tensor_scalar(g1[3][:, 2:4], g1[3][:, 0:2], 0.5, None, ALU.mult))
            step(ve.tensor_scalar(gs[0], gt[:, 0], g1[3][:, 2:3], None, ALU.mult))
            step(ve.scalar_tensor_tensor(gs[0], gt[:, 1], g1[3][:, 3:4], gs[0], ALU.mult, ALU.add))
            step(ve.tensor_reduce(g1[4], gs[0], AX.X, ALU.max))
            step(ve.tensor_tensor(gs[1], gs[0], wide(g1[4]), ALU.subtract))
            ve.wait_ge(g_act, 1)
            step(ve.tensor_reduce(g1[5], gs[2], AX.X, ALU.add))
            step(ve.reciprocal(g1[6], g1[5]))
            step(ve.tensor_tensor(gs[1], gs[2], wide(g1[6]), ALU.mult))
            for g in range(8):
                step(ve.max(gs[3][:, g], gs[1][:, g]))
            step(ve.tensor_tensor(gs[0], gs[1], wide(gs[3][:, :, 1]), ALU.subtract))
            ve.wait_ge(g_act, 2)
            step(ve.tensor_tensor(gs[2], gs[1], gs[4], ALU.mult))
            step(ve.tensor_reduce(g1[7], gs[2], AX.X, ALU.add))
            step(ve.tensor_scalar(g1[8], g1[7], 1e-9, None, ALU.add))
            step(ve.reciprocal(g1[9], g1[8]))
            step(ve.tensor_tensor(gs[5], gs[2], wide(g1[9]), ALU.mult))
            ve.wait_ge(g_full, 6)
            for b in range(2):
                step(ve.scalar_tensor_tensor(
                    zp[:, 2 * TC * b:2 * TC * b + 2 * TC].rearrange("r (n two) -> r n two", two=2),
                    zh[0:R1_, 2 * TC * b:2 * TC * b + 2 * TC].rearrange("r (n two) -> r n two", two=2), DELTA_SCALE,
                    ps[0:R1_, b, :].unsqueeze(2).broadcast_to([R1_, TC, 2]), ALU.mult, ALU.mult))
            ve.sem_inc(f_free, 4)
            with ve.Fori(0, NCH) as c:
                for m in range(KC):
                    ve.wait_ge(f_full, c * 8 + m + 1)
                    ve.wait_ge(st_used, c * 8 + m + 1)
                    ve.scalar_tensor_tensor(stage[m % 2], ps[:, m % 4, :], bias[:, 2 * KC + m:2 * KC + m + 1],
                                            act[:, m, bass.ds(c * TC, TC)], ALU.add, ALU.add).then_inc(f_free, 1)


_INPUTS = ["x", "itok_B_8_3872", "itok_B_14_62", "L0_cond_log_dt", "L0_cond_C", "L0_cond_log_A_real", "L0_cond_A_imag",
           "L0_cond_D", "L0_ffn_qweight", "L0_ffn_lut4", "L0_ffn_lut8", "L0_ffn_bias", "L1_cond_W", "L1_cond_b",
           "L1_cond_lora_A", "L1_cond_lora_B", "L1_ffn_W", "L1_ffn_b", "L1_ffn_A", "L1_ffn_Bmat", "L1_ffn_LiMEs"]


def kernel(**inputs):
    import concourse.bacc as bacc
    from concourse.bass_utils import run_bass_kernel_spmd

    nc = bacc.Bacc("TRN2", target_bir_lowering=False, num_devices=1)
    arrays = {name: np.ascontiguousarray(inputs[name]) for name in _INPUTS}
    arrays["cst"], arrays["feature_rows"] = shape_constants()
    aps = {name: nc.dram_tensor("in_" + name, x.shape, mybir.dt.from_np(x.dtype), kind="ExternalInput").ap()
           for name, x in arrays.items()}
    out = nc.dram_tensor("out_rows", (B, H, L), F32, kind="ExternalOutput").ap()
    build_kernel(nc, aps, out)
    result = run_bass_kernel_spmd(nc, [{"in_" + name: x for name, x in arrays.items()}], core_ids=[0])
    return result.results[0]["out_rows"]
```

```python
from contextlib import ExitStack

import numpy as np

import concourse.bass as bass
from concourse import mybir

F32 = mybir.dt.float32
BF16 = mybir.dt.bfloat16
I32 = mybir.dt.int32
I16 = mybir.dt.int16
U8 = mybir.dt.uint8
ALU = mybir.AluOpType
ACT = mybir.ActivationFunctionType
AX = mybir.AxisListType

P = 128
B, H, L = 32, 64, 1024
T = B * H
KC = L // P
N = 64
NQ = H // 4
TC = 512
NCH = T // TC
R0, R1_, E = 16, 32, 8
BC = TC // H
EST_T = 64.0
LORA_SCALE = 2.0
DELTA_SCALE = 0.5
TWO_PI = 6.283185
MAGIC = 12582912.0
KPAD = P + L
A17 = 17
LW = 3 * A17 + 1
SPLITS = ((0, 3), (3, 6), (6, 8))
NPAIR = 4

C_ID, C_LORA, C_R32, C_R1, C_PHI, C_NPHI, C_LOW, C_OWN, C_PHI4, C_NPHI4, C_END = (
    0, 128, 640, 672, 704, 705, 706, 707, 715, 716, 717)


def shape_constants():
    p = np.arange(P)
    c = np.zeros((P, C_END), np.float32)
    c[:, C_ID:C_ID + P] = np.eye(P)
    c[:, C_LORA:C_LORA + TC] = LORA_SCALE * (p[:, None] // R0 == np.arange(TC)[None] // H)
    c[:, C_R32:C_R32 + 32] = 32 * np.arange(32)
    c[:, C_R1:C_R1 + 32] = np.arange(32)
    c[:, C_PHI] = 0.25 * (p >= N)
    c[:, C_NPHI] = -0.25 * (p >= N)
    c[:, C_LOW] = p % 16
    c[:, C_OWN:C_OWN + 8] = p[:, None] // 16 == np.arange(8)[None]
    c[:, C_PHI4] = c[:, C_PHI] + 0.25
    c[:, C_NPHI4] = c[:, C_NPHI] + 0.25
    feature = np.arange(L, dtype=np.float32)
    return c, np.stack([feature, feature.reshape(KC, P)[:, ::-1].reshape(L)])


def build_kernel(nc, a, out):
    k_pad = nc.dram_tensor("k_pad", (H, KPAD), F32).ap()
    code_lo = nc.dram_tensor("code_lo", (L, L), U8).ap()
    lut_parts = nc.dram_tensor("lut_parts", (L, 16 * LW), BF16).ap()
    high_rows = nc.dram_tensor("high_rows", (T,), U8).ap()

    ctx = ExitStack()
    with ctx:
        ctx.enter_context(nc.allow_non_contiguous_dma(reason="biases and the skip weights: a few KB, once"))

        def sb(name, shape, dt):
            return ctx.enter_context(nc.sbuf_tensor(name, shape, dt))

        def sem(name):
            return ctx.enter_context(nc.semaphore(name))

        act = sb("act", [P, KC, TC + T], F32)
        w01 = sb("w01", [P, 2 * KC * L], F32)
        w2 = sb("w2", [P, KC * L], F32)
        r3 = sb("r3", [P, 4 * L], F32)
        u = sb("u", [P, 2048], F32)
        v = sb("v", [P, 1024], F32)
        cst = sb("cst", [P, C_END - 512], F32)
        identb = sb("identb", [P, P], BF16)
        bias = sb("bias", [P, 3 * KC + 1], F32)
        ids = sb("ids", [1, B], I32)
        ssq = sb("ssq", [P, NQ], F32)
        high = sb("high", [P, NQ], U8)
        aw = sb("aw", [P, KC, R1_ + E], F32)
        small = sb("small", [P, 136], F32)
        lim_sb = sb("lim_sb", [R1_, R1_ + E], F32)
        ps = ctx.enter_context(nc.psum_tensor("ps", [P, 8, 512], F32))

        ident = cst[:, C_ID:C_ID + P]

        def cc(at, n=1):
            at = at if at < C_LORA else at - 512
            return cst[:, at:at + n]

        wl = w01[:, 0:KC * L].rearrange("p (k o) -> p k o", k=KC)
        wh = w01[:, KC * L:2 * KC * L].rearrange("p (k o) -> p k o", k=KC)

        w2b = w2[:, :]
        ut = w2b[:, 0:1024].rearrange("p (c t) -> p c t", c=KC)
        xq = w2b[:, 1024:2048]
        xm = w2b[:, 2048:3072]
        ys = w2b[:, 3072:4096]
        code_t = w2b[:, 4096:6144].bitcast(I32).rearrange("p (k o) -> p k o", k=KC)
        bits = w2b[:, 6144:6656].bitcast(I32).rearrange(
            "p (b g k o) -> p b g k o", b=4, g=8, k=KC)
        mask = w2b[:, 6656:7168].bitcast(BF16)
        mask_rev = w2b[:, 7168:7680].bitcast(BF16)
        lp = w2b[:, 7680:7680 + 8 * LW // 2].bitcast(BF16).rearrange("p (g w) -> p g w", w=LW)
        lb = [u[:, 512 * i:512 * i + 408].bitcast(BF16).rearrange("p (g s o a) -> p g s o a", g=2, s=3, o=8)
              for i in range(2)]
        junk = u[:, 1024:1536].bitcast(BF16)
        toe = r3[:, :].rearrange("p (h c) -> p h c", h=4)
        oh = [act[:, 2 * i:2 * i + 2, 0:TC].bitcast(BF16) for i in range(2)]
        rep = [act[:, 4 + 2 * i:6 + 2 * i, 0:TC].bitcast(U8) for i in range(2)]

        q_in = w01[:, 0:2048].bitcast(I32).rearrange("p (o b w) -> p o b w", o=8, b=8)
        q_t = w01[:, 2048:3072].bitcast(I32)
        q_lo = w01[:, 3072:5120].bitcast(I32)
        codes = w01[:, 5120:9216].bitcast(BF16).rearrange("p (o i) -> p o i", o=8)
        codes_lo = w01[:, 9216:11264].bitcast(U8).rearrange("p (o i) -> p o i", o=8)
        lut_in = w01[:, 11264:13312].rearrange("p (o a b) -> p o a b", o=8, a=16)
        lut4_in = w01[:, 13312:13440].rearrange("p (o b) -> p o b", o=8)
        parts = r3[:, 0:4 * 16 * LW].bitcast(BF16).rearrange("p (o b w) -> p o b w", o=8, b=16)
        rnd, *tp = [act[:, k, TC:TC + 2048].rearrange("p (h m) -> p h m", h=H) for k in range(8)]
        sm = w01[:, 13440:13440 + 24 * 64].rearrange("p (s h) -> p s h", h=64)
        c_in = w01[0:H, 14976:15104].rearrange("p (n two) -> p two n", two=2)
        dup = w01[0:H, 15104:15616].rearrange("p (s d n) -> p s d n", s=4, d=2)
        kt = w01[:, 15616:16128].rearrange("p (q b) -> p q b", q=NQ)
        d_col = w01[:, 16128:16144]
        zeros = w01[0:H, 16144:16272]
        lens = small[:, 0:2]
        lens_i = small[:, 2:3].bitcast(I32)
        frow = w2b[:, 0:2048].rearrange("p (two l) -> p two l", two=2)

        xrow = r3[:, :].rearrange("p (t l) -> p t l", t=4)
        xres = [u[:, TC * i:TC * i + TC] for i in range(2)]
        w_in = u[:, 1024:2048]
        high_all = v[:, 0:T // 4].bitcast(U8)
        high_now = v[:, T // 4:T // 4 + TC // 4].bitcast(U8)
        w1t = w2[:, :].rearrange("p (k o) -> p k o", k=KC)
        mid = w01[:, :].rearrange("p (k t) -> p k t", k=KC)
        la = r3[:, 0:1024].rearrange("p (k r) -> p k r", k=KC)
        lbn = r3[:, 1024:2048].rearrange("p (m r) -> p m r", m=KC)
        lbt = r3[:, 2048:3072]
        inter = r3[:, 3072:3584]
        lmask = r3[:, 3584:4096]
        zh = u[0:R1_ + E, 0:T]
        zbias = small[0:R1_ + E, 3:4]
        ones = small[:, 8:136]
        lim = lim_sb[:, :]
        tail = act[:, :, T:T + TC]
        gt = tail[:, 0, 0:128].rearrange("p (s g e) -> p s g e", s=2, g=8)
        gs = [tail[:, 0, 128 + 64 * i:192 + 64 * i].rearrange("p (g e) -> p g e", g=8) for i in range(6)]
        g1 = [tail[:, 1, 8 * i:8 * i + 8] for i in range(12)]
        w_in2 = [tail[:, 4 + 2 * i:6 + 2 * i, :] for i in range(2)]
        zp = r3[0:R1_, 0:T]
        bm = r3[0:R1_, T:T + L]
        wt = r3[0:E, T + L:T + 2 * L]
        stage = [v[:, TC * i:TC * i + TC] for i in range(2)]
        rows_out = tail.rearrange("p (t two) l -> p t two l", two=2)

        cst_in = sem("cst_in"); ssm_in = sem("ssm_in"); q_loaded = sem("q_loaded"); lut_loaded = sem("lut_loaded")
        len_in = sem("len_in"); d_in = sem("d_in"); bias_in = sem("bias_in")
        held = sem("held")
        dve = sem("dve"); pool = sem("pool")
        act_id = sem("act_id"); act_dup = sem("act_dup"); act_ex = sem("act_ex"); act_big = sem("act_big")
        act_code = sem("act_code"); pool_pow = sem("pool_pow"); pool_parts = sem("pool_parts"); act_shift = sem("act_shift")
        act_lo = sem("act_lo"); code_t_ready = sem("code_t_ready")
        dve_lo = sem("dve_lo"); dve_ssm = sem("dve_ssm"); dve_k = sem("dve_k")
        pe_dup = sem("pe_dup"); pe_code = sem("pe_code"); pe_k = sem("pe_k")
        masks_ready = sem("masks_ready"); p_ready = sem("p_ready"); qc_ready = sem("qc_ready")
        k_stored = sem("k_stored"); lo_stored = sem("lo_stored"); parts_stored = sem("parts_stored")
        xq_in = sem("xq_in"); toe_hi_in = sem("toe_hi_in"); toe_lo_in = sem("toe_lo_in"); conv_hi = sem("conv_hi"); rep_in = [sem("rep_in0"), sem("rep_in1")]; lp_in = sem("lp_in")
        xm_done = sem("xm_done"); lb_done = sem("lb_done"); oh_done = sem("oh_done")
        px_full = sem("px_full"); px_free = sem("px_free"); conv_done = sem("conv_done"); ys_done = sem("ys_done")
        sq_done = sem("sq_done"); unit_done = sem("unit_done");
        mux = [sem("mux%d" % n) for n in range(4)]; mux_free = sem("mux_free"); bits_done = sem("bits_done")

        high_done = sem("high_done"); high_out = sem("high_out"); high_in = sem("high_in"); xr_in = sem("xr_in")
        l0_full = sem("l0_full"); l0_free = sem("l0_free"); l0_sel = sem("l0_sel"); l0_pick = sem("l0_pick"); xt_full = sem("xt_full")
        xres_full = sem("xres_full"); w1_in = sem("w1_in"); w1_full = sem("w1_full"); w1_free = sem("w1_free")
        ids_in = sem("ids_in"); aw_in = sem("aw_in"); lmask_in = sem("lmask_in"); la_in = sem("la_in"); lbn_in = sem("lbn_in")
        aw_full = sem("aw_full"); aw_done = sem("aw_done"); bt_full = sem("bt_full"); bt_done = sem("bt_done")
        in_full = sem("in_full"); in_done = sem("in_done"); c_full = sem("c_full"); c_free = sem("c_free")
        zh_full = sem("zh_full"); zh_done = sem("zh_done")
        g_full = sem("g_full"); g_dve = sem("g_dve"); g_act = sem("g_act"); w2_in = [sem("w2_in0"), sem("w2_in1")]
        w2_full = sem("w2_full"); w2_free = sem("w2_free"); bm_in = sem("bm_in")
        f_full = sem("f_full"); f_free = sem("f_free"); st_used = sem("st_used"); row_free = sem("row_free")
        out_done = sem("out_done")

        block = ctx.enter_context(nc.Block())

        @block.sync
        def _(sp):
            sp.dma_start(cst[:, 0:P], a["cst"][:, 0:P]).then_inc(cst_in, 16)
            sp.dma_start(cst[:, P:C_END - 512], a["cst"][:, 640:C_END]).then_inc(cst_in, 16)
            for b in range(8):
                sp.dma_start(q_in[:, :, b, :], a["L0_ffn_qweight"][b].rearrange("(o p) w -> p o w", p=P)
                             ).then_inc(q_loaded, 16)
            sp.dma_start(ids[:, :], a["itok_B_14_62"].rearrange("(one b) -> one b", one=1)).then_inc(ids_in, 16)
            sp.dma_start(frow, a["feature_rows"].partition_broadcast(P)).then_inc(len_in, 16)
            for hh in range(4):
                sp.dma_start(lens_i[32 * hh:32 * hh + 32, :],
                             a["itok_B_8_3872"].rearrange("(b one) -> b one", one=1)).then_inc(len_in, 16)
            sp.dma_start(lut_in, a["L0_ffn_lut8"].rearrange("(o p) (a b) -> p o a b", p=P, a=16)).then_inc(lut_loaded, 16)
            sp.dma_start(lut4_in, a["L0_ffn_lut4"].rearrange("(o p) b -> p o b", p=P)).then_inc(lut_loaded, 16)
            sp.wait_ge(pool_parts, 1)
            sp.dma_start(lut_parts.rearrange("(o p) w -> p o w", p=P), parts.rearrange("p o b w -> p o (b w)")
                         ).then_inc(parts_stored, 16)
            sp.wait_ge(act_lo, 8)
            sp.dma_start(code_lo.rearrange("(o p) i -> p o i", p=P), codes_lo).then_inc(lo_stored, 16)
            sp.wait_ge(masks_ready, 1)
            x_h = a["x"].rearrange("b h l -> h b l")
            lo_rep = bass.AP(code_lo.tensor, 0, [[64 * L, NQ], [8 * L, 8], [L, 8], [0, 16], [1, L]])
            lp_src = lut_parts.rearrange("(q g o) (b w) -> q (o b) g w", q=NQ, g=8, w=LW)
            toe_src = bass.AP(k_pad.tensor, 1, [[4 * KPAD, NQ], [1, P], [KPAD, 4], [1, L]])
            with sp.Fori(0, NQ) as q:
                sp.wait_ge(xm_done, q + 1)
                for hh in range(4):
                    sp.dma_start(xq[32 * hh:32 * hh + 32], x_h[bass.ds(q * 4 + hh, 1)].rearrange("h b l -> (h b) l")
                                 ).then_inc(xq_in, 16)
                sp.wait_ge(lo_stored, 16)
                for half in range(2):
                    sp.wait_ge(oh_done, q * 4 + 2 * half + 2)
                    sp.sem_inc(held, 1)
                    for g in range(4):
                        sp.dma_start(rep[half][:, g // 2, (g % 2) * L:(g % 2 + 1) * L],
                                     lo_rep[bass.ds(q, 1), 4 * half + g]
                                     ).then_inc(rep_in[half], 16)
                sp.wait_ge(parts_stored, 16)
                sp.wait_ge(lb_done, q * 4 + 4)
                sp.sem_inc(held, 1)
                sp.dma_start(lp, lp_src[bass.ds(q, 1)]).then_inc(lp_in, 16)
                sp.wait_ge(k_stored, 80)
                for part, sem_in, used in ((1, toe_hi_in, conv_hi), (0, toe_lo_in, conv_done)):
                    sp.wait_ge(used, q + 1)
                    for hh in range(4):
                        sp.dma_start(toe[:, hh, 512 * part:512 * part + 512],
                                     toe_src[bass.ds(q, 1), :, hh, 512 * part:512 * part + 512]).then_inc(sem_in, 16)

            sp.wait_ge(high_done, 1)
            for hh in range(4):
                sp.dma_start(high_rows.rearrange("(b q hh) -> hh b q", q=NQ, hh=4)[hh], high[32 * hh:32 * hh + 32, :]
                             ).then_inc(high_out, 16)
            sp.wait_ge(high_out, 64)
            sp.dma_start(high_all, high_rows.partition_broadcast(P)).then_inc(high_in, 16)
            sp.wait_ge(sq_done, NQ + 1)
            sp.wait_ge(unit_done, 12 * NQ + 6)
            x_rows = a["x"].rearrange("b h l -> (b h) l").rearrange("(c t p) l -> c p t l", c=NCH, p=P)
            with sp.Fori(0, NCH) as c:
                sp.wait_ge(xt_full, c * 8 + 8)
                sp.dma_start(xrow, x_rows[bass.ds(c, 1)]).then_inc(xr_in, 16)
                for s in range(2):
                    sp.wait_ge(w1_full, c * 4 + 2 * s + 2)
                    sp.dma_start(w_in, a["L1_cond_W"].rearrange("(n p) i -> n p i", p=P)[bass.ds(c * 2 + s, 1)]
                                 ).then_inc(w1_in, 16)
            sp.wait_ge(l0_free, 8 * NCH + 2)
            sp.wait_ge(w1_full, 4 * NCH + 2)
            sp.dma_start(u[0:E, 0:L], a["L1_ffn_W"][0:E, :]).then_inc(aw_in, 16)
            sp.dma_start(aw[:, :, 0:R1_], a["L1_ffn_A"].rearrange("(k p) r -> p k r", p=P)).then_inc(aw_in, 16)
            sp.dma_start(lim_sb[0:E, 0:R1_], a["L1_ffn_LiMEs"]).then_inc(aw_in, 16)
            sp.dma_start(small[R1_:R1_ + E, 3:4], a["L1_ffn_b"][0:E].rearrange("(e one) -> e one", one=1)
                         ).then_inc(aw_in, 16)
            sp.dma_start(lmask, a["cst"][:, C_LORA:C_LORA + TC]).then_inc(lmask_in, 16)
            sp.wait_ge(ids_in, 16)
            lora_a = a["L1_cond_lora_A"].rearrange("n (k p) r -> n p k r", p=P)
            lora_b = a["L1_cond_lora_B"].rearrange("n (k p) r -> n p k r", p=P)
            with sp.Fori(0, NCH) as c:
                sp.wait_ge(in_full, c + 1)
                sp.wait_ge(bt_full, c * 2 + 2)
                for n in range(BC):
                    who = sp.value_load(ids[0:1, bass.ds(c * BC + n, 1)], min_val=0, max_val=63)
                    sp.dma_start(la[:, :, R0 * n:R0 * n + R0], lora_a[bass.ds(who, 1)]).then_inc(la_in, 16)
                    sp.dma_start(lbn[:, :, R0 * n:R0 * n + R0], lora_b[bass.ds(who, 1)]).then_inc(lbn_in, 16)
            for n in range(KC):
                if n >= 2:
                    sp.wait_ge(w2_full, 2 * n - 2)
                sp.dma_start(w_in2[n % 2], a["L1_ffn_W"][P * n:P * n + P, :]).then_inc(w2_in[n % 2], 16)
                if n == 1:
                    sp.wait_ge(c_full, 8 * NCH)
                    sp.wait_ge(zh_full, NCH)
                    sp.dma_start(bm, a["L1_ffn_Bmat"]).then_inc(bm_in, 16)
            o_rows = out.rearrange("b h l -> (b h) l").rearrange("(c t p) (two l) -> c p t two l", c=NCH, p=P, two=2)
            with sp.Fori(0, NCH) as c:
                sp.wait_ge(row_free, c * 8 + 12)
                for t in range(4):
                    sp.dma_start(o_rows[bass.ds(c, 1), :, t], rows_out[:, t]).then_inc(out_done, 16)
            sp.wait_ge(out_done, 64 * NCH + 64)

        @block.gpsimd
        def _(pl):
            pl.sem_inc(xm_done, 1)
            pl.sem_inc(lb_done, 4)
            pl.memset(zeros, 0.0).then_inc(pool, 1)
            pl.memset(d_col, 0.0).then_inc(pool, 1)
            pl.memset(small[:, 8:136], 1.0).then_inc(pool, 1)
            pl.memset(small[0:R1_, 3:4], 0.0).then_inc(pool, 1)
            pl.wait_ge(pool, 4)
            for hh in range(4):
                pl.dma_start(d_col[32 * hh:32 * hh + 1, :],
                             a["L0_cond_D"].rearrange("(q hh) -> hh q", hh=4)[hh:hh + 1, :]).then_inc(d_in, 16)
            def over(row, ramp):
                return sm[:, row].unsqueeze(2).broadcast_to([P, H, 32]), ramp.unsqueeze(1).broadcast_to([P, H, 32])

            pl.wait_ge(cst_in, 32)
            pl.wait_ge(dve_ssm, 1)
            pl.tensor_tensor(tp[0], *over(3, cc(C_R32, 32)), ALU.mult).then_inc(pool_pow, 1)
            pl.tensor_tensor(tp[1], *over(3, cc(C_R1, 32)), ALU.mult).then_inc(pool_pow, 1)
            pl.wait_ge(lut_loaded, 32)
            lut_t = lut_in.rearrange("p o a b -> p o b a")
            count = [4]

            def link(*instructions):
                for ins in instructions:
                    ins.then_inc(pool, 1)
                count[0] += len(instructions)
                pl.wait_ge(pool, count[0])

            link(pl.memset(parts[:, :, :, 3 * A17:LW], 0.0))
            for part in range(3):
                high_part, low_part = (parts[:, :, :, A17 * part:A17 * part + 16],
                                       parts[:, :, :, A17 * part + 16:A17 * part + 17])
                link(pl.tensor_copy(high_part, lut_t), pl.tensor_copy(low_part, lut4_in.unsqueeze(3)))
                if part < 2:
                    link(pl.tensor_tensor(lut_t, lut_t, high_part, ALU.subtract),
                         pl.tensor_tensor(lut4_in.unsqueeze(3), lut4_in.unsqueeze(3), low_part, ALU.subtract))
            pl.sem_inc(pool_parts, 1)
            pl.wait_ge(act_big, 5)
            pl.tensor_tensor(tp[4], tp[4], tp[1], ALU.mult).then_inc(qc_ready, 1)
            pl.wait_ge(masks_ready, 1)
            with pl.Fori(0, NQ) as q:
                pl.wait_ge(xq_in, q * 64 + 64)
                pl.wait_ge(px_full, q * 4 + 2)
                pl.tensor_tensor(xm.rearrange("p (c l) -> p c l", c=KC),
                                 xq.rearrange("p (c l) -> p c l", c=KC)[:, :, ::-1],
                                 mask_rev.rearrange("p (c l) -> p c l", c=KC), ALU.mult).then_inc(xm_done, 1)
                pl.wait_ge(lp_in, q * 16 + 16)
                for pr in range(NPAIR):
                    pl.wait_ge(unit_done, q * 12 + 3 * pr + 3)
                    for g in range(2):
                        ins = pl.tensor_tensor(
                            lb[pr % 2][:, g],
                            lp[:, 2 * pr + g, 0:3 * A17].rearrange("p (s a) -> p s a", s=3).unsqueeze(2)
                            .broadcast_to([P, 3, 8, A17]),
                            cc(C_OWN, 8).unsqueeze(1).unsqueeze(3).broadcast_to([P, 3, 8, A17]), ALU.mult)
                    ins.then_inc(lb_done, 1)

        @block.scalar
        def _(ac):
            ac.sem_inc(px_free, 2)
            ac.sem_inc(mux_free, 3)
            ac.sem_inc(sq_done, 1)
            ac.sem_inc(w1_free, 2)
            ac.sem_inc(xres_full, 2)
            ac.sem_inc(bt_done, 2)
            ac.sem_inc(c_free, 4)
            ac.sem_inc(zh_done, 1)
            ac.sem_inc(row_free, 4)
            ac.sem_inc(out_done, 64)
            ac.dma_start(c_in.rearrange("p two n -> p n two"), a["L0_cond_C"]).then_inc(ssm_in, 16)
            for s, name in ((0, "L0_cond_log_A_real"), (1, "L0_cond_A_imag")):
                for d in range(2):
                    ac.dma_start(dup[:, s, d], a[name]).then_inc(ssm_in, 16)
            ac.dma_start(sm[:, 0], a["L0_cond_log_dt"].partition_broadcast(P)).then_inc(ssm_in, 16)
            for n, name in enumerate(("L0_ffn_bias", "L1_cond_b", "L1_ffn_b")):
                ac.dma_start(bias[:, KC * n:KC * n + KC], a[name].rearrange("(m p) -> p m", p=P)).then_inc(bias_in, 16)
            ac.wait_ge(cst_in, 32)
            ac.activation(identb[:, :], ident, ACT.Copy).then_inc(act_id, 1)
            ac.wait_ge(ssm_in, 96)
            for s in range(2):
                for d in range(2):
                    ac.activation(dup[:, 2 + s, d], c_in[:, s], ACT.Copy).then_inc(act_dup, 1)
            ac.activation(sm[:, 1], sm[:, 0], ACT.Exp).then_inc(act_ex, 1)
            ac.wait_ge(pe_dup, 1)
            ac.activation(sm[:, 2], ps[:, 0, 0:64], ACT.Exp).then_inc(act_ex, 1)
            ac.wait_ge(dve_ssm, 1)
            ac.activation(sm[:, 6], sm[:, 3], ACT.Tanh, scale=0.5).then_inc(act_ex, 1)
            ac.wait_ge(dve_ssm, 2)
            ac.activation(sm[:, 7], sm[:, 5], ACT.Sin, scale=TWO_PI / 2).then_inc(act_ex, 1)
            ac.activation(sm[:, 8], sm[:, 5], ACT.Sin, scale=TWO_PI).then_inc(act_ex, 1)
            for i, (base, shift) in enumerate(((5, C_PHI4), (5, C_PHI), (6, C_NPHI4))):
                ac.wait_ge(dve_ssm, base - 2)
                ac.activation(tp[2 + i], tp[base], ACT.Identity, bias=cc(shift)).then_inc(act_shift, 1)
            for i in range(2):
                ac.wait_ge(pool_pow, i + 1)
                ac.activation(tp[i], tp[i], ACT.Exp).then_inc(act_big, 1)
            ac.wait_ge(dve_lo, 1)
            src = q_lo.bitcast(U8).rearrange("p (o j w k) -> p o w k j", o=8, j=8, w=32)
            for o in range(8):
                ac.activation(codes_lo[:, o].rearrange("p (w k j) -> p w k j", w=32, k=4), src[:, o], ACT.Copy
                              ).then_inc(act_lo, 1)
            for i in range(3):
                ac.wait_ge(dve_ssm, 5 + i)
                ac.activation(tp[2 + i], tp[2 + i], ACT.Sin, scale=TWO_PI).then_inc(act_big, 1)
            src = w01[:, 0:2048].bitcast(U8).rearrange("p (o j w k) -> p o w k j", o=8, j=8, w=32)
            for o in range(8):
                ac.activation(codes[:, o].rearrange("p (w k j) -> p w k j", w=32, k=4), src[:, o], ACT.Copy
                              ).then_inc(act_code, 1)
            for k in range(KC):
                ac.wait_ge(pe_code, k + 1)
                ac.activation(code_t[:, k].bitcast(U8), ps[:, 4 + k % 4, :].bitcast(BF16), ACT.Copy
                              ).then_inc(code_t_ready, 1)
            ac.wait_ge(bias_in, 48)
            def take(q, u):
                pr, j = u // 3, u % 3
                ac.wait_ge(mux[3], q * 12 + u + 2)
                first, end = SPLITS[j]
                src = ps[:, 2 + 2 * j:4 + 2 * j, 0:A17 * 8 * (end - first)].rearrange(
                    "p g (k o a) -> p g k o a", a=A17, o=8)
                for w, row in ((wh, 0), (wl, 16)):
                    ins = ac.activation(
                        w[:, first:end, bass.ds(q * 64 + 16 * pr, 16)].rearrange("p k (g o) -> p g k o", g=2),
                        src[:, :, :, :, row], ACT.Copy)
                ins.then_inc(mux_free, 1)

            def masked_rows(q):
                for k in range(2):
                    ac.wait_ge(px_full, q * 4 + k + 5)
                    ac.activation(ut[:, 4 * k:4 * k + 4], ps[:, k].rearrange("p (c t) -> p c t", c=4), ACT.Copy
                                  ).then_inc(px_free, 1)

            def quad(q, last):
                for u in range(9):
                    take(q, u)
                ac.wait_ge(ys_done, q + 2)
                ac.activation(junk, ys, ACT.Square, accum_out=ssq[:, bass.ds(q, 1)]).then_inc(sq_done, 1)
                take(q, 9)
                for k in range(2):
                    ac.wait_ge(px_full, q * 4 + k + 7)
                    dst = act[:, 4 * k:4 * k + 4, TC:TC + T].rearrange("p c (b h) -> p c b h", b=B)
                    ac.activation(dst[:, :, :, bass.ds(q * 4, 4)],
                                  ps[:, k].rearrange("p (c hh b) -> p c b hh", c=4, hh=4), ACT.Copy
                                  ).then_inc(px_free, 1)
                take(q, 10)
                if not last:
                    masked_rows(q + 1)
                take(q, 11)

            ac.wait_ge(dve_k, 2)
            ac.dma_start(k_pad[:, 0:P], zeros).then_inc(k_stored, 16)
            for hh in range(4):
                ac.dma_start(k_pad[:, P:KPAD].rearrange("(q hh) (a b) -> hh a q b", hh=4, b=32)[hh],
                             kt[32 * hh:32 * hh + 32]).then_inc(k_stored, 16)
            masked_rows(0)
            with ac.Fori(0, NQ - 1) as q:
                quad(q, False)
            quad(NQ - 1, True)

            ac.wait_ge(mux[3], 12 * NQ + 1)
            ac.wait_ge(unit_done, 12 * NQ + 6)
            with ac.Fori(0, NCH) as c:
                for m in range(KC):
                    ac.wait_ge(xt_full, c * 8 + m + 9)
                    ac.wait_ge(l0_free, c * 8 + m + 1)
                    ac.activation(xres[m % 2], ps[:, 4 + m % 2, :], ACT.Copy).then_inc(xres_full, 1)
                    if m in (1, 5):
                        for b in range(2):
                            ac.wait_ge(w1_full, c * 4 + m // 2 + b + 3)
                            ac.activation(w1t[:, 4 * b:4 * b + 4, bass.ds(c * 256 + P * (m // 4), P)],
                                          ps[:, 6 + b].rearrange("p (k o) -> p k o", k=4), ACT.Copy
                                          ).then_inc(w1_free, 1)
            ac.wait_ge(aw_full, 1)
            ac.wait_ge(aw_in, 64)
            ac.activation(aw[:, :, R1_:R1_ + E], ps[:, 7, 0:64].rearrange("p (k e) -> p k e", e=E), ACT.Copy
                          ).then_inc(aw_done, 1)
            ac.activation(lim_sb[:, R1_:R1_ + E], ps[0:R1_, 7, 64:72], ACT.Copy).then_inc(aw_done, 1)
            with ac.Fori(0, NCH) as c:
                for b in range(2):
                    ac.wait_ge(bt_full, c * 2 + b + 3)
                    ac.activation(lbt[:, TC * b:TC * b + TC], ps[:, 4 + b, :], ACT.Copy).then_inc(bt_done, 1)
                for m in range(KC):
                    ac.wait_ge(c_full, c * 8 + m + 1)
                    ac.activation(mid[:, m, bass.ds(c * TC, TC)], ps[:, m % 4, :], ACT.Identity,
                                  bias=bias[:, KC + m:KC + m + 1]).then_inc(c_free, 1)
                ac.wait_ge(zh_full, c + 1)
                ac.activation(zh[:, bass.ds(c * TC, TC)], ps[0:R1_ + E, 7, :], ACT.Identity, bias=zbias
                              ).then_inc(zh_done, 1)
            def w2_rows(n):
                for b in range(2):
                    ac.wait_ge(w2_full, 2 * n + b + 1)
                    ac.activation(w1t[:, 4 * b:4 * b + 4, P * n:P * n + P],
                                  ps[:, 4 + 2 * (n % 2) + b].rearrange("p (k o) -> p k o", k=4), ACT.Copy
                                  ).then_inc(w2_free, 1)

            for n in range(6):
                w2_rows(n)
            ac.wait_ge(g_dve, 11)
            ac.activation(gs[2], gs[1], ACT.Exp).then_inc(g_act, 1)
            ac.wait_ge(g_dve, 23)
            ac.activation(gs[4], gs[0], ACT.Sigmoid, scale=2.0).then_inc(g_act, 1)
            for n in range(6, KC):
                w2_rows(n)
            for b in range(2):
                ac.wait_ge(g_full, 4 + b)
                ac.activation(wt[:, TC * b:TC * b + TC], ps[0:E, 2 + b, :], ACT.Copy).then_inc(g_act, 1)
            with ac.Fori(0, NCH) as c:
                for m in range(KC):
                    ac.wait_ge(st_used, c * 8 + m + 3)
                    if m == 0:
                        ac.wait_ge(out_done, c * 64 + 64)
                    ac.activation(rows_out[:, :, m // 4, P * (m % 4):P * (m % 4) + P],
                                  ps[:, 4 + m % 4].rearrange("p (t o) -> p t o", t=4), ACT.Copy).then_inc(row_free, 1)

        @block.tensor
        def _(pe):
            pe.sem_inc(conv_done, 1)
            pe.sem_inc(conv_hi, 1)
            pe.sem_inc(px_full, 4)
            pe.sem_inc(unit_done, 6)
            pe.wait_ge(cst_in, 32)
            pe.wait_ge(act_dup, 4)
            for s in range(4):
                mm = pe.transpose(ps[:, 0, 64 * s:64 * s + 64], dup[:, s].rearrange("p d n -> p (d n)"),
                                  ident[0:H, 0:H])
            mm.then_inc(pe_dup, 1)
            pe.wait_ge(act_id, 1)
            for k in range(KC):
                for o in range(8):
                    pe.wait_ge(act_code, max(o + 1, 8 if k else 0))
                    if k >= 4:
                        pe.wait_ge(code_t_ready, k - 3)
                    mm = pe.transpose(ps[:, 4 + k % 4, :].bitcast(BF16)[:, o * P:o * P + P],
                                      codes[:, o, k * P:k * P + P], identb[:, :])
                mm.then_inc(pe_code, 1)
            pe.wait_ge(p_ready, 1)
            pe.wait_ge(qc_ready, 1)
            for h in range(H):
                r = 32 * (h % 4)
                mm = pe.matmul(ps[r:r + 32, 1, 32 * (h // 4):32 * (h // 4) + 32], tp[2][:, h], tp[4][:, h],
                               start=(h < 4), stop=True, skip_group_check=True)
            mm.then_inc(pe_k, 1)

            def unit(q, u):
                pr, j = u // 3, u % 3
                if j == 0:
                    pe.wait_ge(oh_done, q * 4 + pr + 5)
                    pe.wait_ge(lb_done, q * 4 + pr + 5)
                pe.wait_ge(mux_free, q * 12 + u + 1)
                first, end = SPLITS[j]
                for k in range(first, end):
                    at = A17 * 8 * (k - first)
                    for g in range(2):
                        for part in range(3):
                            mm = pe.matmul(ps[:, 2 + 2 * j + g, at:at + A17 * 8], oh[pr % 2][:, g, k * P:k * P + P],
                                           lb[pr % 2][:, g, part].rearrange("p o a -> p (o a)"), start=(part == 0),
                                           stop=(part == 2), skip_group_check=True)
                mm.then_inc(unit_done, 1)

            def transposes(src, q, batch):
                pe.wait_ge(px_free, q * 4 + batch + 1)
                for c in range(4):
                    k = 4 * (batch % 2) + c
                    mm = pe.transpose(ps[:, batch % 2, c * P:c * P + P], src[:, k * P:k * P + P], ident)
                mm.then_inc(px_full, 1)

            def convolve(bank, j):
                lo = max(512 * bank, P * j)
                for hh in range(4):
                    mm = pe.matmul(ps[32 * hh:32 * hh + 32, bank, lo - 512 * bank:512], ut[:, j, 32 * hh:32 * hh + 32],
                                   toe[:, hh, lo - P * j:512 * bank + 512 - P * j],
                                   start=(j == 0), stop=(j == 4 * bank + 3), skip_group_check=True)
                return mm

            after = {0: ((1, 0),), 1: ((1, 1),), 2: ((1, 2),), 3: ((1, 3),), 4: ((1, 4),), 5: ((1, 5),),
                     6: ((1, 6), (1, 7)), 7: ((0, 0), (0, 1)), 8: ((0, 2), (0, 3))}

            def quad(q, last):
                for u in range(3 * NPAIR):
                    unit(q, u)
                    if u == 0:
                        pe.wait_ge(px_free, q * 4 + 4)
                        pe.wait_ge(toe_hi_in, q * 64 + 64)
                    if u == 1:
                        pe.wait_ge(toe_lo_in, q * 64 + 64)
                    for bank, j in after.get(u, ()):
                        mm = convolve(bank, j)
                    if u == 3:
                        mm.then_inc(conv_hi, 1)
                    if u == 8:
                        mm.then_inc(conv_done, 1)
                    if u == 10:
                        pe.wait_ge(ys_done, q + 2)
                        transposes(ys, q, 2)
                        transposes(ys, q, 3)
                if not last:
                    pe.wait_ge(xm_done, q + 3)
                    transposes(xm, q + 1, 0)
                    transposes(xm, q + 1, 1)

            pe.wait_ge(xm_done, 2)
            transposes(xm, 0, 0)
            pe.wait_ge(dve_k, 2)
            transposes(xm, 0, 1)
            with pe.Fori(0, NQ - 1) as q:
                quad(q, False)
            quad(NQ - 1, True)

            pe.sem_inc(xt_full, 8)
            pe.sem_inc(w1_full, 2)
            pe.wait_ge(mux_free, 12 * NQ + 3)
            pe.wait_ge(px_free, 4 * NQ + 2)
            with pe.Fori(0, NCH) as c:
                for m in range(KC):
                    pe.wait_ge(l0_free, c * 8 + m + 1)
                    for bank, w in ((m % 2, wl), (2 + m % 2, wh)):
                        for k in range(KC):
                            mm = pe.matmul(ps[:, bank, :], w[:, k, P * m:P * m + P],
                                           act[:, k, bass.ds(c * TC + TC, TC)], start=(k == 0), stop=(k == KC - 1))
                    mm.then_inc(l0_full, 1)
                    if m == 0:
                        pe.wait_ge(xr_in, c * 16 + 16)
                    pe.wait_ge(xres_full, c * 8 + m + 1)
                    for t in range(4):
                        mm = pe.transpose(ps[:, 4 + m % 2, P * t:P * t + P], xrow[:, t, P * m:P * m + P], ident)
                    mm.then_inc(xt_full, 1)
                    if m in (1, 5):
                        pe.wait_ge(w1_in, c * 32 + 16 * (m // 4) + 16)
                        for b in range(2):
                            pe.wait_ge(w1_free, c * 4 + m // 2 + b + 1)
                            for k in range(4):
                                mm = pe.transpose(ps[:, 6 + b, P * k:P * k + P],
                                                  w_in[:, P * (4 * b + k):P * (4 * b + k) + P], ident)
                            mm.then_inc(w1_full, 1)
            pe.sem_inc(in_full, 1)
            pe.sem_inc(bt_full, 2)
            pe.wait_ge(aw_in, 64)
            for k in range(KC):
                pe.transpose(ps[:, 7, E * k:E * k + E], u[0:E, P * k:P * k + P], ident[0:E, 0:E])
            pe.transpose(ps[0:R1_, 7, 64:72], lim_sb[0:E, 0:R1_], ident[0:E, 0:E]).then_inc(aw_full, 1)
            pe.wait_ge(w1_free, 4 * NCH + 2)
            pe.wait_ge(l0_free, 8 * NCH + 2)
            pe.wait_ge(aw_done, 2)
            with pe.Fori(0, NCH) as c:
                pe.wait_ge(lbn_in, c * 128 + 128)
                pe.wait_ge(bt_done, c * 2 + 2)
                for m in range(KC):
                    mm = pe.transpose(ps[:, 4 + m // 4, P * (m % 4):P * (m % 4) + P], lbn[:, m], ident)
                    if m % 4 == 3:
                        mm.then_inc(bt_full, 1)
                pe.wait_ge(la_in, c * 128 + 128)
                pe.wait_ge(in_done, c + 1)
                for k in range(KC):
                    mm = pe.matmul(ps[:, 6, :], la[:, k], act[:, k, bass.ds(c * TC, TC)], start=(k == 0),
                                   stop=(k == KC - 1))
                mm.then_inc(in_full, 1)
                for m in range(KC):
                    pe.wait_ge(c_free, c * 8 + m + 1)
                    for k in range(KC):
                        pe.matmul(ps[:, m % 4, :], w1t[:, k, P * m:P * m + P], act[:, k, bass.ds(c * TC, TC)],
                                  start=(k == 0), stop=False)
                    if m == 0:
                        pe.wait_ge(bt_done, c * 2 + 4)
                        pe.wait_ge(in_done, c + 2)
                    pe.matmul(ps[:, m % 4, :], lbt[:, P * m:P * m + P], inter, start=False, stop=True
                              ).then_inc(c_full, 1)
                pe.wait_ge(c_free, c * 8 + 12)
                pe.wait_ge(zh_done, c + 1)
                for k in range(KC):
                    mm = pe.matmul(ps[0:R1_ + E, 7, :], aw[:, k, :], mid[:, k, bass.ds(c * TC, TC)], start=(k == 0),
                                   stop=(k == KC - 1))
                mm.then_inc(zh_full, 1)
            def w2_rows(n):
                pe.wait_ge(w2_in[n % 2], 16 * (n // 2) + 16)
                for b in range(2):
                    if n >= 2:
                        pe.wait_ge(w2_free, 2 * n + b - 3)
                    for k in range(4):
                        mm = pe.transpose(ps[:, 4 + 2 * (n % 2) + b, P * k:P * k + P],
                                          w_in2[n % 2][:, b, P * k:P * k + P], ident)
                    mm.then_inc(w2_full, 1)

            pe.wait_ge(zh_done, NCH + 1)
            anchors = zh.rearrange("r (n two) -> r n two", two=2)[:, :, 1]
            for g in range(8):
                pe.matmul(ps[:, 0, E * g:E * g + E], anchors[0:R1_, P * g:P * g + P], lim_sb[:, R1_:R1_ + E],
                          start=True, stop=True, skip_group_check=True)
            for g in range(8):
                mm = pe.matmul(ps[:, 3, E * g:E * g + E], anchors[R1_:R1_ + E, P * g:P * g + P],
                               cst[R1_:R1_ + E, R1_:R1_ + E], start=True, stop=True, skip_group_check=True)
            mm.then_inc(g_full, 1)
            w2_rows(0)
            w2_rows(1)
            pe.wait_ge(g_dve, 2)
            pe.transpose(ps[0:2, 1, 0:P], g1[0][:, 0:2], ident).then_inc(g_full, 1)
            w2_rows(2)
            w2_rows(3)
            pe.wait_ge(g_dve, 5)
            pe.matmul(ps[:, 2, 0:2], ones[0:2, :], g1[2][0:2, 0:2], start=True, stop=True).then_inc(g_full, 1)
            for n in range(4, KC):
                w2_rows(n)
            pe.wait_ge(g_dve, 28)
            for g in range(8):
                mm = pe.transpose(ps[0:E, 2 + g // 4, P * (g % 4):P * (g % 4) + P], gs[5][:, g], ident)
                if g % 4 == 3:
                    mm.then_inc(g_full, 1)
            pe.wait_ge(g_act, 4)
            for b in range(2):
                mm = pe.matmul(ps[0:R1_, b, :], lim_sb[0:E, 0:R1_], wt[:, TC * b:TC * b + TC], start=True, stop=True)
            mm.then_inc(g_full, 1)
            pe.sem_inc(st_used, 2)
            pe.wait_ge(w2_free, 16)
            pe.wait_ge(bm_in, 16)
            pe.wait_ge(g_dve, 30)
            with pe.Fori(0, NCH) as c:
                def rows(m):
                    pe.wait_ge(f_free, c * 8 + m + 5)
                    pe.wait_ge(row_free, c * 8 + m + 1)
                    for t in range(4):
                        mm = pe.transpose(ps[:, 4 + m % 4, P * t:P * t + P], stage[m % 2][:, P * t:P * t + P], ident)
                    mm.then_inc(st_used, 1)

                for m in range(KC):
                    pe.wait_ge(f_free, c * 8 + m + 1)
                    for k in range(KC):
                        pe.matmul(ps[:, m % 4, :], w1t[:, k, P * m:P * m + P], mid[:, k, bass.ds(c * TC, TC)],
                                  start=(k == 0), stop=False)
                    pe.matmul(ps[:, m % 4, :], bm[:, P * m:P * m + P], zp[:, bass.ds(c * TC, TC)], start=False,
                              stop=True).then_inc(f_full, 1)
                    if m:
                        rows(m - 1)
                rows(KC - 1)

        @block.vector
        def _(ve):
            count = [0]

            def link(ins):
                count[0] += 1
                ins.then_inc(dve, 1)
                ve.wait_ge(dve, count[0])

            ve.sem_inc(oh_done, 4)
            ve.sem_inc(ys_done, 1)
            ve.sem_inc(mux[3], 1)
            ve.wait_ge(act_ex, 2)
            link(ve.scalar_tensor_tensor(sm[:, 3], sm[:, 2], -1.0, sm[:, 1], ALU.mult, ALU.mult))
            ve.sem_inc(dve_ssm, 1)
            link(ve.tensor_tensor(sm[:, 4], ps[:, 0, 64:128], sm[:, 1], ALU.mult))
            link(ve.tensor_scalar(sm[:, 4], sm[:, 4], float(1 / (2 * np.pi)), None, ALU.mult))
            link(ve.tensor_scalar(sm[:, 9], sm[:, 4], MAGIC, MAGIC, ALU.add, ALU.subtract))
            link(ve.tensor_tensor(sm[:, 5], sm[:, 4], sm[:, 9], ALU.subtract))
            ve.sem_inc(dve_ssm, 1)
            def over(row, ramp):
                return sm[:, row].unsqueeze(2).broadcast_to([P, H, 32]), ramp.unsqueeze(1).broadcast_to([P, H, 32])

            ve.wait_ge(cst_in, 32)
            link(ve.tensor_tensor(tp[5], *over(5, cc(C_R32, 32)), ALU.mult))
            ve.sem_inc(dve_ssm, 1)
            link(ve.tensor_tensor(tp[6], *over(5, cc(C_R1, 32)), ALU.mult))
            ve.sem_inc(dve_ssm, 1)
            ve.wait_ge(q_loaded, 128)
            planes = w01[:, 0:2048].bitcast(I32)
            for s, keep in ((4, 0x0F0F0F0F), (2, 0x33333333), (1, 0x55555555)):
                v4 = planes.rearrange("p (x two y) -> p x two y", two=2, y=s * 32)
                lo, hi = v4[:, :, 0], v4[:, :, 1]
                t = q_t.rearrange("p (x y) -> p x y", y=s * 32)
                link(ve.scalar_tensor_tensor(t, lo, s, hi, ALU.logical_shift_right, ALU.bitwise_xor))
                link(ve.tensor_scalar(t, t, keep, None, ALU.bitwise_and))
                link(ve.tensor_tensor(hi, hi, t, ALU.bitwise_xor))
                link(ve.scalar_tensor_tensor(lo, t, s, lo, ALU.logical_shift_left, ALU.bitwise_xor))
            ve.tensor_scalar(q_lo, planes, 0x0F0F0F0F, None, ALU.bitwise_and).then_inc(dve_lo, 1)
            for i in range(3):
                ve.wait_ge(act_shift, i + 1)
                link(ve.tensor_scalar(rnd, tp[2 + i], MAGIC, MAGIC, ALU.add, ALU.subtract))
                link(ve.tensor_tensor(tp[2 + i], tp[2 + i], rnd, ALU.subtract))
                ve.sem_inc(dve_ssm, 1)
            ve.wait_ge(len_in, 80)
            link(ve.tensor_copy(lens[:, 0:1], lens_i))
            ve.tensor_scalar(mask, frow[:, 0], lens[:, 0:1], None, ALU.is_lt).then_inc(dve, 1)
            count[0] += 1
            link(ve.tensor_scalar(mask_rev, frow[:, 1], lens[:, 0:1], None, ALU.is_lt))
            ve.sem_inc(masks_ready, 1)
            ve.wait_ge(act_ex, 5)
            t = lambda n: sm[:, n]
            one_minus, em1 = t(9), t(10)
            link(ve.tensor_scalar(one_minus, t(6), -1.0, 1.0, ALU.mult, ALU.add))
            link(ve.reciprocal(t(11), one_minus))
            link(ve.scalar_tensor_tensor(em1, t(6), 2.0, t(11), ALU.mult, ALU.mult))
            link(ve.scalar_tensor_tensor(t(12), t(7), -2.0, t(7), ALU.mult, ALU.mult))
            link(ve.scalar_tensor_tensor(t(13), t(12), 1.0, em1, ALU.add, ALU.mult))
            link(ve.tensor_tensor(t(13), t(13), t(12), ALU.add))
            link(ve.scalar_tensor_tensor(t(14), em1, 1.0, t(8), ALU.add, ALU.mult))
            cr, ci, ai = ps[:, 0, 128:192], ps[:, 0, 192:256], ps[:, 0, 64:128]
            link(ve.tensor_tensor(t(15), cr, t(13), ALU.mult))
            link(ve.tensor_tensor(t(16), ci, t(14), ALU.mult))
            link(ve.tensor_tensor(t(15), t(15), t(16), ALU.subtract))
            link(ve.tensor_tensor(t(16), cr, t(14), ALU.mult))
            link(ve.tensor_tensor(t(17), ci, t(13), ALU.mult))
            link(ve.tensor_tensor(t(16), t(16), t(17), ALU.add))
            link(ve.tensor_tensor(t(17), t(2), t(2), ALU.mult))
            link(ve.tensor_copy(t(20), ai))
            link(ve.tensor_tensor(t(18), t(20), t(20), ALU.mult))
            link(ve.tensor_tensor(t(17), t(17), t(18), ALU.add))
            link(ve.reciprocal(t(18), t(17)))
            link(ve.tensor_tensor(t(19), t(16), t(20), ALU.mult))
            link(ve.tensor_tensor(t(21), t(15), t(2), ALU.mult))
            link(ve.tensor_tensor(t(19), t(19), t(21), ALU.subtract))
            link(ve.scalar_tensor_tensor(t(22), t(19), 2.0, t(18), ALU.mult, ALU.mult))
            link(ve.tensor_tensor(t(19), t(16), t(2), ALU.mult))
            link(ve.tensor_tensor(t(21), t(15), t(20), ALU.mult))
            link(ve.tensor_tensor(t(19), t(19), t(21), ALU.add))
            link(ve.scalar_tensor_tensor(t(23), t(19), -2.0, t(18), ALU.mult, ALU.mult))
            ve.wait_ge(act_big, 5)
            full = lambda n: sm[:, n].unsqueeze(2).broadcast_to([P, H, 32])
            link(ve.tensor_tensor(tp[2], tp[2], full(22), ALU.mult))
            link(ve.tensor_tensor(tp[3], tp[3], full(23), ALU.mult))
            link(ve.tensor_tensor(tp[2], tp[2], tp[3], ALU.subtract))
            ve.tensor_tensor(tp[2], tp[2], tp[0], ALU.mult).then_inc(p_ready, 1)
            for pr in range(2):
                ve.wait_ge(rep_in[0], 64)
                ve.tensor_scalar(oh[pr], rep[0][:, pr].rearrange("p (g i) -> p g i", g=2), cc(C_LOW), None,
                                 ALU.is_equal).then_inc(oh_done, 1)
            ve.wait_ge(pe_k, 1)
            link(ve.tensor_copy(kt.rearrange("p q b -> p (q b)"), ps[:, 1, :]))
            ve.wait_ge(d_in, 64)
            ve.wait_ge(pool, 3)
            link(ve.tensor_tensor(kt[:, :, 0], kt[:, :, 0], d_col, ALU.add))
            ve.sem_inc(dve_k, 2)
            ve.wait_ge(code_t_ready, 8)

            def quad(q, last):
                ve.wait_ge(mux[3], q * 12 + 1)
                for b in range(4):
                    bit = 0x10101010 << b
                    bit -= (1 << 32) if bit >= 1 << 31 else 0
                    ve.tensor_scalar(bits[:, b].rearrange("p g k o -> p k g o"),
                                     code_t[:, :, bass.ds(q * 16, 16)].rearrange("p k (g o) -> p k g o", g=8), bit, None, ALU.bitwise_and
                                     ).then_inc(bits_done, 1)
                ve.wait_ge(bits_done, q * 4 + 4)
                byte = w2b[:, 6144:6656].bitcast(U8).rearrange("p (b g ko) -> p b g ko", b=4, g=8)

                def level(step, u):
                    pr, j = u // 3, u % 3
                    first, end = SPLITS[j]
                    w = (8, 4, 2, 1)[step]
                    rows = ps[:, 2 + 2 * j:4 + 2 * j, 0:A17 * 8 * (end - first)].rearrange(
                        "p g (ko a) -> p g ko a", a=A17)
                    if step:
                        ve.wait_ge(mux[step - 1], q * 12 + u + 1)
                    else:
                        ve.wait_ge(unit_done, q * 12 + u + 7)
                    ve.sem_inc(held, 1)
                    m = byte[:, 3 - step, 2 * pr:2 * pr + 2, 8 * first:8 * end]
                    ve.copy_predicated(rows[:, :, :, 0:w], m.unsqueeze(3).broadcast_to([P, 2, 8 * (end - first), w]),
                                       rows[:, :, :, w:2 * w]).then_inc(mux[step], 1)

                for u in range(3 * NPAIR):
                    level(0, u)
                    if u:
                        level(2, u - 1)
                    level(1, u)
                    if u:
                        level(3, u - 1)
                    if u % 3 == 2 and (u < 6 or not last):
                        pr = u // 3
                        nxt = (pr + 2) % 4
                        ve.wait_ge(rep_in[nxt // 2], (q + (pr + 2) // 4) * 64 + 64)
                        ve.tensor_scalar(oh[nxt % 2], rep[nxt // 2][:, nxt % 2].rearrange("p (g i) -> p g i", g=2),
                                         cc(C_LOW), None, ALU.is_equal).then_inc(oh_done, 1)
                    if u == 9:
                        ve.wait_ge(conv_done, q + 2)
                        ve.wait_ge(px_free, q * 4 + 4)
                        ve.wait_ge(sq_done, q + 1)
                        ve.tensor_tensor(ys, ps[:, 0:2, :].rearrange("p x l -> p (x l)"), mask, ALU.mult
                                         ).then_inc(ys_done, 1)
                level(2, u)
                level(3, u)

            with ve.Fori(0, NQ - 1) as q:
                quad(q, False)
            quad(NQ - 1, True)

            ve.wait_ge(sq_done, NQ + 1)
            ve.tensor_scalar(high[:, :], ssq[:, :], EST_T * EST_T, None, ALU.is_gt).then_inc(high_done, 1)
            ve.sem_inc(l0_free, 2)
            ve.wait_ge(high_in, 16)
            with ve.Fori(0, NCH) as c:
                ve.wait_ge(l0_free, c * 8 + 2)
                ve.tensor_copy(high_now, high_all[:, bass.ds(c * TC, TC)]).then_inc(l0_pick, 1)
                for m in range(KC):
                    if m == 0:
                        ve.wait_ge(l0_pick, c + 1)
                    ve.wait_ge(l0_full, c * 8 + m + 1)
                    ve.sem_inc(held, 1)
                    ve.copy_predicated(ps[:, m % 2, :], high_now, ps[:, 2 + m % 2, :]).then_inc(l0_sel, 1)
                    ve.wait_ge(l0_sel, c * 8 + m + 1)
                    ve.wait_ge(xres_full, c * 8 + m + 3)
                    ve.scalar_tensor_tensor(act[:, m, bass.ds(c * TC, TC)], ps[:, m % 2, :], bias[:, m:m + 1],
                                            xres[m % 2], ALU.add, ALU.add).then_inc(l0_free, 1)
            ve.sem_inc(in_done, 1)
            ve.wait_ge(lmask_in, 16)
            with ve.Fori(0, NCH) as c:
                ve.wait_ge(in_full, c + 2)
                ve.tensor_tensor(inter, ps[:, 6, :], lmask, ALU.mult).then_inc(in_done, 1)
            def step(ins):
                gate[0] += 1
                ins.then_inc(g_dve, 1)
                ve.wait_ge(g_dve, gate[0])

            gate = [0]
            wide = lambda x: x.unsqueeze(2).broadcast_to([P, 8, E])
            ve.wait_ge(g_full, 1)
            step(ve.tensor_copy(gt.rearrange("p s g e -> p s (g e)"), ps[:, 0:4:3, 0:64]))
            step(ve.tensor_reduce(g1[0][:, 0:2], gt, AX.XY, ALU.max, apply_absolute_value=True))
            ve.wait_ge(g_full, 2)
            step(ve.tensor_reduce(g1[1][0:2, 0:1], ps[0:2, 1, 0:P], AX.X, ALU.max))
            step(ve.tensor_scalar(g1[1][0:2, 1:2], g1[1][0:2, 0:1], 1e-6, None, ALU.max))
            step(ve.tensor_scalar(g1[2][0:2, 0:2], cst[0:2, 0:2], g1[1][0:2, 1:2], None, ALU.mult))
            ve.wait_ge(g_full, 3)
            step(ve.reciprocal(g1[3][:, 0:2], ps[:, 2, 0:2]))
            step(ve.tensor_scalar(g1[3][:, 2:4], g1[3][:, 0:2], 0.5, None, ALU.mult))
            step(ve.tensor_scalar(gs[0], gt[:, 0], g1[3][:, 2:3], None, ALU.mult))
            step(ve.scalar_tensor_tensor(gs[0], gt[:, 1], g1[3][:, 3:4], gs[0], ALU.mult, ALU.add))
            step(ve.tensor_reduce(g1[4], gs[0], AX.X, ALU.max))
            step(ve.tensor_tensor(gs[1], gs[0], wide(g1[4]), ALU.subtract))
            ve.wait_ge(g_act, 1)
            step(ve.tensor_reduce(g1[5], gs[2], AX.X, ALU.add))
            step(ve.reciprocal(g1[6], g1[5]))
            step(ve.tensor_tensor(gs[1], gs[2], wide(g1[6]), ALU.mult))
            for g in range(8):
                step(ve.max(gs[3][:, g], gs[1][:, g]))
            step(ve.tensor_tensor(gs[0], gs[1], wide(gs[3][:, :, 1]), ALU.subtract))
            ve.wait_ge(g_act, 2)
            step(ve.tensor_tensor(gs[2], gs[1], gs[4], ALU.mult))
            step(ve.tensor_reduce(g1[7], gs[2], AX.X, ALU.add))
            step(ve.tensor_scalar(g1[8], g1[7], 1e-9, None, ALU.add))
            step(ve.reciprocal(g1[9], g1[8]))
            step(ve.tensor_tensor(gs[5], gs[2], wide(g1[9]), ALU.mult))
            ve.wait_ge(g_full, 6)
            for b in range(2):
                step(ve.scalar_tensor_tensor(
                    zp[:, 2 * TC * b:2 * TC * b + 2 * TC].rearrange("r (n two) -> r n two", two=2),
                    zh[0:R1_, 2 * TC * b:2 * TC * b + 2 * TC].rearrange("r (n two) -> r n two", two=2), DELTA_SCALE,
                    ps[0:R1_, b, :].unsqueeze(2).broadcast_to([R1_, TC, 2]), ALU.mult, ALU.mult))
            ve.sem_inc(f_free, 4)
            with ve.Fori(0, NCH) as c:
                for m in range(KC):
                    ve.wait_ge(f_full, c * 8 + m + 1)
                    ve.wait_ge(st_used, c * 8 + m + 1)
                    ve.scalar_tensor_tensor(stage[m % 2], ps[:, m % 4, :], bias[:, 2 * KC + m:2 * KC + m + 1],
                                            act[:, m, bass.ds(c * TC, TC)], ALU.add, ALU.add).then_inc(f_free, 1)


_INPUTS = ["x", "itok_B_8_3872", "itok_B_14_62", "L0_cond_log_dt", "L0_cond_C", "L0_cond_log_A_real", "L0_cond_A_imag",
           "L0_cond_D", "L0_ffn_qweight", "L0_ffn_lut4", "L0_ffn_lut8", "L0_ffn_bias", "L1_cond_W", "L1_cond_b",
           "L1_cond_lora_A", "L1_cond_lora_B", "L1_ffn_W", "L1_ffn_b", "L1_ffn_A", "L1_ffn_Bmat", "L1_ffn_LiMEs"]


def kernel(**inputs):
    import concourse.bacc as bacc
    from concourse.bass_utils import run_bass_kernel_spmd

    nc = bacc.Bacc("TRN2", target_bir_lowering=False, num_devices=1)
    arrays = {name: np.ascontiguousarray(inputs[name]) for name in _INPUTS}
    arrays["cst"], arrays["feature_rows"] = shape_constants()
    aps = {name: nc.dram_tensor("in_" + name, x.shape, mybir.dt.from_np(x.dtype), kind="ExternalInput").ap()
           for name, x in arrays.items()}
    out = nc.dram_tensor("out_rows", (B, H, L), F32, kind="ExternalOutput").ap()
    build_kernel(nc, aps, out)
    result = run_bass_kernel_spmd(nc, [{"in_" + name: x for name, x in arrays.items()}], core_ids=[0])
    return result.results[0]["out_rows"]
```

```python
from contextlib import ExitStack

import numpy as np

import concourse.bass as bass
from concourse import mybir

F32 = mybir.dt.float32
BF16 = mybir.dt.bfloat16
F32R = mybir.dt.float32r
I32 = mybir.dt.int32
I16 = mybir.dt.int16
U8 = mybir.dt.uint8
ALU = mybir.AluOpType
ACT = mybir.ActivationFunctionType
AX = mybir.AxisListType

P = 128
B, H, L = 32, 64, 1024
T = B * H
KC = L // P
N = 64
NQ = H // 4
TC = 512
NCH = T // TC
R0, R1_, E = 16, 32, 8
BC = TC // H
EST_T = 64.0
LORA_SCALE = 2.0
DELTA_SCALE = 0.5
TWO_PI = 6.283185
MAGIC = 12582912.0
KPAD = P + L
A17 = 17
LW = 3 * A17 + 1
SPLITS = ((0, 3), (3, 6), (6, 8))
NPAIR = 4

C_ID, C_LORA, C_R32, C_R1, C_PHI, C_NPHI, C_LOW, C_OWN, C_PHI4, C_NPHI4, C_END = (
    0, 128, 640, 672, 704, 705, 706, 707, 715, 716, 717)


def shape_constants():
    p = np.arange(P)
    c = np.zeros((P, C_END), np.float32)
    c[:, C_ID:C_ID + P] = np.eye(P)
    c[:, C_LORA:C_LORA + TC] = LORA_SCALE * (p[:, None] // R0 == np.arange(TC)[None] // H)
    c[:, C_R32:C_R32 + 32] = 32 * np.arange(32)
    c[:, C_R1:C_R1 + 32] = np.arange(32)
    c[:, C_PHI] = 0.25 * (p >= N)
    c[:, C_NPHI] = -0.25 * (p >= N)
    c[:, C_LOW] = p % 16
    c[:, C_OWN:C_OWN + 8] = p[:, None] // 16 == np.arange(8)[None]
    c[:, C_PHI4] = c[:, C_PHI] + 0.25
    c[:, C_NPHI4] = c[:, C_NPHI] + 0.25
    feature = np.arange(L, dtype=np.float32)
    return c, np.stack([feature, feature.reshape(KC, P)[:, ::-1].reshape(L)])


def build_kernel(nc, a, out):
    k_pad = nc.dram_tensor("k_pad", (H, KPAD), F32).ap()
    code_lo = nc.dram_tensor("code_lo", (L, L), U8).ap()
    lut_parts = nc.dram_tensor("lut_parts", (L, 16 * LW), BF16).ap()
    x1_store = nc.dram_tensor("x1_store", (NCH, P, KC, TC), F32).ap()
    high_rows = nc.dram_tensor("high_rows", (T,), U8).ap()

    ctx = ExitStack()
    with ctx:
        ctx.enter_context(nc.allow_non_contiguous_dma(reason="biases and the skip weights: a few KB, once"))

        def sb(name, shape, dt):
            return ctx.enter_context(nc.sbuf_tensor(name, shape, dt))

        def sem(name):
            return ctx.enter_context(nc.semaphore(name))

        act = sb("act", [P, KC, TC + T], F32)
        ruv = sb("ruv", [P, 7 * L], F32)
        r3, u, v = ruv[:, 0:4 * L], ruv[:, 4 * L:6 * L], ruv[:, 6 * L:7 * L]
        cst = sb("cst", [P, C_END - 512], F32)
        identb = sb("identb", [P, P], BF16)
        bias = sb("bias", [P, 3 * KC + 1], F32)
        ids = sb("ids", [1, B], I32)
        ssq = sb("ssq", [P, NQ], F32)
        high = sb("high", [P, NQ], U8)
        aw = sb("aw", [P, KC, R1_ + E], F32)
        small = sb("small", [P, 136], F32)
        lim_sb = sb("lim_sb", [R1_, R1_ + E], F32)
        with ExitStack() as layer0:
            w01 = layer0.enter_context(nc.sbuf_tensor("w01", [P, 2 * KC * L], F32))
            w2 = layer0.enter_context(nc.sbuf_tensor("w2", [P, KC * L], F32))
        hi_lo = sb("hi_lo", [P, 2 * KC * L], F32R)
        w_low = sb("w_low", [P, KC * L], F32R)
        ps = ctx.enter_context(nc.psum_tensor("ps", [P, 8, 512], F32))

        ident = cst[:, C_ID:C_ID + P]

        def cc(at, n=1):
            at = at if at < C_LORA else at - 512
            return cst[:, at:at + n]

        wl = w01[:, 0:KC * L].rearrange("p (k o) -> p k o", k=KC)
        wh = w01[:, KC * L:2 * KC * L].rearrange("p (k o) -> p k o", k=KC)

        w2b = w2[:, :]
        ut = w2b[:, 0:1024].rearrange("p (c t) -> p c t", c=KC)
        xq = w2b[:, 1024:2048]
        xm = w2b[:, 2048:3072]
        ys = w2b[:, 3072:4096]
        code_t = w2b[:, 4096:6144].bitcast(I32).rearrange("p (k o) -> p k o", k=KC)
        bits = w2b[:, 6144:6656].bitcast(I32).rearrange(
            "p (b g k o) -> p b g k o", b=4, g=8, k=KC)
        mask = w2b[:, 6656:7168].bitcast(BF16)
        mask_rev = w2b[:, 7168:7680].bitcast(BF16)
        lp = w2b[:, 7680:7680 + 8 * LW // 2].bitcast(BF16).rearrange("p (g w) -> p g w", w=LW)
        lb = [u[:, 512 * i:512 * i + 408].bitcast(BF16).rearrange("p (g s o a) -> p g s o a", g=2, s=3, o=8)
              for i in range(2)]
        junk = u[:, 1024:1536].bitcast(BF16)
        toe = r3[:, :].rearrange("p (h c) -> p h c", h=4)
        oh = [act[:, 2 * i:2 * i + 2, 0:TC].bitcast(BF16) for i in range(2)]
        rep = [act[:, 4 + 2 * i:6 + 2 * i, 0:TC].bitcast(U8) for i in range(2)]

        q_in = w01[:, 0:2048].bitcast(I32).rearrange("p (o b w) -> p o b w", o=8, b=8)
        q_t = w01[:, 2048:3072].bitcast(I32)
        q_lo = w01[:, 3072:5120].bitcast(I32)
        codes = w01[:, 5120:9216].bitcast(BF16).rearrange("p (o i) -> p o i", o=8)
        codes_lo = w01[:, 9216:11264].bitcast(U8).rearrange("p (o i) -> p o i", o=8)
        lut_in = w01[:, 11264:13312].rearrange("p (o a b) -> p o a b", o=8, a=16)
        lut4_in = w01[:, 13312:13440].rearrange("p (o b) -> p o b", o=8)
        parts = r3[:, 0:4 * 16 * LW].bitcast(BF16).rearrange("p (o b w) -> p o b w", o=8, b=16)
        rnd, *tp = [act[:, k, TC:TC + 2048].rearrange("p (h m) -> p h m", h=H) for k in range(8)]
        sm = w01[:, 13440:13440 + 24 * 64].rearrange("p (s h) -> p s h", h=64)
        c_in = w01[0:H, 14976:15104].rearrange("p (n two) -> p two n", two=2)
        dup = w01[0:H, 15104:15616].rearrange("p (s d n) -> p s d n", s=4, d=2)
        kt = w01[:, 15616:16128].rearrange("p (q b) -> p q b", q=NQ)
        d_col = w01[:, 16128:16144]
        zeros = w01[0:H, 16144:16272]
        lens = small[:, 0:2]
        lens_i = small[:, 2:3].bitcast(I32)
        frow = w2b[:, 0:2048].rearrange("p (two l) -> p two l", two=2)

        xrow = r3[:, :].rearrange("p (t l) -> p t l", t=4)
        xres = [u[:, TC * i:TC * i + TC] for i in range(2)]
        w_in = u[:, 1024:2048]
        high_all = v[:, 0:T // 4].bitcast(U8)
        high_now = v[:, T // 4:T // 4 + TC // 4].bitcast(U8)
        w1t = w2[:, :].rearrange("p (k o) -> p k o", k=KC)
        mid = act[:, :, 0:T]
        w_hi = hi_lo[:, 0:KC * L].rearrange("p (k o) -> p k o", k=KC)
        w_lo = w_low[:, :].rearrange("p (k o) -> p k o", k=KC)
        x_hi = hi_lo[:, KC * L:KC * L + KC * TC].rearrange("p (k t) -> p k t", k=KC)
        x_lo = hi_lo[:, KC * L + KC * TC:2 * KC * L].rearrange("p (k t) -> p k t", k=KC)
        la = u[:, 1024:2048].rearrange("p (k r) -> p k r", k=KC)
        lbn = r3[:, 0:1024].rearrange("p (m r) -> p m r", m=KC)
        lbt = r3[:, 1024:2048]
        inter = r3[:, 2048:2560]
        lmask = r3[:, 2560:3072]
        zh = ruv[0:R1_ + E, 3072:3072 + T]
        zbias = small[0:R1_ + E, 3:4]
        ones = small[:, 8:136]
        lim = lim_sb[:, :]
        tail = act[:, :, T:T + TC]
        gt = tail[:, 0, 0:128].rearrange("p (s g e) -> p s g e", s=2, g=8)
        gs = [tail[:, 0, 128 + 64 * i:192 + 64 * i].rearrange("p (g e) -> p g e", g=8) for i in range(6)]
        g1 = [tail[:, 1, 8 * i:8 * i + 8] for i in range(12)]
        w_in2 = [tail[:, 2:4, :], tail[:, 4:6, :], tail[:, 6:8, :], v.rearrange("p (b l) -> p b l", b=2),
                 u[:, 1024:2048].rearrange("p (b l) -> p b l", b=2)]
        zp = r3[0:R1_, 0:T]
        bm = r3[0:R1_, T:T + L]
        wt = u[0:E, L:2 * L]
        stage = [v[:, TC * i:TC * i + TC] for i in range(2)]
        rows_out = tail.rearrange("p (t two) l -> p t two l", two=2)

        cst_in = sem("cst_in"); ssm_in = sem("ssm_in"); q_loaded = sem("q_loaded"); lut_loaded = sem("lut_loaded")
        len_in = sem("len_in"); d_in = sem("d_in"); bias_in = sem("bias_in")
        held = sem("held")
        dve = sem("dve"); pool = sem("pool")
        act_id = sem("act_id"); act_dup = sem("act_dup"); act_ex = sem("act_ex"); act_big = sem("act_big")
        act_code = sem("act_code"); pool_pow = sem("pool_pow"); pool_parts = sem("pool_parts")
        act_shift = sem("act_shift")
        act_lo = sem("act_lo"); code_t_ready = sem("code_t_ready")
        dve_lo = sem("dve_lo"); dve_ssm = sem("dve_ssm"); dve_k = sem("dve_k")
        pe_dup = sem("pe_dup"); pe_code = sem("pe_code"); pe_k = sem("pe_k")
        masks_ready = sem("masks_ready"); p_ready = sem("p_ready"); qc_ready = sem("qc_ready")
        k_stored = sem("k_stored"); lo_stored = sem("lo_stored"); parts_stored = sem("parts_stored")
        xq_in = sem("xq_in"); toe_hi_in = sem("toe_hi_in"); toe_lo_in = sem("toe_lo_in")
        conv_hi = sem("conv_hi"); rep_in = [sem("rep_in0"), sem("rep_in1")]; lp_in = sem("lp_in")
        xm_done = sem("xm_done"); lb_done = sem("lb_done"); oh_done = sem("oh_done")
        px_full = sem("px_full"); px_free = sem("px_free"); conv_done = sem("conv_done"); ys_done = sem("ys_done")
        sq_done = sem("sq_done"); unit_done = sem("unit_done");
        mux = [sem("mux%d" % n) for n in range(4)]; mux_free = sem("mux_free"); bits_done = sem("bits_done")

        high_done = sem("high_done"); high_out = sem("high_out"); high_in = sem("high_in"); xr_in = sem("xr_in")
        l0_full = sem("l0_full"); l0_free = sem("l0_free"); l0_sel = sem("l0_sel"); l0_pick = sem("l0_pick")
        xt_full = sem("xt_full")
        xres_full = sem("xres_full"); w1_in = sem("w1_in"); w1_full = sem("w1_full"); w1_free = sem("w1_free")
        x1_out = sem("x1_out"); x1_in = [sem("x1_in%d" % k) for k in range(KC)]; x_used = sem("x_used")
        w_split = sem("w_split")
        split_hi = sem("split_hi"); split_lo = sem("split_lo"); w_rounded = sem("w_rounded")
        ids_in = sem("ids_in"); aw_in = sem("aw_in"); lmask_in = sem("lmask_in"); la_in = sem("la_in")
        lbn_in = sem("lbn_in")
        aw_full = sem("aw_full"); aw_done = sem("aw_done"); bt_full = sem("bt_full"); bt_done = sem("bt_done")
        in_full = sem("in_full"); in_done = sem("in_done"); c_full = sem("c_full"); c_free = sem("c_free")
        zh_full = sem("zh_full"); zh_done = sem("zh_done")
        g_full = sem("g_full"); g_dve = sem("g_dve"); g_act = sem("g_act")
        w2_in = [sem("w2_in%d" % n) for n in range(5)]
        w2_full = sem("w2_full"); w2_free = sem("w2_free"); bm_in = sem("bm_in")
        f_full = sem("f_full"); f_free = sem("f_free"); st_used = sem("st_used"); row_free = sem("row_free")
        out_done = sem("out_done")

        block = ctx.enter_context(nc.Block())

        @block.sync
        def _(sp):
            sp.dma_start(cst[:, 0:P], a["cst"][:, 0:P]).then_inc(cst_in, 16)
            sp.dma_start(cst[:, P:C_END - 512], a["cst"][:, 640:C_END]).then_inc(cst_in, 16)
            for b in range(8):
                sp.dma_start(q_in[:, :, b, :], a["L0_ffn_qweight"][b].rearrange("(o p) w -> p o w", p=P)
                             ).then_inc(q_loaded, 16)
            sp.dma_start(ids[:, :], a["itok_B_14_62"].rearrange("(one b) -> one b", one=1)).then_inc(ids_in, 16)
            sp.dma_start(frow, a["feature_rows"].partition_broadcast(P)).then_inc(len_in, 16)
            for hh in range(4):
                sp.dma_start(lens_i[32 * hh:32 * hh + 32, :],
                             a["itok_B_8_3872"].rearrange("(b one) -> b one", one=1)).then_inc(len_in, 16)
            sp.dma_start(lut_in, a["L0_ffn_lut8"].rearrange("(o p) (a b) -> p o a b", p=P, a=16)).then_inc(lut_loaded, 16)
            sp.dma_start(lut4_in, a["L0_ffn_lut4"].rearrange("(o p) b -> p o b", p=P)).then_inc(lut_loaded, 16)
            sp.dma_start(u[0:E, 0:L], a["L1_ffn_W"][0:E, :]).then_inc(aw_in, 16)
            sp.dma_start(aw[:, :, 0:R1_], a["L1_ffn_A"].rearrange("(k p) r -> p k r", p=P)).then_inc(aw_in, 16)
            sp.dma_start(lim_sb[0:E, 0:R1_], a["L1_ffn_LiMEs"]).then_inc(aw_in, 16)
            sp.dma_start(small[R1_:R1_ + E, 3:4], a["L1_ffn_b"][0:E].rearrange("(e one) -> e one", one=1)
                         ).then_inc(aw_in, 16)
            sp.wait_ge(pool_parts, 1)
            sp.dma_start(lut_parts.rearrange("(o p) w -> p o w", p=P), parts.rearrange("p o b w -> p o (b w)")
                         ).then_inc(parts_stored, 16)
            sp.wait_ge(act_lo, 8)
            sp.dma_start(code_lo.rearrange("(o p) i -> p o i", p=P), codes_lo).then_inc(lo_stored, 16)
            sp.wait_ge(masks_ready, 1)
            x_h = a["x"].rearrange("b h l -> h b l")
            lo_rep = bass.AP(code_lo.tensor, 0, [[64 * L, NQ], [8 * L, 8], [L, 8], [0, 16], [1, L]])
            lp_src = lut_parts.rearrange("(q g o) (b w) -> q (o b) g w", q=NQ, g=8, w=LW)
            toe_src = bass.AP(k_pad.tensor, 1, [[4 * KPAD, NQ], [1, P], [KPAD, 4], [1, L]])
            with sp.Fori(0, NQ) as q:
                sp.wait_ge(xm_done, q + 1)
                for hh in range(4):
                    sp.dma_start(xq[32 * hh:32 * hh + 32], x_h[bass.ds(q * 4 + hh, 1)].rearrange("h b l -> (h b) l")
                                 ).then_inc(xq_in, 16)
                sp.wait_ge(lo_stored, 16)
                for half in range(2):
                    sp.wait_ge(oh_done, q * 4 + 2 * half + 2)
                    sp.sem_inc(held, 1)
                    for g in range(4):
                        sp.dma_start(rep[half][:, g // 2, (g % 2) * L:(g % 2 + 1) * L],
                                     lo_rep[bass.ds(q, 1), 4 * half + g]
                                     ).then_inc(rep_in[half], 16)
                sp.wait_ge(parts_stored, 16)
                sp.wait_ge(lb_done, q * 4 + 4)
                sp.sem_inc(held, 1)
                sp.dma_start(lp, lp_src[bass.ds(q, 1)]).then_inc(lp_in, 16)
                sp.wait_ge(k_stored, 80)
                for part, sem_in, used in ((1, toe_hi_in, conv_hi), (0, toe_lo_in, conv_done)):
                    sp.wait_ge(used, q + 1)
                    for hh in range(4):
                        sp.dma_start(toe[:, hh, 512 * part:512 * part + 512],
                                     toe_src[bass.ds(q, 1), :, hh, 512 * part:512 * part + 512]).then_inc(sem_in, 16)

            sp.wait_ge(high_done, 1)
            for hh in range(4):
                sp.dma_start(high_rows.rearrange("(b q hh) -> hh b q", q=NQ, hh=4)[hh], high[32 * hh:32 * hh + 32, :]
                             ).then_inc(high_out, 16)
            sp.wait_ge(high_out, 64)
            sp.dma_start(high_all, high_rows.partition_broadcast(P)).then_inc(high_in, 16)
            sp.wait_ge(sq_done, NQ + 1)
            sp.wait_ge(unit_done, 12 * NQ + 6)
            x_rows = a["x"].rearrange("b h l -> (b h) l").rearrange("(c t p) l -> c p t l", c=NCH, p=P)
            with sp.Fori(0, NCH) as c:
                sp.wait_ge(xt_full, c * 8 + 8)
                sp.dma_start(xrow, x_rows[bass.ds(c, 1)]).then_inc(xr_in, 16)
                for s in range(2):
                    sp.wait_ge(w1_full, c * 4 + 2 * s + 2)
                    sp.dma_start(w_in, a["L1_cond_W"].rearrange("(n p) i -> n p i", p=P)[bass.ds(c * 2 + s, 1)]
                                 ).then_inc(w1_in, 16)
            sp.wait_ge(w1_full, 4 * NCH + 2)
            sp.wait_ge(ids_in, 16)
            lora_a = a["L1_cond_lora_A"].rearrange("n (k p) r -> n p k r", p=P)
            lora_b = a["L1_cond_lora_B"].rearrange("n (k p) r -> n p k r", p=P)
            with sp.Fori(0, NCH) as c:
                sp.wait_ge(l0_free, c * 8 + 10)
                sp.dma_start(x1_store[bass.ds(c, 1)].rearrange("c p k t -> (c p) k t"),
                             act[:, :, bass.ds(c * TC, TC)]).then_inc(x1_out, 16)
                sp.wait_ge(in_full, c + 1)
                who = []
                for n in range(BC):
                    who.append(sp.value_load(ids[0:1, bass.ds(c * BC + n, 1)], min_val=0, max_val=63))
                    sp.dma_start(la[:, :, R0 * n:R0 * n + R0], lora_a[bass.ds(who[n], 1)]).then_inc(la_in, 16)
                sp.wait_ge(xt_full, 8 * NCH + 8)
                sp.wait_ge(in_done, c + 1)
                sp.sem_inc(held, 1)
                sp.dma_start(lmask, a["cst"][:, C_LORA:C_LORA + TC]).then_inc(lmask_in, 16)
                sp.wait_ge(bt_full, c * 2 + 2)
                for n in range(BC):
                    sp.dma_start(lbn[:, :, R0 * n:R0 * n + R0], lora_b[bass.ds(who[n], 1)]).then_inc(lbn_in, 16)
            for n in range(KC):
                if n == 0:
                    sp.wait_ge(l0_free, 8 * NCH + 2)
                if n == 4:
                    sp.wait_ge(in_full, NCH + 1)
                if n >= 5:
                    sp.wait_ge(w2_full, 2 * n - 8)
                sp.dma_start(w_in2[n % 5], a["L1_ffn_W"][P * n:P * n + P, :].rearrange("p (b l) -> p b l", b=2)
                             ).then_inc(w2_in[n % 5], 16)
                if n == 4:
                    sp.wait_ge(c_full, 8 * NCH)
                    sp.wait_ge(zh_full, NCH)
                    sp.dma_start(bm, a["L1_ffn_Bmat"]).then_inc(bm_in, 16)
            o_rows = out.rearrange("b h l -> (b h) l").rearrange("(c t p) (two l) -> c p t two l", c=NCH, p=P, two=2)

            def residual(c, first):
                for k in range(KC):
                    sp.wait_ge(split_lo, c * 8 + 8 * NCH + k + 1)
                    sp.sem_inc(held, 1)
                    if not first:
                        sp.wait_ge(f_free, c * 8 + k - 3)
                        sp.sem_inc(held, 1)
                    sp.dma_start(mid[:, k, bass.ds(c * TC, TC)],
                                 x1_store[bass.ds(c, 1), :, k].rearrange("c p t -> (c p) t")).then_inc(x1_in[k], 16)

            def results(c):
                sp.wait_ge(row_free, c * 8 + 12)
                for t in range(4):
                    sp.dma_start(o_rows[bass.ds(c, 1), :, t], rows_out[:, t]).then_inc(out_done, 16)

            sp.wait_ge(x1_out, 16 * NCH)
            residual(0, True)
            with sp.Fori(0, NCH - 1) as c:
                residual(c + 1, False)
                results(c)
            results(NCH - 1)
            sp.wait_ge(out_done, 64 * NCH + 64)

        @block.gpsimd
        def _(pl):
            pl.sem_inc(xm_done, 1)
            pl.sem_inc(lb_done, 4)
            pl.memset(zeros, 0.0).then_inc(pool, 1)
            pl.memset(d_col, 0.0).then_inc(pool, 1)
            pl.memset(small[:, 8:136], 1.0).then_inc(pool, 1)
            pl.memset(small[0:R1_, 3:4], 0.0).then_inc(pool, 1)
            pl.wait_ge(pool, 4)
            for hh in range(4):
                pl.dma_start(d_col[32 * hh:32 * hh + 1, :],
                             a["L0_cond_D"].rearrange("(q hh) -> hh q", hh=4)[hh:hh + 1, :]).then_inc(d_in, 16)
            def over(row, ramp):
                return sm[:, row].unsqueeze(2).broadcast_to([P, H, 32]), ramp.unsqueeze(1).broadcast_to([P, H, 32])

            pl.wait_ge(cst_in, 32)
            pl.wait_ge(dve_ssm, 1)
            pl.tensor_tensor(tp[0], *over(3, cc(C_R32, 32)), ALU.mult).then_inc(pool_pow, 1)
            pl.tensor_tensor(tp[1], *over(3, cc(C_R1, 32)), ALU.mult).then_inc(pool_pow, 1)
            pl.wait_ge(lut_loaded, 32)
            lut_t = lut_in.rearrange("p o a b -> p o b a")
            count = [4]

            def link(*instructions):
                for ins in instructions:
                    ins.then_inc(pool, 1)
                count[0] += len(instructions)
                pl.wait_ge(pool, count[0])

            link(pl.memset(parts[:, :, :, 3 * A17:LW], 0.0))
            for part in range(3):
                high_part, low_part = (parts[:, :, :, A17 * part:A17 * part + 16],
                                       parts[:, :, :, A17 * part + 16:A17 * part + 17])
                link(pl.tensor_copy(high_part, lut_t), pl.tensor_copy(low_part, lut4_in.unsqueeze(3)))
                if part < 2:
                    link(pl.tensor_tensor(lut_t, lut_t, high_part, ALU.subtract),
                         pl.tensor_tensor(lut4_in.unsqueeze(3), lut4_in.unsqueeze(3), low_part, ALU.subtract))
            pl.sem_inc(pool_parts, 1)
            pl.wait_ge(act_big, 5)
            pl.tensor_tensor(tp[4], tp[4], tp[1], ALU.mult).then_inc(qc_ready, 1)
            pl.wait_ge(masks_ready, 1)
            pl.wait_ge(aw_full, 1)
            with pl.Fori(0, NQ) as q:
                pl.wait_ge(xq_in, q * 64 + 64)
                pl.wait_ge(px_full, q * 4 + 2)
                pl.tensor_tensor(xm.rearrange("p (c l) -> p c l", c=KC),
                                 xq.rearrange("p (c l) -> p c l", c=KC)[:, :, ::-1],
                                 mask_rev.rearrange("p (c l) -> p c l", c=KC), ALU.mult).then_inc(xm_done, 1)
                pl.wait_ge(lp_in, q * 16 + 16)
                for pr in range(NPAIR):
                    pl.wait_ge(unit_done, q * 12 + 3 * pr + 3)
                    for g in range(2):
                        ins = pl.tensor_tensor(
                            lb[pr % 2][:, g],
                            lp[:, 2 * pr + g, 0:3 * A17].rearrange("p (s a) -> p s a", s=3).unsqueeze(2)
                            .broadcast_to([P, 3, 8, A17]),
                            cc(C_OWN, 8).unsqueeze(1).unsqueeze(3).broadcast_to([P, 3, 8, A17]), ALU.mult)
                    ins.then_inc(lb_done, 1)

        @block.scalar
        def _(ac):
            ac.sem_inc(px_free, 2)
            ac.sem_inc(mux_free, 3)
            ac.sem_inc(sq_done, 1)
            ac.sem_inc(w1_free, 2)
            ac.sem_inc(xres_full, 2)
            ac.sem_inc(bt_done, 2)
            ac.sem_inc(c_free, 4)
            ac.sem_inc(zh_done, 1)
            ac.sem_inc(row_free, 4)
            ac.sem_inc(out_done, 64)
            ac.dma_start(c_in.rearrange("p two n -> p n two"), a["L0_cond_C"]).then_inc(ssm_in, 16)
            for s, name in ((0, "L0_cond_log_A_real"), (1, "L0_cond_A_imag")):
                for d in range(2):
                    ac.dma_start(dup[:, s, d], a[name]).then_inc(ssm_in, 16)
            ac.dma_start(sm[:, 0], a["L0_cond_log_dt"].partition_broadcast(P)).then_inc(ssm_in, 16)
            for n, name in enumerate(("L0_ffn_bias", "L1_cond_b", "L1_ffn_b")):
                ac.dma_start(bias[:, KC * n:KC * n + KC], a[name].rearrange("(m p) -> p m", p=P)).then_inc(bias_in, 16)
            ac.wait_ge(cst_in, 32)
            ac.activation(identb[:, :], ident, ACT.Copy).then_inc(act_id, 1)
            ac.wait_ge(ssm_in, 96)
            for s in range(2):
                for d in range(2):
                    ac.activation(dup[:, 2 + s, d], c_in[:, s], ACT.Copy).then_inc(act_dup, 1)
            ac.activation(sm[:, 1], sm[:, 0], ACT.Exp).then_inc(act_ex, 1)
            ac.wait_ge(pe_dup, 1)
            ac.activation(sm[:, 2], ps[:, 0, 0:64], ACT.Exp).then_inc(act_ex, 1)
            ac.wait_ge(dve_ssm, 1)
            ac.activation(sm[:, 6], sm[:, 3], ACT.Tanh, scale=0.5).then_inc(act_ex, 1)
            ac.wait_ge(dve_ssm, 2)
            ac.activation(sm[:, 7], sm[:, 5], ACT.Sin, scale=TWO_PI / 2).then_inc(act_ex, 1)
            ac.activation(sm[:, 8], sm[:, 5], ACT.Sin, scale=TWO_PI).then_inc(act_ex, 1)
            ac.wait_ge(aw_full, 1)
            ac.wait_ge(aw_in, 64)
            ac.activation(aw[:, :, R1_:R1_ + E], ps[:, 3, 0:64].rearrange("p (k e) -> p k e", e=E), ACT.Copy
                          ).then_inc(aw_done, 1)
            ac.activation(lim_sb[:, R1_:R1_ + E], ps[0:R1_, 3, 64:72], ACT.Copy).then_inc(aw_done, 1)
            for i, (base, shift) in enumerate(((5, C_PHI4), (5, C_PHI), (6, C_NPHI4))):
                ac.wait_ge(dve_ssm, base - 2)
                ac.activation(tp[2 + i], tp[base], ACT.Identity, bias=cc(shift)).then_inc(act_shift, 1)
            for i in range(2):
                ac.wait_ge(pool_pow, i + 1)
                ac.activation(tp[i], tp[i], ACT.Exp).then_inc(act_big, 1)
            ac.wait_ge(dve_lo, 1)
            src = q_lo.bitcast(U8).rearrange("p (o j w k) -> p o w k j", o=8, j=8, w=32)
            for o in range(8):
                ac.activation(codes_lo[:, o].rearrange("p (w k j) -> p w k j", w=32, k=4), src[:, o], ACT.Copy
                              ).then_inc(act_lo, 1)
            for i in range(3):
                ac.wait_ge(dve_ssm, 5 + i)
                ac.activation(tp[2 + i], tp[2 + i], ACT.Sin, scale=TWO_PI).then_inc(act_big, 1)
            src = w01[:, 0:2048].bitcast(U8).rearrange("p (o j w k) -> p o w k j", o=8, j=8, w=32)
            for o in range(8):
                ac.activation(codes[:, o].rearrange("p (w k j) -> p w k j", w=32, k=4), src[:, o], ACT.Copy
                              ).then_inc(act_code, 1)
            for k in range(KC):
                ac.wait_ge(pe_code, k + 1)
                ac.activation(code_t[:, k].bitcast(U8), ps[:, 4 + k % 4, :].bitcast(BF16), ACT.Copy
                              ).then_inc(code_t_ready, 1)
            ac.wait_ge(bias_in, 48)
            def take(q, u):
                pr, j = u // 3, u % 3
                ac.wait_ge(mux[3], q * 12 + u + 2)
                first, end = SPLITS[j]
                src = ps[:, 2 + 2 * j:4 + 2 * j, 0:A17 * 8 * (end - first)].rearrange(
                    "p g (k o a) -> p g k o a", a=A17, o=8)
                for w, row in ((wh, 0), (wl, 16)):
                    ins = ac.activation(
                        w[:, first:end, bass.ds(q * 64 + 16 * pr, 16)].rearrange("p k (g o) -> p g k o", g=2),
                        src[:, :, :, :, row], ACT.Copy)
                ins.then_inc(mux_free, 1)

            def masked_rows(q):
                for k in range(2):
                    ac.wait_ge(px_full, q * 4 + k + 5)
                    ac.activation(ut[:, 4 * k:4 * k + 4], ps[:, k].rearrange("p (c t) -> p c t", c=4), ACT.Copy
                                  ).then_inc(px_free, 1)

            def quad(q, last):
                for u in range(9):
                    take(q, u)
                for k in range(2):
                    ac.wait_ge(px_full, q * 4 + k + 7)
                    dst = act[:, 4 * k:4 * k + 4, TC:TC + T].rearrange("p c (b h) -> p c b h", b=B)
                    ac.activation(dst[:, :, :, bass.ds(q * 4, 4)],
                                  ps[:, k].rearrange("p (c hh b) -> p c b hh", c=4, hh=4), ACT.Copy
                                  ).then_inc(px_free, 1)
                take(q, 9)
                if not last:
                    masked_rows(q + 1)
                ac.wait_ge(ys_done, q + 2)
                ac.activation(junk, ys, ACT.Square, accum_out=ssq[:, bass.ds(q, 1)]).then_inc(sq_done, 1)
                take(q, 10)
                take(q, 11)

            ac.wait_ge(dve_k, 2)
            ac.dma_start(k_pad[:, 0:P], zeros).then_inc(k_stored, 16)
            for hh in range(4):
                ac.dma_start(k_pad[:, P:KPAD].rearrange("(q hh) (a b) -> hh a q b", hh=4, b=32)[hh],
                             kt[32 * hh:32 * hh + 32]).then_inc(k_stored, 16)
            masked_rows(0)
            with ac.Fori(0, NQ - 1) as q:
                quad(q, False)
            quad(NQ - 1, True)

            ac.wait_ge(mux[3], 12 * NQ + 1)
            ac.wait_ge(unit_done, 12 * NQ + 6)
            with ac.Fori(0, NCH) as c:
                for m in range(KC):
                    ac.wait_ge(xt_full, c * 8 + m + 9)
                    ac.wait_ge(l0_free, c * 8 + m + 1)
                    ac.activation(xres[m % 2], ps[:, 4 + m % 2, :], ACT.Copy).then_inc(xres_full, 1)
                    if m in (1, 5):
                        for b in range(2):
                            ac.wait_ge(w1_full, c * 4 + m // 2 + b + 3)
                            ac.activation(w1t[:, 4 * b:4 * b + 4, bass.ds(c * 256 + P * (m // 4), P)],
                                          ps[:, 6 + b].rearrange("p (k o) -> p k o", k=4), ACT.Copy
                                          ).then_inc(w1_free, 1)
            def split(chunk, seq):
                for k in range(KC):
                    ac.wait_ge(x_used, seq * 8 + k + 1)
                    ac.activation(x_hi[:, k], act[:, k, bass.ds(chunk * TC, TC)], ACT.Copy).then_inc(split_hi, 1)

            ac.wait_ge(l0_free, 8 * NCH + 2)
            split(0, 0)
            for m in range(KC):
                ac.activation(w_hi[:, :, P * m:P * m + P], w1t[:, :, P * m:P * m + P], ACT.Copy).then_inc(w_rounded, 1)

            def cond(c, last):
                for b in range(2):
                    ac.wait_ge(bt_full, c * 2 + b + 3)
                    ac.activation(lbt[:, TC * b:TC * b + TC], ps[:, 4 + b, :], ACT.Copy).then_inc(bt_done, 1)
                ac.wait_ge(x1_out, c * 16 + 16)
                for m in range(KC):
                    if m == KC - 1:
                        split(0 if last else c + 1, c + 1)
                    ac.wait_ge(c_full, c * 8 + m + 1)
                    ac.activation(mid[:, m, bass.ds(c * TC, TC)], ps[:, m % 4, :], ACT.Identity,
                                  bias=bias[:, KC + m:KC + m + 1]).then_inc(c_free, 1)
                ac.wait_ge(zh_full, c + 1)
                ac.activation(zh[:, bass.ds(c * TC, TC)], ps[0:R1_ + E, 7, :], ACT.Identity, bias=zbias
                              ).then_inc(zh_done, 1)
            with ac.Fori(0, NCH - 1) as c:
                cond(c, False)
            cond(NCH - 1, True)

            def w2_rows(n):
                for b in range(2):
                    ac.wait_ge(w2_full, 2 * n + b + 1)
                    ac.activation(w_hi[:, 4 * b:4 * b + 4, P * n:P * n + P],
                                  ps[:, 4 + 2 * (n % 2) + b].rearrange("p (k o) -> p k o", k=4), ACT.Copy
                                  ).then_inc(w_rounded, 1)

            for n in range(5):
                w2_rows(n)
            ac.wait_ge(g_dve, 11)
            ac.activation(gs[2], gs[1], ACT.Exp).then_inc(g_act, 1)
            w2_rows(5)
            ac.wait_ge(g_dve, 23)
            ac.activation(gs[4], gs[0], ACT.Exp, scale=-2.0).then_inc(g_act, 1)
            for b in range(2):
                ac.wait_ge(g_full, 4 + b)
                ac.activation(wt[:, TC * b:TC * b + TC], ps[0:E, 6 + b, :], ACT.Copy).then_inc(g_act, 1)
            w2_rows(6)
            w2_rows(7)
            def ffn(c, last):
                for m in range(KC):
                    if m == 6 and not last:
                        split(c + 1, c + NCH + 1)
                    ac.wait_ge(st_used, c * 8 + m + 3)
                    if m == 0:
                        ac.wait_ge(out_done, c * 64 + 64)
                    ac.activation(rows_out[:, :, m // 4, P * (m % 4):P * (m % 4) + P],
                                  ps[:, 4 + m % 4].rearrange("p (t o) -> p t o", t=4), ACT.Copy).then_inc(row_free, 1)

            with ac.Fori(0, NCH - 1) as c:
                ffn(c, False)
            ffn(NCH - 1, True)

        @block.tensor
        def _(pe):
            pe.sem_inc(conv_done, 1)
            pe.sem_inc(conv_hi, 1)
            pe.sem_inc(px_full, 4)
            pe.sem_inc(x_used, 8)
            pe.sem_inc(in_full, 1)
            pe.sem_inc(bt_full, 2)
            pe.sem_inc(unit_done, 6)
            pe.wait_ge(cst_in, 32)
            pe.wait_ge(act_dup, 4)
            for s in range(4):
                mm = pe.transpose(ps[:, 0, 64 * s:64 * s + 64], dup[:, s].rearrange("p d n -> p (d n)"),
                                  ident[0:H, 0:H])
            mm.then_inc(pe_dup, 1)
            pe.wait_ge(aw_in, 64)
            for k in range(KC):
                pe.transpose(ps[:, 3, E * k:E * k + E], u[0:E, P * k:P * k + P], ident[0:E, 0:E])
            pe.transpose(ps[0:R1_, 3, 64:72], lim_sb[0:E, 0:R1_], ident[0:E, 0:E]).then_inc(aw_full, 1)
            pe.wait_ge(act_id, 1)
            for k in range(KC):
                for o in range(8):
                    pe.wait_ge(act_code, max(o + 1, 8 if k else 0))
                    if k >= 4:
                        pe.wait_ge(code_t_ready, k - 3)
                    mm = pe.transpose(ps[:, 4 + k % 4, :].bitcast(BF16)[:, o * P:o * P + P],
                                      codes[:, o, k * P:k * P + P], identb[:, :])
                mm.then_inc(pe_code, 1)
            pe.wait_ge(p_ready, 1)
            pe.wait_ge(qc_ready, 1)
            for h in range(H):
                r = 32 * (h % 4)
                mm = pe.matmul(ps[r:r + 32, 1, 32 * (h // 4):32 * (h // 4) + 32], tp[2][:, h], tp[4][:, h],
                               start=(h < 4), stop=True, skip_group_check=True)
            mm.then_inc(pe_k, 1)

            def unit(q, u):
                pr, j = u // 3, u % 3
                if j == 0:
                    pe.wait_ge(oh_done, q * 4 + pr + 5)
                    pe.wait_ge(lb_done, q * 4 + pr + 5)
                pe.wait_ge(mux_free, q * 12 + u + 1)
                first, end = SPLITS[j]
                for k in range(first, end):
                    at = A17 * 8 * (k - first)
                    for g in range(2):
                        for part in range(3):
                            mm = pe.matmul(ps[:, 2 + 2 * j + g, at:at + A17 * 8], oh[pr % 2][:, g, k * P:k * P + P],
                                           lb[pr % 2][:, g, part].rearrange("p o a -> p (o a)"), start=(part == 0),
                                           stop=(part == 2), skip_group_check=True)
                mm.then_inc(unit_done, 1)

            def transposes(src, q, batch):
                pe.wait_ge(px_free, q * 4 + batch + 1)
                for c in range(4):
                    k = 4 * (batch % 2) + c
                    mm = pe.transpose(ps[:, batch % 2, c * P:c * P + P], src[:, k * P:k * P + P], ident)
                mm.then_inc(px_full, 1)

            def convolve(bank, j):
                lo = max(512 * bank, P * j)
                for hh in range(4):
                    mm = pe.matmul(ps[32 * hh:32 * hh + 32, bank, lo - 512 * bank:512], ut[:, j, 32 * hh:32 * hh + 32],
                                   toe[:, hh, lo - P * j:512 * bank + 512 - P * j],
                                   start=(j == 0), stop=(j == 4 * bank + 3), skip_group_check=True)
                return mm

            after = {0: ((1, 0),), 1: ((1, 1),), 2: ((1, 2),), 3: ((1, 3),), 4: ((1, 4),), 5: ((1, 5),),
                     6: ((1, 6), (1, 7)), 7: ((0, 0),), 8: ((0, 1), (0, 2), (0, 3))}

            def quad(q, last):
                for u in range(3 * NPAIR):
                    unit(q, u)
                    if u == 0:
                        pe.wait_ge(px_free, q * 4 + 4)
                        pe.wait_ge(toe_hi_in, q * 64 + 64)
                    if u == 1:
                        pe.wait_ge(toe_lo_in, q * 64 + 64)
                    for bank, j in after.get(u, ()):
                        mm = convolve(bank, j)
                    if u == 3:
                        mm.then_inc(conv_hi, 1)
                    if u == 8:
                        mm.then_inc(conv_done, 1)
                    if u == 10:
                        pe.wait_ge(ys_done, q + 2)
                        transposes(ys, q, 2)
                        transposes(ys, q, 3)
                if not last:
                    pe.wait_ge(xm_done, q + 3)
                    transposes(xm, q + 1, 0)
                    transposes(xm, q + 1, 1)

            pe.wait_ge(aw_done, 2)
            pe.wait_ge(xm_done, 2)
            transposes(xm, 0, 0)
            pe.wait_ge(dve_k, 2)
            transposes(xm, 0, 1)
            with pe.Fori(0, NQ - 1) as q:
                quad(q, False)
            quad(NQ - 1, True)

            pe.sem_inc(xt_full, 8)
            pe.sem_inc(w1_full, 2)
            pe.wait_ge(mux_free, 12 * NQ + 3)
            pe.wait_ge(px_free, 4 * NQ + 2)
            with pe.Fori(0, NCH) as c:
                for m in range(KC):
                    def products():
                        pe.wait_ge(l0_free, c * 8 + m + 1)
                        for bank, w in ((m % 2, wl), (2 + m % 2, wh)):
                            for k in range(KC):
                                mm = pe.matmul(ps[:, bank, :], w[:, k, P * m:P * m + P],
                                               act[:, k, bass.ds(c * TC + TC, TC)], start=(k == 0), stop=(k == KC - 1))
                        mm.then_inc(l0_full, 1)

                    def x_rows():
                        pe.wait_ge(xres_full, c * 8 + m + 1)
                        for t in range(4):
                            mm = pe.transpose(ps[:, 4 + m % 2, P * t:P * t + P], xrow[:, t, P * m:P * m + P], ident)
                        mm.then_inc(xt_full, 1)

                    if m == 0:
                        products()
                        pe.wait_ge(xr_in, c * 16 + 16)
                        x_rows()
                    else:
                        x_rows()
                        products()
                    if m in (1, 5):
                        pe.wait_ge(w1_in, c * 32 + 16 * (m // 4) + 16)
                        for b in range(2):
                            pe.wait_ge(w1_free, c * 4 + m // 2 + b + 1)
                            for k in range(4):
                                mm = pe.transpose(ps[:, 6 + b, P * k:P * k + P],
                                                  w_in[:, P * (4 * b + k):P * (4 * b + k) + P], ident)
                            mm.then_inc(w1_full, 1)
            pe.wait_ge(w1_free, 4 * NCH + 2)
            def product(bank, m, seq, split_wait):
                for k in range(KC):
                    if m == 0:
                        split_wait(seq * 8 + k + 1)
                    for part, (w, x) in enumerate(((w_hi, x_hi), (w_hi, x_lo), (w_lo, x_hi))):
                        mm = pe.matmul(ps[:, bank, :], w[:, k, P * m:P * m + P], x[:, k], start=(k == 0 and part == 0),
                                       stop=False)
                    if m == KC - 1:
                        mm.then_inc(x_used, 1)

            with pe.Fori(0, NCH) as c:
                pe.wait_ge(l0_free, c * 8 + 10)
                pe.wait_ge(la_in, c * 128 + 128)
                pe.wait_ge(in_done, c + 1)
                for k in range(KC):
                    mm = pe.matmul(ps[:, 6, :], la[:, k], act[:, k, bass.ds(c * TC, TC)], start=(k == 0),
                                   stop=(k == KC - 1))
                mm.then_inc(in_full, 1)
                pe.wait_ge(lbn_in, c * 128 + 128)
                pe.wait_ge(bt_done, c * 2 + 2)
                for m in range(KC):
                    mm = pe.transpose(ps[:, 4 + m // 4, P * (m % 4):P * (m % 4) + P], lbn[:, m], ident)
                    if m % 4 == 3:
                        mm.then_inc(bt_full, 1)
                pe.wait_ge(l0_free, 8 * NCH + 2)
                for m in range(KC):
                    pe.wait_ge(c_free, c * 8 + m + 1)
                    pe.wait_ge(w_split, m + 1)
                    product(m % 4, m, c, lambda n: pe.wait_ge(split_lo, n))
                    if m == 0:
                        pe.wait_ge(bt_done, c * 2 + 4)
                        pe.wait_ge(in_done, c + 2)
                    pe.matmul(ps[:, m % 4, :], lbt[:, P * m:P * m + P], inter, start=False, stop=True
                              ).then_inc(c_full, 1)
                pe.wait_ge(zh_done, c + 1)
                for k in range(KC):
                    pe.wait_ge(c_free, c * 8 + k + 5)
                    pe.sem_inc(held, 1)
                    mm = pe.matmul(ps[0:R1_ + E, 7, :], aw[:, k, :], mid[:, k, bass.ds(c * TC, TC)], start=(k == 0),
                                   stop=(k == KC - 1))
                mm.then_inc(zh_full, 1)
            def w2_rows(n):
                pe.wait_ge(w2_in[n % 5], 16 * (n // 5) + 16)
                for b in range(2):
                    if n >= 2:
                        pe.wait_ge(w2_free, 2 * n + b - 3)
                    for k in range(4):
                        mm = pe.transpose(ps[:, 4 + 2 * (n % 2) + b, P * k:P * k + P],
                                          w_in2[n % 5][:, b, P * k:P * k + P], ident)
                    mm.then_inc(w2_full, 1)

            w2_rows(0)
            pe.wait_ge(zh_done, NCH + 1)
            anchors = zh.rearrange("r (n two) -> r n two", two=2)[:, :, 1]
            for g in range(8):
                pe.matmul(ps[:, 0, E * g:E * g + E], anchors[0:R1_, P * g:P * g + P], lim_sb[:, R1_:R1_ + E],
                          start=True, stop=True, skip_group_check=True)
            for g in range(8):
                mm = pe.matmul(ps[:, 3, E * g:E * g + E], anchors[R1_:R1_ + E, P * g:P * g + P],
                               cst[R1_:R1_ + E, R1_:R1_ + E], start=True, stop=True, skip_group_check=True)
            mm.then_inc(g_full, 1)
            w2_rows(1)
            pe.wait_ge(g_dve, 2)
            pe.transpose(ps[0:2, 1, 0:P], g1[0][:, 0:2], ident).then_inc(g_full, 1)
            w2_rows(2)
            pe.wait_ge(g_dve, 5)
            pe.matmul(ps[:, 2, 0:2], ones[0:2, :], g1[2][0:2, 0:2], start=True, stop=True).then_inc(g_full, 1)
            for n in range(3, 6):
                w2_rows(n)

            def weights(c, m):
                pe.wait_ge(f_free, c * 8 + m + 1)
                product(m % 4, m, c + NCH, lambda n: pe.wait_ge(split_lo, n))

            def experts(c, m):
                pe.matmul(ps[:, m % 4, :], bm[:, P * m:P * m + P], zp[:, bass.ds(c * TC, TC)], start=False,
                          stop=True).then_inc(f_full, 1)

            def rows(c, m):
                pe.wait_ge(f_free, c * 8 + m + 5)
                pe.wait_ge(row_free, c * 8 + m + 1)
                for t in range(4):
                    mm = pe.transpose(ps[:, 4 + m % 4, P * t:P * t + P], stage[m % 2][:, P * t:P * t + P], ident)
                mm.then_inc(st_used, 1)

            pe.sem_inc(st_used, 2)
            pe.wait_ge(g_dve, 6)
            pe.wait_ge(w2_free, 2)
            weights(0, 0)
            pe.wait_ge(w2_free, 12)
            pe.wait_ge(g_dve, 30)
            for g in range(8):
                mm = pe.transpose(ps[0:E, 6 + g // 4, P * (g % 4):P * (g % 4) + P], gs[5][:, g], ident)
                if g % 4 == 3:
                    mm.then_inc(g_full, 1)
            w2_rows(6)
            weights(0, 1)
            pe.wait_ge(w2_free, 14)
            pe.wait_ge(g_act, 4)
            for b in range(2):
                mm = pe.matmul(ps[0:R1_, 4 + b, :], lim_sb[0:E, 0:R1_], wt[:, TC * b:TC * b + TC], start=True, stop=True)
            mm.then_inc(g_full, 1)
            w2_rows(7)
            weights(0, 2)
            pe.wait_ge(bm_in, 16)
            pe.wait_ge(g_dve, 32)
            for m in range(3):
                experts(0, m)
            pe.wait_ge(w2_free, 16)
            for m in range(3, KC):
                weights(0, m)
                if m == 3:
                    rows(0, 0)
                    rows(0, 1)
                else:
                    rows(0, m - 2)
                experts(0, m)
            rows(0, KC - 2)
            with pe.Fori(1, NCH) as c:
                for m in range(KC):
                    weights(c, m)
                    experts(c, m)
                    if m:
                        rows(c, m - 1)
                    else:
                        rows(c - 1, KC - 1)
            rows(NCH - 1, KC - 1)

        @block.vector
        def _(ve):
            count = [0]

            def link(ins):
                count[0] += 1
                ins.then_inc(dve, 1)
                ve.wait_ge(dve, count[0])

            ve.sem_inc(oh_done, 4)
            ve.sem_inc(f_free, 4)
            ve.sem_inc(ys_done, 1)
            ve.sem_inc(mux[3], 1)
            ve.wait_ge(act_ex, 2)
            link(ve.scalar_tensor_tensor(sm[:, 3], sm[:, 2], -1.0, sm[:, 1], ALU.mult, ALU.mult))
            ve.sem_inc(dve_ssm, 1)
            link(ve.tensor_tensor(sm[:, 4], ps[:, 0, 64:128], sm[:, 1], ALU.mult))
            link(ve.tensor_scalar(sm[:, 4], sm[:, 4], float(1 / (2 * np.pi)), None, ALU.mult))
            link(ve.tensor_scalar(sm[:, 9], sm[:, 4], MAGIC, MAGIC, ALU.add, ALU.subtract))
            link(ve.tensor_tensor(sm[:, 5], sm[:, 4], sm[:, 9], ALU.subtract))
            ve.sem_inc(dve_ssm, 1)
            def over(row, ramp):
                return sm[:, row].unsqueeze(2).broadcast_to([P, H, 32]), ramp.unsqueeze(1).broadcast_to([P, H, 32])

            ve.wait_ge(cst_in, 32)
            link(ve.tensor_tensor(tp[5], *over(5, cc(C_R32, 32)), ALU.mult))
            ve.sem_inc(dve_ssm, 1)
            link(ve.tensor_tensor(tp[6], *over(5, cc(C_R1, 32)), ALU.mult))
            ve.sem_inc(dve_ssm, 1)
            ve.wait_ge(q_loaded, 128)
            planes = w01[:, 0:2048].bitcast(I32)
            for s, keep in ((4, 0x0F0F0F0F), (2, 0x33333333), (1, 0x55555555)):
                v4 = planes.rearrange("p (x two y) -> p x two y", two=2, y=s * 32)
                lo, hi = v4[:, :, 0], v4[:, :, 1]
                t = q_t.rearrange("p (x y) -> p x y", y=s * 32)
                link(ve.scalar_tensor_tensor(t, lo, s, hi, ALU.logical_shift_right, ALU.bitwise_xor))
                link(ve.tensor_scalar(t, t, keep, None, ALU.bitwise_and))
                link(ve.tensor_tensor(hi, hi, t, ALU.bitwise_xor))
                link(ve.scalar_tensor_tensor(lo, t, s, lo, ALU.logical_shift_left, ALU.bitwise_xor))
            ve.tensor_scalar(q_lo, planes, 0x0F0F0F0F, None, ALU.bitwise_and).then_inc(dve_lo, 1)
            for i in range(3):
                ve.wait_ge(act_shift, i + 1)
                link(ve.tensor_scalar(rnd, tp[2 + i], MAGIC, MAGIC, ALU.add, ALU.subtract))
                link(ve.tensor_tensor(tp[2 + i], tp[2 + i], rnd, ALU.subtract))
                ve.sem_inc(dve_ssm, 1)
            ve.wait_ge(len_in, 80)
            link(ve.tensor_copy(lens[:, 0:1], lens_i))
            ve.tensor_scalar(mask, frow[:, 0], lens[:, 0:1], None, ALU.is_lt).then_inc(dve, 1)
            count[0] += 1
            link(ve.tensor_scalar(mask_rev, frow[:, 1], lens[:, 0:1], None, ALU.is_lt))
            ve.sem_inc(masks_ready, 1)
            ve.wait_ge(act_ex, 5)
            t = lambda n: sm[:, n]
            one_minus, em1 = t(9), t(10)
            link(ve.tensor_scalar(one_minus, t(6), -1.0, 1.0, ALU.mult, ALU.add))
            link(ve.reciprocal(t(11), one_minus))
            link(ve.scalar_tensor_tensor(em1, t(6), 2.0, t(11), ALU.mult, ALU.mult))
            link(ve.scalar_tensor_tensor(t(12), t(7), -2.0, t(7), ALU.mult, ALU.mult))
            link(ve.scalar_tensor_tensor(t(13), t(12), 1.0, em1, ALU.add, ALU.mult))
            link(ve.tensor_tensor(t(13), t(13), t(12), ALU.add))
            link(ve.scalar_tensor_tensor(t(14), em1, 1.0, t(8), ALU.add, ALU.mult))
            cr, ci, ai = ps[:, 0, 128:192], ps[:, 0, 192:256], ps[:, 0, 64:128]
            link(ve.tensor_tensor(t(15), cr, t(13), ALU.mult))
            link(ve.tensor_tensor(t(16), ci, t(14), ALU.mult))
            link(ve.tensor_tensor(t(15), t(15), t(16), ALU.subtract))
            link(ve.tensor_tensor(t(16), cr, t(14), ALU.mult))
            link(ve.tensor_tensor(t(17), ci, t(13), ALU.mult))
            link(ve.tensor_tensor(t(16), t(16), t(17), ALU.add))
            link(ve.tensor_tensor(t(17), t(2), t(2), ALU.mult))
            link(ve.tensor_copy(t(20), ai))
            link(ve.tensor_tensor(t(18), t(20), t(20), ALU.mult))
            link(ve.tensor_tensor(t(17), t(17), t(18), ALU.add))
            link(ve.reciprocal(t(18), t(17)))
            link(ve.tensor_tensor(t(19), t(16), t(20), ALU.mult))
            link(ve.tensor_tensor(t(21), t(15), t(2), ALU.mult))
            link(ve.tensor_tensor(t(19), t(19), t(21), ALU.subtract))
            link(ve.scalar_tensor_tensor(t(22), t(19), 2.0, t(18), ALU.mult, ALU.mult))
            link(ve.tensor_tensor(t(19), t(16), t(2), ALU.mult))
            link(ve.tensor_tensor(t(21), t(15), t(20), ALU.mult))
            link(ve.tensor_tensor(t(19), t(19), t(21), ALU.add))
            link(ve.scalar_tensor_tensor(t(23), t(19), -2.0, t(18), ALU.mult, ALU.mult))
            ve.wait_ge(act_big, 5)
            full = lambda n: sm[:, n].unsqueeze(2).broadcast_to([P, H, 32])
            link(ve.tensor_tensor(tp[2], tp[2], full(22), ALU.mult))
            link(ve.tensor_tensor(tp[3], tp[3], full(23), ALU.mult))
            link(ve.tensor_tensor(tp[2], tp[2], tp[3], ALU.subtract))
            ve.tensor_tensor(tp[2], tp[2], tp[0], ALU.mult).then_inc(p_ready, 1)
            for pr in range(2):
                ve.wait_ge(rep_in[0], 64)
                ve.tensor_scalar(oh[pr], rep[0][:, pr].rearrange("p (g i) -> p g i", g=2), cc(C_LOW), None,
                                 ALU.is_equal).then_inc(oh_done, 1)
            ve.wait_ge(pe_k, 1)
            link(ve.tensor_copy(kt.rearrange("p q b -> p (q b)"), ps[:, 1, :]))
            ve.wait_ge(d_in, 64)
            ve.wait_ge(pool, 3)
            link(ve.tensor_tensor(kt[:, :, 0], kt[:, :, 0], d_col, ALU.add))
            ve.sem_inc(dve_k, 2)
            ve.wait_ge(code_t_ready, 8)

            def quad(q, last):
                ve.wait_ge(mux[3], q * 12 + 1)
                for b in range(4):
                    bit = 0x10101010 << b
                    bit -= (1 << 32) if bit >= 1 << 31 else 0
                    ve.tensor_scalar(bits[:, b].rearrange("p g k o -> p k g o"),
                                     code_t[:, :, bass.ds(q * 16, 16)].rearrange("p k (g o) -> p k g o", g=8), bit, None, ALU.bitwise_and
                                     ).then_inc(bits_done, 1)
                ve.wait_ge(bits_done, q * 4 + 4)
                byte = w2b[:, 6144:6656].bitcast(U8).rearrange("p (b g ko) -> p b g ko", b=4, g=8)

                def level(step, u):
                    pr, j = u // 3, u % 3
                    first, end = SPLITS[j]
                    w = (8, 4, 2, 1)[step]
                    rows = ps[:, 2 + 2 * j:4 + 2 * j, 0:A17 * 8 * (end - first)].rearrange(
                        "p g (ko a) -> p g ko a", a=A17)
                    if step:
                        ve.wait_ge(mux[step - 1], q * 12 + u + 1)
                    else:
                        ve.wait_ge(unit_done, q * 12 + u + 7)
                    ve.sem_inc(held, 1)
                    m = byte[:, 3 - step, 2 * pr:2 * pr + 2, 8 * first:8 * end]
                    ve.copy_predicated(rows[:, :, :, 0:w], m.unsqueeze(3).broadcast_to([P, 2, 8 * (end - first), w]),
                                       rows[:, :, :, w:2 * w]).then_inc(mux[step], 1)

                for u in range(3 * NPAIR):
                    if u == 9:
                        ve.wait_ge(conv_done, q + 2)
                        ve.wait_ge(px_free, q * 4 + 4)
                        ve.wait_ge(sq_done, q + 1)
                        ve.tensor_tensor(ys, ps[:, 0:2, :].rearrange("p x l -> p (x l)"), mask, ALU.mult
                                         ).then_inc(ys_done, 1)
                    level(0, u)
                    if u:
                        level(2, u - 1)
                    level(1, u)
                    if u:
                        level(3, u - 1)
                    if u % 3 == 2 and (u < 6 or not last):
                        pr = u // 3
                        nxt = (pr + 2) % 4
                        ve.wait_ge(rep_in[nxt // 2], (q + (pr + 2) // 4) * 64 + 64)
                        ve.tensor_scalar(oh[nxt % 2], rep[nxt // 2][:, nxt % 2].rearrange("p (g i) -> p g i", g=2),
                                         cc(C_LOW), None, ALU.is_equal).then_inc(oh_done, 1)
                level(2, u)
                level(3, u)

            with ve.Fori(0, NQ - 1) as q:
                quad(q, False)
            quad(NQ - 1, True)

            ve.wait_ge(sq_done, NQ + 1)
            ve.tensor_scalar(high[:, :], ssq[:, :], EST_T * EST_T, None, ALU.is_gt).then_inc(high_done, 1)
            ve.sem_inc(l0_free, 2)
            ve.wait_ge(high_in, 16)
            with ve.Fori(0, NCH) as c:
                ve.wait_ge(l0_free, c * 8 + 2)
                ve.tensor_copy(high_now, high_all[:, bass.ds(c * TC, TC)]).then_inc(l0_pick, 1)
                for m in range(KC):
                    if m == 0:
                        ve.wait_ge(l0_pick, c + 1)
                    ve.wait_ge(l0_full, c * 8 + m + 1)
                    ve.sem_inc(held, 1)
                    ve.copy_predicated(ps[:, m % 2, :], high_now, ps[:, 2 + m % 2, :]).then_inc(l0_sel, 1)
                    ve.wait_ge(l0_sel, c * 8 + m + 1)
                    ve.wait_ge(xres_full, c * 8 + m + 3)
                    ve.scalar_tensor_tensor(act[:, m, bass.ds(c * TC, TC)], ps[:, m % 2, :], bias[:, m:m + 1],
                                            xres[m % 2], ALU.add, ALU.add).then_inc(l0_free, 1)
            ve.sem_inc(in_done, 1)
            def split(chunk, seq):
                for k in range(KC):
                    ve.wait_ge(split_hi, seq * 8 + k + 1)
                    ve.tensor_tensor(x_lo[:, k], act[:, k, bass.ds(chunk * TC, TC)], x_hi[:, k].bitcast(F32),
                                     ALU.subtract).then_inc(split_lo, 1)

            def projections(c):
                ve.wait_ge(in_full, c + 2)
                ve.wait_ge(lmask_in, c * 16 + 16)
                ve.tensor_tensor(inter, ps[:, 6, :], lmask, ALU.mult).then_inc(in_done, 1)

            split(0, 0)
            for m in range(KC):
                ve.wait_ge(w_rounded, m + 1)
                block_m = w1t[:, :, P * m:P * m + P]
                ve.tensor_tensor(w_lo[:, :, P * m:P * m + P], block_m, w_hi[:, :, P * m:P * m + P].bitcast(F32),
                                 ALU.subtract).then_inc(w_split, 1)
                if m == 1:
                    projections(0)
            split(1, 1)
            with ve.Fori(1, NCH - 1) as c:
                projections(c)
                split(c + 1, c + 1)
            projections(NCH - 1)
            split(0, NCH)

            def w2_rows(n):
                for b in range(2):
                    ve.wait_ge(w_rounded, KC + 2 * n + b + 1)
                    at = (slice(None), slice(4 * b, 4 * b + 4), slice(P * n, P * n + P))
                    ve.tensor_tensor(w_lo[at], ps[:, 4 + 2 * (n % 2) + b].rearrange("p (k o) -> p k o", k=4),
                                     w_hi[at].bitcast(F32), ALU.subtract).then_inc(w2_free, 1)

            def step(ins):
                gate[0] += 1
                ins.then_inc(g_dve, 1)
                ve.wait_ge(g_dve, gate[0])

            gate = [0]
            wide = lambda x: x.unsqueeze(2).broadcast_to([P, 8, E])
            w2_rows(0)
            ve.wait_ge(g_full, 1)
            step(ve.tensor_copy(gt.rearrange("p s g e -> p s (g e)"), ps[:, 0:4:3, 0:64]))
            step(ve.tensor_reduce(g1[0][:, 0:2], gt, AX.XY, ALU.max, apply_absolute_value=True))
            w2_rows(1)
            ve.wait_ge(g_full, 2)
            step(ve.tensor_reduce(g1[1][0:2, 0:1], ps[0:2, 1, 0:P], AX.X, ALU.max))
            step(ve.tensor_scalar(g1[1][0:2, 1:2], g1[1][0:2, 0:1], 1e-6, None, ALU.max))
            step(ve.tensor_scalar(g1[2][0:2, 0:2], cst[0:2, 0:2], g1[1][0:2, 1:2], None, ALU.mult))
            w2_rows(2)
            ve.wait_ge(g_full, 3)
            step(ve.reciprocal(g1[3][:, 0:2], ps[:, 2, 0:2]))
            step(ve.tensor_scalar(g1[3][:, 2:4], g1[3][:, 0:2], 0.5, None, ALU.mult))
            step(ve.tensor_scalar(gs[0], gt[:, 0], g1[3][:, 2:3], None, ALU.mult))
            step(ve.scalar_tensor_tensor(gs[0], gt[:, 1], g1[3][:, 3:4], gs[0], ALU.mult, ALU.add))
            step(ve.tensor_reduce(g1[4], gs[0], AX.X, ALU.max))
            step(ve.tensor_tensor(gs[1], gs[0], wide(g1[4]), ALU.subtract))
            w2_rows(3)
            w2_rows(4)
            ve.wait_ge(g_act, 1)
            step(ve.tensor_reduce(g1[5], gs[2], AX.X, ALU.add))
            step(ve.reciprocal(g1[6], g1[5]))
            step(ve.tensor_tensor(gs[1], gs[2], wide(g1[6]), ALU.mult))
            for g in range(8):
                step(ve.max(gs[3][:, g], gs[1][:, g]))
            step(ve.tensor_tensor(gs[0], gs[1], wide(gs[3][:, :, 1]), ALU.subtract))
            w2_rows(5)
            ve.wait_ge(g_act, 2)
            step(ve.tensor_scalar(gs[4], gs[4], 1.0, None, ALU.add))
            step(ve.reciprocal(gs[4], gs[4]))
            step(ve.tensor_tensor(gs[2], gs[1], gs[4], ALU.mult))
            step(ve.tensor_reduce(g1[7], gs[2], AX.X, ALU.add))
            step(ve.tensor_scalar(g1[8], g1[7], 1e-9, None, ALU.add))
            step(ve.reciprocal(g1[9], g1[8]))
            step(ve.tensor_tensor(gs[5], gs[2], wide(g1[9]), ALU.mult))
            w2_rows(6)
            ve.wait_ge(g_full, 6)
            for b in range(2):
                step(ve.scalar_tensor_tensor(
                    zp[:, 2 * TC * b:2 * TC * b + 2 * TC].rearrange("r (n two) -> r n two", two=2),
                    zh[0:R1_, 2 * TC * b:2 * TC * b + 2 * TC].rearrange("r (n two) -> r n two", two=2), DELTA_SCALE,
                    ps[0:R1_, 4 + b, :].unsqueeze(2).broadcast_to([R1_, TC, 2]), ALU.mult, ALU.mult))
            w2_rows(7)
            def ffn(c, last):
                for m in range(KC):
                    ve.wait_ge(f_full, c * 8 + m + 1)
                    ve.wait_ge(st_used, c * 8 + m + 1)
                    ve.wait_ge(x1_in[m], c * 16 + 16)
                    ve.scalar_tensor_tensor(stage[m % 2], ps[:, m % 4, :], bias[:, 2 * KC + m:2 * KC + m + 1],
                                            mid[:, m, bass.ds(c * TC, TC)], ALU.add, ALU.add).then_inc(f_free, 1)
                    if m == 6 and not last:
                        split(c + 1, c + NCH + 1)

            with ve.Fori(0, NCH - 1) as c:
                ffn(c, False)
            ffn(NCH - 1, True)


_INPUTS = ["x", "itok_B_8_3872", "itok_B_14_62", "L0_cond_log_dt", "L0_cond_C", "L0_cond_log_A_real", "L0_cond_A_imag",
           "L0_cond_D", "L0_ffn_qweight", "L0_ffn_lut4", "L0_ffn_lut8", "L0_ffn_bias", "L1_cond_W", "L1_cond_b",
           "L1_cond_lora_A", "L1_cond_lora_B", "L1_ffn_W", "L1_ffn_b", "L1_ffn_A", "L1_ffn_Bmat", "L1_ffn_LiMEs"]


def kernel(**inputs):
    import concourse.bacc as bacc
    from concourse.bass_utils import run_bass_kernel_spmd

    nc = bacc.Bacc("TRN2", target_bir_lowering=False, num_devices=1)
    arrays = {name: np.ascontiguousarray(inputs[name]) for name in _INPUTS}
    arrays["cst"], arrays["feature_rows"] = shape_constants()
    aps = {name: nc.dram_tensor("in_" + name, x.shape, mybir.dt.from_np(x.dtype), kind="ExternalInput").ap()
           for name, x in arrays.items()}
    out = nc.dram_tensor("out_rows", (B, H, L), F32, kind="ExternalOutput").ap()
    build_kernel(nc, aps, out)
    result = run_bass_kernel_spmd(nc, [{"in_" + name: x for name, x in arrays.items()}], core_ids=[0])
    return result.results[0]["out_rows"]
```
